# Optimizing a Trainium2 kernel written in Bass

```python
import numpy as np
import jax
import jax.numpy as jnp

def _softmax(x, axis=-1):
    return jax.nn.softmax(x, axis=axis)

def _gelu(x):
    return jax.nn.gelu(x, approximate=True)

def _silu(x):
    return jax.nn.silu(x)

def _sigmoid(x):
    return jax.nn.sigmoid(x)

def _layernorm(x, axis=-1, eps=1e-05):
    m = jnp.mean(x, axis=axis, keepdims=True)
    v = jnp.var(x, axis=axis, keepdims=True)
    return (x - m) / jnp.sqrt(v + eps)

def _scatter_add(tgt, idx, src, axis=0):
    return tgt.at[idx].add(src)

def _segment_sum(src, seg, n):
    return jax.ops.segment_sum(src, seg, n)
kernel_name = 'mk_adaln_d2_jaxref_r8_bdd788'

def setup_inputs(seed: int=0):
    np.random.seed(seed)
    _w = jnp.asarray

    def _L0_attn_setup():
        import jax, jax.numpy as jnp
        import numpy as np
        B, N, DIM, H, DH = (2, 256, 128, 16, 64)
        INNER = H * DH
        EPS = 1e-12
        MAX_LOG_SCALE = np.log(1.0 / 0.01)
        key = jax.random.key(seed)
        k1, k2, k3, k4 = jax.random.split(key, 4)
        x = jax.random.normal(k1, (B, N, DIM), dtype=jnp.float32)
        w_qkv = jax.random.normal(k2, (DIM, 3 * INNER), dtype=jnp.float32) * DIM ** (-0.5)
        w_out = jax.random.normal(k3, (INNER, DIM), dtype=jnp.float32) * INNER ** (-0.5)
        b_out = jax.random.normal(k4, (DIM,), dtype=jnp.float32) * 0.01
        logit_scale = jnp.full((H, 1, 1), jnp.log(10.0), dtype=jnp.float32)
        return {'x': x, 'w_qkv': w_qkv, 'w_out': w_out, 'b_out': b_out, 'logit_scale': logit_scale}
    _L0_attn_in = _L0_attn_setup()

    def _L0_ffn_setup():
        import jax, jax.numpy as jnp
        import numpy as np
        DIM = 128
        N_EXPERTS = 8
        TOPK = 2
        CAPACITY_FACTOR = 1.25
        B, S = (2, 256)

        def _moe(x, Wr, W1, b1, W2, b2):
            Bsz, Sl, D = x.shape
            E = Wr.shape[1]
            T = Bsz * Sl
            capacity = max(1, int(T * CAPACITY_FACTOR / E))
            xt = x.reshape(T, D)
            probs_full = jax.nn.softmax(xt @ Wr, axis=-1)
            topv, topi = jax.lax.top_k(probs_full, TOPK)
            topv = topv / jnp.sum(topv, axis=-1, keepdims=True)
            onehot = jax.nn.one_hot(topi, E, dtype=x.dtype)
            rank = jnp.cumsum(onehot, axis=0)
            keep = (rank <= capacity).astype(x.dtype) * onehot
            w = jnp.einsum('tk,tke->te', topv, keep)
            h = jax.nn.gelu(jnp.einsum('td,edf->etf', xt, W1) + b1[:, None, :], approximate=False)
            y = jnp.einsum('etf,efd->etd', h, W2) + b2[:, None, :]
            out = jnp.einsum('te,etd->td', w, y)
            return out.reshape(Bsz, Sl, D)
        key = jax.random.key(seed)
        ks = jax.random.split(key, 6)
        D, E, F = (DIM, N_EXPERTS, 4 * DIM)
        x = jax.random.normal(ks[0], (B, S, D), dtype=jnp.float32)
        Wr = jax.random.normal(ks[1], (D, E), dtype=jnp.float32) * (1.0 / np.sqrt(D))
        W1 = jax.random.normal(ks[2], (E, D, F), dtype=jnp.float32) * (1.0 / np.sqrt(D))
        b1 = jnp.zeros((E, F), dtype=jnp.float32)
        W2 = jax.random.normal(ks[3], (E, F, D), dtype=jnp.float32) * (1.0 / np.sqrt(F))
        b2 = jnp.zeros((E, D), dtype=jnp.float32)
        return {'x': x, 'Wr': Wr, 'W1': W1, 'b1': b1, 'W2': W2, 'b2': b2}
    _L0_ffn_in = _L0_ffn_setup()
    _L0_c = _w((lambda *s: np.random.randn(*s).astype(np.float32) * 0.05)(2, 128))
    _L0_wmod = _w((lambda *s: np.random.randn(*s).astype(np.float32) * 0.05)(128, 6 * 128) * 128 ** (-0.5))

    def _L1_attn_setup():
        import jax, jax.numpy as jnp
        import numpy as np
        import math
        B, L, H, D, HID = (2, 128, 16, 64, 128)

        def _rope_tables(seq_len, dim):
            inv_freq = 1.0 / 10000.0 ** (jnp.arange(0, dim, 2, dtype=jnp.float32) / dim)
            t = jnp.arange(seq_len, dtype=jnp.float32)
            freqs = jnp.outer(t, inv_freq)
            emb = jnp.concatenate([freqs, freqs], -1)
            return (jnp.cos(emb), jnp.sin(emb))

        def _rotate_half(x):
            x1, x2 = jnp.split(x, 2, axis=-1)
            return jnp.concatenate([-x2, x1], axis=-1)

        def _apply_rope(x, cos, sin):
            return x * cos + _rotate_half(x) * sin

        def _forward(x, w_qkv, w_o, log_p, log_a, w1, b1, w2, b2):
            Bx, Lx, _ = x.shape
            qkv = jnp.dot(x, w_qkv).reshape(Bx, Lx, 3, H, D)
            qkv = jnp.transpose(qkv, (2, 0, 3, 1, 4))
            q, k, v = (qkv[0], qkv[1], qkv[2])
            cos, sin = _rope_tables(Lx, D)
            cos, sin = (cos[None, None], sin[None, None])
            q = _apply_rope(q, cos, sin)
            k = _apply_rope(k, cos, sin)
            scale = 1.0 / math.sqrt(D)
            scores = jnp.einsum('bhid,bhjd->bhij', q, k) * scale
            pos = jnp.arange(Lx, dtype=jnp.float32)
            dist = jnp.abs(pos[None, :] - pos[:, None])
            p = jax.nn.softplus(log_p)
            a = jax.nn.softplus(log_a)
            kerple = -p * jnp.log1p(a * dist[None])
            attn_t = jnp.transpose(scores, (0, 2, 3, 1))
            kerple_t = jnp.broadcast_to(jnp.transpose(kerple, (1, 2, 0))[None], attn_t.shape)
            combined = jnp.concatenate([attn_t, kerple_t], axis=-1)
            hdn = jax.nn.gelu(jnp.dot(combined, w1) + b1, approximate=False)
            refined = jnp.dot(hdn, w2) + b2
            refined = jnp.transpose(refined, (0, 3, 1, 2))
            scores = scores + kerple[None] + refined
            causal = jnp.tril(jnp.ones((Lx, Lx), dtype=bool))
            scores = jnp.where(causal[None, None], scores, -jnp.inf)
            weights = jax.nn.softmax(scores, axis=-1)
            out = jnp.einsum('bhij,bhjd->bhid', weights, v)
            out = jnp.transpose(out, (0, 2, 1, 3)).reshape(Bx, Lx, H * D)
            return jnp.dot(out, w_o)
        key = jax.random.key(seed)
        ks = jax.random.split(key, 8)
        s = 0.02
        return {'x': jax.random.normal(ks[0], (B, L, HID), jnp.float32), 'w_qkv': jax.random.normal(ks[1], (HID, 3 * H * D), jnp.float32) * s, 'w_o': jax.random.normal(ks[2], (H * D, HID), jnp.float32) * s, 'log_p': jax.random.normal(ks[3], (H, 1, 1), jnp.float32) * 0.02, 'log_a': jax.random.normal(ks[4], (H, 1, 1), jnp.float32) * 0.02, 'w1': jax.random.normal(ks[5], (2 * H, 2 * H), jnp.float32) * s, 'b1': jnp.zeros((2 * H,), jnp.float32), 'w2': jax.random.normal(ks[6], (2 * H, H), jnp.float32) * s, 'b2': jnp.zeros((H,), jnp.float32)}
    _L1_attn_in = _L1_attn_setup()

    def _L1_ffn_setup():
        import jax, jax.numpy as jnp
        import numpy as np
        E, K, H, I, SI = (32, 8, 128, 64, 256)
        CAP = 256
        LIMIT = 7.0
        SCALE = 2.5
        B, S = (2, 256)
        key = jax.random.key(seed)
        ks = jax.random.split(key, 8)
        s = 0.02
        return {'hidden_states': jax.random.normal(ks[0], (B, S, H), jnp.float32), 'router_weight': jax.random.normal(ks[1], (E, H), jnp.float32) * s, 'e_score_correction_bias': jnp.zeros((E,), jnp.float32), 'gate_up_proj': jax.random.normal(ks[2], (E, 2 * I, H), jnp.float32) * s, 'down_proj': jax.random.normal(ks[3], (E, H, I), jnp.float32) * s, 'shared_gate': jax.random.normal(ks[4], (SI, H), jnp.float32) * s, 'shared_up': jax.random.normal(ks[5], (SI, H), jnp.float32) * s, 'shared_down': jax.random.normal(ks[6], (H, SI), jnp.float32) * s}
    _L1_ffn_in = _L1_ffn_setup()
    _L1_c = _w((lambda *s: np.random.randn(*s).astype(np.float32) * 0.05)(2, 128))
    _L1_wmod = _w((lambda *s: np.random.randn(*s).astype(np.float32) * 0.05)(128, 6 * 128) * 128 ** (-0.5))
    _d = {'L0_attn_x': _L0_attn_in['x'], 'L0_attn_w_qkv': _L0_attn_in['w_qkv'], 'L0_attn_w_out': _L0_attn_in['w_out'], 'L0_attn_b_out': _L0_attn_in['b_out'], 'L0_attn_logit_scale': _L0_attn_in['logit_scale'], 'L0_ffn_Wr': _L0_ffn_in['Wr'], 'L0_ffn_W1': _L0_ffn_in['W1'], 'L0_ffn_b1': _L0_ffn_in['b1'], 'L0_ffn_W2': _L0_ffn_in['W2'], 'L0_ffn_b2': _L0_ffn_in['b2'], 'L0_c': _L0_c, 'L0_wmod': _L0_wmod, 'L1_attn_w_qkv': _L1_attn_in['w_qkv'], 'L1_attn_w_o': _L1_attn_in['w_o'], 'L1_attn_log_p': _L1_attn_in['log_p'], 'L1_attn_log_a': _L1_attn_in['log_a'], 'L1_attn_w1': _L1_attn_in['w1'], 'L1_attn_b1': _L1_attn_in['b1'], 'L1_attn_w2': _L1_attn_in['w2'], 'L1_attn_b2': _L1_attn_in['b2'], 'L1_ffn_router_weight': _L1_ffn_in['router_weight'], 'L1_ffn_e_score_correction_bias': _L1_ffn_in['e_score_correction_bias'], 'L1_ffn_gate_up_proj': _L1_ffn_in['gate_up_proj'], 'L1_ffn_down_proj': _L1_ffn_in['down_proj'], 'L1_ffn_shared_gate': _L1_ffn_in['shared_gate'], 'L1_ffn_shared_up': _L1_ffn_in['shared_up'], 'L1_ffn_shared_down': _L1_ffn_in['shared_down'], 'L1_c': _L1_c, 'L1_wmod': _L1_wmod}
    _x0 = _d['L0_attn_x']
    _d['L0_attn_x'] = jax.random.normal(jax.random.fold_in(jax.random.key(seed), 1), (2, 1024, 128), dtype=_x0.dtype)
    del _x0
    return _d

def reference(L0_attn_x, L0_attn_w_qkv, L0_attn_w_out, L0_attn_b_out, L0_attn_logit_scale, L0_ffn_Wr, L0_ffn_W1, L0_ffn_b1, L0_ffn_W2, L0_ffn_b2, L0_c, L0_wmod, L1_attn_w_qkv, L1_attn_w_o, L1_attn_log_p, L1_attn_log_a, L1_attn_w1, L1_attn_b1, L1_attn_w2, L1_attn_b2, L1_ffn_router_weight, L1_ffn_e_score_correction_bias, L1_ffn_gate_up_proj, L1_ffn_down_proj, L1_ffn_shared_gate, L1_ffn_shared_up, L1_ffn_shared_down, L1_c, L1_wmod):

    def _L0_attn_ref(x, w_qkv, w_out, b_out, logit_scale):
        import jax, jax.numpy as jnp
        import numpy as np
        B, N, DIM, H, DH = (2, 256, 128, 16, 64)
        INNER = H * DH
        EPS = 1e-12
        MAX_LOG_SCALE = np.log(1.0 / 0.01)
        b, n, dim = x.shape
        h = logit_scale.shape[0]
        qkv = x @ w_qkv
        q, k, v = jnp.split(qkv, 3, axis=-1)
        split_heads = lambda t: t.reshape(b, n, h, -1).transpose(0, 2, 1, 3)
        q, k, v = (split_heads(q), split_heads(k), split_heads(v))
        qn = q / jnp.maximum(jnp.linalg.norm(q, axis=-1, keepdims=True), EPS)
        kn = k / jnp.maximum(jnp.linalg.norm(k, axis=-1, keepdims=True), EPS)
        scale = jnp.exp(jnp.minimum(logit_scale, MAX_LOG_SCALE))
        cos_dots = jnp.einsum('bhid,bhjd->bhij', qn, kn) * scale
        attn = jax.nn.softmax(cos_dots, axis=-1)
        out = jnp.einsum('bhij,bhjd->bhid', attn, v)
        out = out.transpose(0, 2, 1, 3).reshape(b, n, -1)
        return out @ w_out + b_out

    def _L0_ffn_ref(x, Wr, W1, b1, W2, b2):
        import jax, jax.numpy as jnp
        import numpy as np
        DIM = 128
        N_EXPERTS = 8
        TOPK = 2
        CAPACITY_FACTOR = 1.25
        B, S = (2, 256)

        def _moe(x, Wr, W1, b1, W2, b2):
            Bsz, Sl, D = x.shape
            E = Wr.shape[1]
            T = Bsz * Sl
            capacity = max(1, int(T * CAPACITY_FACTOR / E))
            xt = x.reshape(T, D)
            probs_full = jax.nn.softmax(xt @ Wr, axis=-1)
            topv, topi = jax.lax.top_k(probs_full, TOPK)
            topv = topv / jnp.sum(topv, axis=-1, keepdims=True)
            onehot = jax.nn.one_hot(topi, E, dtype=x.dtype)
            rank = jnp.cumsum(onehot, axis=0)
            keep = (rank <= capacity).astype(x.dtype) * onehot
            w = jnp.einsum('tk,tke->te', topv, keep)
            h = jax.nn.gelu(jnp.einsum('td,edf->etf', xt, W1) + b1[:, None, :], approximate=False)
            y = jnp.einsum('etf,efd->etd', h, W2) + b2[:, None, :]
            out = jnp.einsum('te,etd->td', w, y)
            return out.reshape(Bsz, Sl, D)
        return _moe(x, Wr, W1, b1, W2, b2)

    def _L1_attn_ref(x, w_qkv, w_o, log_p, log_a, w1, b1, w2, b2):
        import jax, jax.numpy as jnp
        import numpy as np
        import math
        B, L, H, D, HID = (2, 128, 16, 64, 128)

        def _rope_tables(seq_len, dim):
            inv_freq = 1.0 / 10000.0 ** (jnp.arange(0, dim, 2, dtype=jnp.float32) / dim)
            t = jnp.arange(seq_len, dtype=jnp.float32)
            freqs = jnp.outer(t, inv_freq)
            emb = jnp.concatenate([freqs, freqs], -1)
            return (jnp.cos(emb), jnp.sin(emb))

        def _rotate_half(x):
            x1, x2 = jnp.split(x, 2, axis=-1)
            return jnp.concatenate([-x2, x1], axis=-1)

        def _apply_rope(x, cos, sin):
            return x * cos + _rotate_half(x) * sin

        def _forward(x, w_qkv, w_o, log_p, log_a, w1, b1, w2, b2):
            Bx, Lx, _ = x.shape
            qkv = jnp.dot(x, w_qkv).reshape(Bx, Lx, 3, H, D)
            qkv = jnp.transpose(qkv, (2, 0, 3, 1, 4))
            q, k, v = (qkv[0], qkv[1], qkv[2])
            cos, sin = _rope_tables(Lx, D)
            cos, sin = (cos[None, None], sin[None, None])
            q = _apply_rope(q, cos, sin)
            k = _apply_rope(k, cos, sin)
            scale = 1.0 / math.sqrt(D)
            scores = jnp.einsum('bhid,bhjd->bhij', q, k) * scale
            pos = jnp.arange(Lx, dtype=jnp.float32)
            dist = jnp.abs(pos[None, :] - pos[:, None])
            p = jax.nn.softplus(log_p)
            a = jax.nn.softplus(log_a)
            kerple = -p * jnp.log1p(a * dist[None])
            attn_t = jnp.transpose(scores, (0, 2, 3, 1))
            kerple_t = jnp.broadcast_to(jnp.transpose(kerple, (1, 2, 0))[None], attn_t.shape)
            combined = jnp.concatenate([attn_t, kerple_t], axis=-1)
            hdn = jax.nn.gelu(jnp.dot(combined, w1) + b1, approximate=False)
            refined = jnp.dot(hdn, w2) + b2
            refined = jnp.transpose(refined, (0, 3, 1, 2))
            scores = scores + kerple[None] + refined
            causal = jnp.tril(jnp.ones((Lx, Lx), dtype=bool))
            scores = jnp.where(causal[None, None], scores, -jnp.inf)
            weights = jax.nn.softmax(scores, axis=-1)
            out = jnp.einsum('bhij,bhjd->bhid', weights, v)
            out = jnp.transpose(out, (0, 2, 1, 3)).reshape(Bx, Lx, H * D)
            return jnp.dot(out, w_o)
        return _forward(x, w_qkv, w_o, log_p, log_a, w1, b1, w2, b2)

    def _L1_ffn_ref(hidden_states, router_weight, e_score_correction_bias, gate_up_proj, down_proj, shared_gate, shared_up, shared_down):
        import jax, jax.numpy as jnp
        import numpy as np
        E, K, H, I, SI = (32, 8, 128, 64, 256)
        CAP = 256
        LIMIT = 7.0
        SCALE = 2.5
        B, S = (2, 256)
        b, s, _ = hidden_states.shape
        T = b * s
        x = hidden_states.reshape(T, H)
        logits = x.astype(jnp.float32) @ router_weight.astype(jnp.float32).T
        scores = jax.nn.sigmoid(logits)
        _, idx = jax.lax.top_k(scores + e_score_correction_bias, K)
        w = jnp.take_along_axis(scores, idx, axis=1)
        w = w / (w.sum(-1, keepdims=True) + 1e-20) * SCALE
        e_flat = idx.reshape(-1)
        onehot = jax.nn.one_hot(e_flat, E, dtype=jnp.int32)
        pos = jnp.cumsum(onehot, axis=0) - onehot
        pos = jnp.take_along_axis(pos, e_flat[:, None], axis=1)[:, 0]
        keep = pos < CAP
        slot = jnp.where(keep, e_flat * CAP + pos, E * CAP)
        tok = jnp.arange(T * K) // K
        buf = jnp.zeros((E * CAP + 1, H), x.dtype).at[slot].set(x[tok])
        xe = buf[:E * CAP].reshape(E, CAP, H)
        gu = jnp.einsum('ech,eoh->eco', xe, gate_up_proj)
        g, u = (gu[..., :I], gu[..., I:])
        g = jnp.minimum(g, LIMIT)
        u = jnp.clip(u, -LIMIT, LIMIT)
        h = jax.nn.silu(g) * u
        ye = jnp.einsum('eci,ehi->ech', h, down_proj)
        yp = ye.reshape(E * CAP, H)[jnp.minimum(slot, E * CAP - 1)]
        yp = jnp.where(keep[:, None], yp, 0.0) * w.reshape(-1)[:, None]
        routed = jax.ops.segment_sum(yp, tok, num_segments=T).reshape(b, s, H)
        shared = jax.nn.silu(hidden_states @ shared_gate.T) * (hidden_states @ shared_up.T) @ shared_down.T
        return routed + shared
    x = L0_attn_x
    mod = (_silu(L0_c) @ L0_wmod).reshape(L0_c.shape[0], 6, 1, -1)
    sa, ca, ga, sb, cb, gb = (mod[:, 0], mod[:, 1], mod[:, 2], mod[:, 3], mod[:, 4], mod[:, 5])
    ga = (2 * (ga >= 0) - 1) * jnp.maximum(jnp.abs(ga), 0.25)
    gb = (2 * (gb >= 0) - 1) * jnp.maximum(jnp.abs(gb), 0.25)
    h = _layernorm(x, axis=-1) * (1 + ca) + sa
    x = x + ga * _L0_attn_ref(h, L0_attn_w_qkv, L0_attn_w_out, L0_attn_b_out, L0_attn_logit_scale)
    h = _layernorm(x, axis=-1) * (1 + cb) + sb
    x = x + gb * _L0_ffn_ref(h, L0_ffn_Wr, L0_ffn_W1, L0_ffn_b1, L0_ffn_W2, L0_ffn_b2)
    mod = (_silu(L1_c) @ L1_wmod).reshape(L1_c.shape[0], 6, 1, -1)
    sa, ca, ga, sb, cb, gb = (mod[:, 0], mod[:, 1], mod[:, 2], mod[:, 3], mod[:, 4], mod[:, 5])
    ga = (2 * (ga >= 0) - 1) * jnp.maximum(jnp.abs(ga), 0.25)
    gb = (2 * (gb >= 0) - 1) * jnp.maximum(jnp.abs(gb), 0.25)
    h = _layernorm(x, axis=-1) * (1 + ca) + sa
    x = x + ga * _L1_attn_ref(h, L1_attn_w_qkv, L1_attn_w_o, L1_attn_log_p, L1_attn_log_a, L1_attn_w1, L1_attn_b1, L1_attn_w2, L1_attn_b2)
    h = _layernorm(x, axis=-1) * (1 + cb) + sb
    x = x + gb * _L1_ffn_ref(h, L1_ffn_router_weight, L1_ffn_e_score_correction_bias, L1_ffn_gate_up_proj, L1_ffn_down_proj, L1_ffn_shared_gate, L1_ffn_shared_up, L1_ffn_shared_down)
    return x

_drawn_inputs = setup_inputs


def setup_inputs(seed=0):
    import zlib

    import numpy as np

    out = dict(_drawn_inputs(seed))
    spreads = {'L0_attn_logit_scale': (2.3025851249694824, 0.2),
     'L0_ffn_b1': (0.0, 0.643),
     'L0_ffn_b2': (0.0, 0.443),
     'L1_attn_b1': (0.0, 0.8),
     'L1_attn_b2': (0.0, 2.0),
     'L1_ffn_e_score_correction_bias': (0.0, 0.8)}
    factors = {'L0_attn_b_out': 8.0,
     'L1_attn_w_qkv': 8.0,
     'L1_attn_w_o': 8.0,
     'L1_attn_log_p': 8.0,
     'L1_attn_log_a': 21.441,
     'L1_attn_w1': 8.0,
     'L1_attn_w2': 8.0,
     'L1_ffn_router_weight': 8.0,
     'L1_ffn_gate_up_proj': 8.0,
     'L1_ffn_down_proj': 8.0,
     'L1_ffn_shared_gate': 8.0,
     'L1_ffn_shared_up': 8.0,
     'L1_ffn_shared_down': 8.0,
     'L1_c': 8.0,
     'L1_wmod': 8.0}
    for name, (base, spread) in spreads.items():
        noise = np.random.default_rng([zlib.crc32(name.encode()), seed]).standard_normal(out[name].shape)
        drawn = base * np.exp(spread * noise) if base else spread * noise
        out[name] = jnp.asarray(drawn.astype(out[name].dtype))
    for name, factor in factors.items():
        out[name] = (out[name] * factor).astype(out[name].dtype)
    return out
```

```python
from contextlib import ExitStack

import concourse.bass as bass
import numpy as np
from concourse import mybir

F32 = mybir.dt.float32
ALU = mybir.AluOpType
ACT = mybir.ActivationFunctionType
AX = mybir.AxisListType

P = 128
B = 2
N = 1024
D = 128
H = 16
DH = 64
NT = N // P
TT = B * NT
T = B * N
NP = H // 2
INNER = H * DH
BANK = 512
NEG = -1.0e30

E0, F0, CAP0 = 8, 512, int(T * 1.25 / 8)
E1, I1, SI, CAP1, TOP1 = 32, 64, 256, 256, 8


class Core:

    def __init__(self, nc, ctx, ins):
        self.nc, self.ctx, self.ins, self.named, self.count = nc, ctx, ins, {}, 0

    def sbuf(self, c, name, shape):
        self.count += 1
        return c.enter_context(self.nc.sbuf_tensor(f"{name}_{self.count}", shape, F32))

    def psum(self, c, name, width):
        self.count += 1
        return c.enter_context(self.nc.psum_tensor(f"{name}_{self.count}", [P, width], F32))

    def signals(self, names):
        out = []
        for n in names.split():
            if n not in self.named:
                self.named[n] = self.ctx.enter_context(self.nc.semaphore(n))
            out.append(self.named[n])
        return out

    def clear_signals(self):
        nums = sorted(s.num for s in self.named.values())
        if not nums:
            return
        with self.nc.Block() as block:
            @block.sync
            def _(sp):
                sp.sem_clear(range(nums[0], nums[-1] + 1))



def modulation(core, name, ident, mod, gate_a, gate_b, bias_row):
    nc, ins = core.nc, core.ins
    cond_in, trans_ready, condT_ready, modulated, gates_done, act_step, dve_step = core.signals(
        "cond_in trans_ready condT_ready modulated gates_done act_step dve_step")
    core.clear_signals()
    with ExitStack() as c:
        sb = lambda n, s: core.sbuf(c, n, s)
        W = sb("mod_w", [P, 6 * D])
        cT = sb("mod_cT", [P, B])
        e = sb("mod_e", [P, B])
        cb = sb("mod_cb", [P, B, P])
        t1 = sb("mod_t1", [P, 2 * B * D])
        t2 = sb("mod_t2", [P, 2 * B * D])
        t3 = sb("mod_t3", [P, 2 * B * D])
        ps_m = core.psum(c, "mod_pm", 6 * B)
        ps_g = core.psum(c, "mod_pg", 2 * B * D)
        block = c.enter_context(nc.Block())

        @block.sync
        def _(sp):
            sp.dma_start(W[:, :], ins[name + "_wmod"]).then_inc(cond_in, 16)
            with nc.allow_non_contiguous_dma(reason="256 values"):
                for b in range(B):
                    sp.dma_start(cT[:, b:b + 1], ins[name + "_c"][b, :].rearrange("(d a) -> d a", a=1)).then_inc(cond_in, 16)

        @block.scalar
        def _(act):
            act.wait_ge(cond_in, 48)
            nc.scalar.activation(e[:, :], cT[:, :], ACT.Exp, scale=-1.0).then_inc(act_step, 1)

        @block.vector
        def _(dve):
            dve.wait_ge(act_step, 1)
            nc.vector.tensor_scalar(e[:, :], e[:, :], 1.0, None, op0=ALU.add).then_inc(dve_step, 1)
            dve.wait_ge(dve_step, 1)
            nc.vector.reciprocal(e[:, :], e[:, :]).then_inc(dve_step, 1)
            dve.wait_ge(dve_step, 2)
            nc.vector.tensor_tensor(cT[:, :], cT[:, :], e[:, :], op=ALU.mult).then_inc(dve_step, 1)
            dve.wait_ge(dve_step, 3)
            nc.vector.tensor_copy(cb[:, :, :], cT[:, :].unsqueeze(2).to_broadcast([P, B, P])).then_inc(condT_ready, 1)
            dve.wait_ge(modulated, 1)
            nc.vector.tensor_copy(mod[:, :, :], ps_m[:, :].rearrange("p (k b) -> p k b", b=B)).then_inc(dve_step, 1)
            dve.wait_ge(dve_step, 4)
            for k in (1, 4):
                nc.vector.tensor_scalar(mod[:, k, :], mod[:, k, :], 1.0, None, op0=ALU.add).then_inc(dve_step, 1)
            count = 6

            def gate(x, a, size):
                nonlocal count
                nc.vector.tensor_scalar(a, x, 0.0, 2.0, op0=ALU.is_ge, op1=ALU.mult).then_inc(dve_step, 1)
                nc.vector.scalar_tensor_tensor(size, x, -1.0, x, op0=ALU.mult, op1=ALU.max).then_inc(dve_step, 1)
                count += 2
                dve.wait_ge(dve_step, count)
                nc.vector.tensor_scalar(size, size, 0.25, None, op0=ALU.max).then_inc(dve_step, 1)
                count += 1
                dve.wait_ge(dve_step, count)
                nc.vector.scalar_tensor_tensor(x, a, -1.0, size, op0=ALU.add, op1=ALU.mult).then_inc(dve_step, 1)
                count += 1
                dve.wait_ge(dve_step, count)

            for k in (2, 5):
                gate(mod[:, k, :], t2[:, 0:B], t3[:, 0:B])
            nc.vector.tensor_copy(t1[:, :], ps_g[:, :]).then_inc(dve_step, 1)
            count += 1
            dve.wait_ge(dve_step, count)
            gate(t1[:, :], t2[:, :], t3[:, :])
            half = B * D
            nc.vector.tensor_copy(gate_a[:, :, :], t1[:, 0:half].rearrange("p (b d) -> p b d", b=B)).then_inc(dve_step, 1)
            nc.vector.tensor_copy(gate_b[:, :, :], t1[:, half:2 * half].rearrange("p (b d) -> p b d", b=B)).then_inc(dve_step, 1)

        @block.tensor
        def _(pe):
            pe.wait_ge(condT_ready, 1)
            for k in range(6):
                nc.tensor.matmul(ps_m[:, B * k:B * k + B], W[:, D * k:D * k + D], cT[:, :], start=(k == 0), stop=True,
                                 skip_group_check=True)
            for g, k in enumerate((2, 5)):
                for b in range(B):
                    at = (g * B + b) * D
                    last = nc.tensor.matmul(ps_g[:, at:at + D], cb[:, b, :], W[:, D * k:D * k + D],
                                            start=(g == 0 and b == 0), stop=True, skip_group_check=True)
            last.then_inc(modulated, 1)



def layer_norm(core, X, xT, ident, expo, shift, scale, bias_row):
    nc = core.nc
    dve_step, powered, normed, xhatT, evac = core.signals("dve_step powered normed xhatT evac")
    core.clear_signals()
    with ExitStack() as c:
        xc = core.sbuf(c, "ln_xc", [P, TT, D])
        sq = core.sbuf(c, "ln_sq", [P, TT, D])
        m = core.sbuf(c, "ln_m", [P, TT])
        v = core.sbuf(c, "ln_v", [P, TT])
        ps = [core.psum(c, f"ln_ps{i}", BANK) for i in range(TT // 4)]
        block = c.enter_context(nc.Block())

        @block.vector
        def _(dve):
            nc.vector.tensor_reduce(m[:, :], X[:, :, :], axis=AX.X, op=ALU.add).then_inc(dve_step, 1)
            dve.wait_ge(dve_step, 1)
            nc.vector.tensor_scalar(m[:, :], m[:, :], 1.0 / D, None, op0=ALU.mult).then_inc(dve_step, 1)
            dve.wait_ge(dve_step, 2)
            nc.vector.tensor_tensor(xc[:, :, :], X[:, :, :], m[:, :].unsqueeze(2).to_broadcast([P, TT, D]),
                                    op=ALU.subtract).then_inc(dve_step, 1)
            dve.wait_ge(dve_step, 3)
            nc.vector.tensor_tensor(sq[:, :, :], xc[:, :, :], xc[:, :, :], op=ALU.mult).then_inc(dve_step, 1)
            dve.wait_ge(dve_step, 4)
            nc.vector.tensor_reduce(v[:, :], sq[:, :, :], axis=AX.X, op=ALU.add).then_inc(dve_step, 1)
            dve.wait_ge(dve_step, 5)
            nc.vector.tensor_scalar(v[:, :], v[:, :], 1.0 / D, 1e-5, op0=ALU.mult, op1=ALU.add).then_inc(dve_step, 1)
            dve.wait_ge(powered, 1)
            nc.vector.tensor_tensor(xc[:, :, :], xc[:, :, :], v[:, :].unsqueeze(2).to_broadcast([P, TT, D]),
                                    op=ALU.mult).then_inc(normed, 1)
            if bias_row is not None:
                for b in range(B):
                    rows = X[:, b * NT:(b + 1) * NT, :]
                    nc.vector.tensor_tensor(rows, rows, bias_row[:, b, :].unsqueeze(1).to_broadcast([P, NT, D]),
                                            op=ALU.add).then_inc(dve_step, 1)
            for i in range(0, TT // 4, 2):
                dve.wait_ge(xhatT, i + 1)
                b = i * 4 // NT
                nc.vector.tensor_scalar(xT[:, i * BANK:(i + 1) * BANK], ps[i][:, :], scale[:, b:b + 1], shift[:, b:b + 1],
                                        op0=ALU.mult, op1=ALU.add).then_inc(evac, 1)

        @block.gpsimd
        def _(pool):
            pool.wait_ge(dve_step, 6)
            nc.gpsimd.tensor_tensor(v[:, :], v[:, :], expo[:, 0:1].to_broadcast([P, TT]), op=ALU.pow).then_inc(powered, 1)

        @block.tensor
        def _(pe):
            pe.wait_ge(normed, 1)
            for i in range(TT // 4):
                for j in range(4):
                    last = nc.tensor.transpose(ps[i][:, j * P:(j + 1) * P], xc[:, 4 * i + j, :], ident[:, :])
                last.then_inc(xhatT, 1)

        @block.scalar
        def _(act):
            for i in range(1, TT // 4, 2):
                act.wait_ge(xhatT, i + 1)
                b = i * 4 // NT
                nc.scalar.activation(xT[:, i * BANK:(i + 1) * BANK], ps[i][:, :], ACT.Identity,
                                     scale=scale[:, b:b + 1], bias=shift[:, b:b + 1]).then_inc(evac, 1)



def project_qkv(core, layer, b, xT, w_qkv, qT, kT, V, ident, expo, extra):
    nc = core.nc
    (x_copied, qk_made, v_made, v_out, squared, summed, powered, qk_ready, qkT_made, qkT_out,
     dve_step, pool_step) = core.signals(
        "x_copied qk_made v_made v_out squared summed powered qk_ready qkT_made qkT_out dve_step pool_step")
    core.clear_signals()
    with ExitStack() as c:
        sb = lambda n, s: core.sbuf(c, n, s)
        xs = sb("qkv_x", [P, P])
        sq = sb("qkv_sq", [P, 2 * INNER])
        qk = sb("qkv_qk", [P, 2 * INNER])
        rn = sb("qkv_rn", [P, 2 * H])
        U = core.psum(c, "qkv_u", 2 * INNER)
        Z = core.psum(c, "qkv_z", 2 * INNER)
        block = c.enter_context(nc.Block())
        heads = lambda t: t[:, :].rearrange("p (h d) -> p h d", d=DH)
        halves = lambda t: t[:, :].rearrange("p (h s d) -> p h s d", s=2, d=DH // 2)

        @block.gpsimd
        def _(pool):
            with pool.Fori(0, NT) as t:
                pool.wait_ge(v_made, t + 1)
                nc.gpsimd.tensor_copy(xs[:, :], xT[:, bass.ts(t + b * NT, P)]).then_inc(x_copied, 1)
                if layer == 0:
                    pool.wait_ge(summed, t + 1)
                    nc.gpsimd.tensor_tensor(rn[:, :], rn[:, :], expo[:, 0:1].to_broadcast([P, 2 * H]),
                                            op=ALU.pow).then_inc(pool_step, 1)
                    pool.wait_ge(pool_step, t + 1)
                    nc.gpsimd.tensor_tensor(rn[:, 0:H], rn[:, 0:H], extra[:, :], op=ALU.mult).then_inc(powered, 1)

        @block.tensor
        def _(pe):
            pe.sem_inc(v_made, 1)
            pe.sem_inc(qkT_made, 1)
            with pe.Fori(0, NT) as t:
                pe.wait_ge(x_copied, t + 1)
                pe.wait_ge(qk_ready, t + 1)
                for j in range(4):
                    last = nc.tensor.matmul(U[:, j * BANK:(j + 1) * BANK], xs[:, :], w_qkv[:, j * BANK:(j + 1) * BANK],
                                            start=True, stop=True)
                last.then_inc(qk_made, 1)
                pe.wait_ge(qkT_out, 4 * t + 4)
                for j in range(2):
                    last = nc.tensor.matmul(Z[:, j * BANK:(j + 1) * BANK], xs[:, :],
                                            w_qkv[:, (4 + j) * BANK:(5 + j) * BANK], start=True, stop=True)
                last.then_inc(v_made, 1)
                pe.wait_ge(v_out, 2 * t + 2)
                pe.wait_ge(qk_ready, t + 2)
                for j in range(2 * NP):
                    last = nc.tensor.transpose(Z[:, j * P:(j + 1) * P], qk[:, j * P:(j + 1) * P], ident[:, :])
                last.then_inc(qkT_made, 1)

        @block.scalar
        def _(act):
            act.sem_inc(qkT_out, 4)
            with act.Fori(0, NT) as t:
                if layer == 0:
                    act.wait_ge(qk_made, t + 1)
                    nc.scalar.activation(sq[:, :], U[:, :], ACT.Square).then_inc(squared, 1)
                act.wait_ge(v_made, t + 2)
                for j in range(2):
                    nc.scalar.activation(V[:, bass.ds(t, 1), j * (H // 2):(j + 1) * (H // 2), 0:DH],
                                         Z[:, j * BANK:(j + 1) * BANK].rearrange("p (a h d) -> p a h d", a=1, d=DH),
                                         ACT.Copy).then_inc(v_out, 1)
                act.wait_ge(qkT_made, t + 2)
                for j, dst in enumerate((qT, kT)):
                    for s in range(2):
                        nc.scalar.activation(dst[:, 4 * s:4 * s + 4, bass.ts(t, P)],
                                             Z[:, (2 * j + s) * BANK:(2 * j + s + 1) * BANK].rearrange("p (a q) -> p a q", q=P),
                                             ACT.Copy).then_inc(qkT_out, 1)

        @block.vector
        def _(dve):
            dve.sem_inc(qk_ready, 1)
            with dve.Fori(0, NT) as t:
                if layer == 0:
                    dve.wait_ge(squared, t + 1)
                    nc.vector.tensor_reduce(rn[:, :], heads(sq), axis=AX.X, op=ALU.add).then_inc(dve_step, 1)
                    dve.wait_ge(dve_step, t + 1)
                    nc.vector.tensor_scalar(rn[:, :], rn[:, :], 1e-24, None, op0=ALU.max).then_inc(summed, 1)
                    dve.wait_ge(powered, t + 1)
                    dve.wait_ge(qkT_made, t + 1)
                    nc.vector.tensor_tensor(heads(qk), heads(U), rn[:, :].unsqueeze(2).to_broadcast([P, 2 * H, DH]),
                                            op=ALU.mult).then_inc(qk_ready, 1)
                else:
                    cos, sin = extra
                    dve.wait_ge(qk_made, t + 1)
                    u, s, o = halves(U), halves(sq), halves(qk)
                    half = DH // 2
                    tab = lambda x: x[:, bass.ds(t, 1), :].to_broadcast([P, 2 * H, half])
                    nc.vector.tensor_tensor(s[:, :, 0, :], u[:, :, 1, :], tab(sin), op=ALU.mult).then_inc(dve_step, 1)
                    nc.vector.tensor_tensor(s[:, :, 1, :], u[:, :, 0, :], tab(sin), op=ALU.mult).then_inc(dve_step, 1)
                    dve.wait_ge(qkT_made, t + 1)
                    nc.vector.tensor_tensor(o[:, :, 0, :], u[:, :, 0, :], tab(cos), op=ALU.mult).then_inc(dve_step, 1)
                    nc.vector.tensor_tensor(o[:, :, 1, :], u[:, :, 1, :], tab(cos), op=ALU.mult).then_inc(dve_step, 1)
                    dve.wait_ge(dve_step, 6 * t + 4)
                    nc.vector.tensor_tensor(o[:, :, 0, :], o[:, :, 0, :], s[:, :, 0, :], op=ALU.subtract).then_inc(dve_step, 1)
                    nc.vector.tensor_tensor(o[:, :, 1, :], o[:, :, 1, :], s[:, :, 1, :], op=ALU.add).then_inc(dve_step, 1)
                    dve.wait_ge(dve_step, 6 * t + 6)
                    nc.vector.sem_inc(qk_ready, 1)



def cosine_attention(core, b, X, qT, kT, V, w_out, ident, gate):
    nc = core.nc
    (q_copied, scores_made, max_made, probs_made, probsT_a, probsT_b, a_out, b_out, pv_made, sums_inv, o_normed,
     oT_made, oT_out, y_made, x_step, x_done) = core.signals(
        "q_copied scores_made max_made probs_made probsT_a probsT_b a_out b_out pv_made sums_inv o_normed oT_made oT_out "
        "y_made x_step x_done")
    core.clear_signals()
    with ExitStack() as c:
        sb = lambda n, s: core.sbuf(c, n, s)
        pb = lambda n, w: core.psum(c, n, w)
        qs = sb("ca_q", [P, NP, P])
        probs = [sb(f"ca_p{i}", [P, N]) for i in range(2)]
        probsT = [sb(f"ca_pT{i}", [P, N]) for i in range(2)]
        nmax = sb("ca_nmax", [P, H])
        sums = sb("ca_sum", [P, H])
        on = sb("ca_on", [P, INNER])
        oT = sb("ca_oT", [P, INNER])
        yg = sb("ca_yg", [P, D])
        S = [pb(f"ca_s{i}", N) for i in range(2)]
        Z = [pb(f"ca_z{i}", BANK) for i in range(2)]
        O = pb("ca_o", INNER)
        block = c.enter_context(nc.Block())

        @block.tensor
        def _(pe):
            def scores(i, h):
                r = slice(DH * (h % 2), DH * (h % 2) + DH)
                if h >= 2:
                    pe.wait_ge(probs_made, i * H + h - 1)
                for j in range(2):
                    last = nc.tensor.matmul(S[h % 2][:, j * BANK:(j + 1) * BANK], qs[r, h // 2, :],
                                            kT[r, h // 2, j * BANK:(j + 1) * BANK], start=True, stop=True)
                last.then_inc(scores_made, 1)

            def transpose(i, h):
                pe.wait_ge(probs_made, i * H + h + 1)
                for half, done, out in ((0, probsT_a, a_out), (1, probsT_b, b_out)):
                    pe.wait_ge(out, i * H + h + 1)
                    for j in range(4):
                        at = (4 * half + j) * P
                        last = nc.tensor.transpose(Z[half][:, j * P:(j + 1) * P], probs[h % 2][:, at:at + P], ident[:, :])
                    last.then_inc(done, 1)

            def values(i, h):
                pe.wait_ge(a_out, i * H + h + 2)
                pe.wait_ge(b_out, i * H + h + 2)
                for j in range(NT):
                    last = nc.tensor.matmul(O[:, h * DH:(h + 1) * DH], probsT[h % 2][:, j * P:(j + 1) * P],
                                            V[:, j, h, 0:DH], start=(j == 0), stop=(j == NT - 1))
                last.then_inc(pv_made, 1)

            pe.sem_inc(scores_made, 1)
            with pe.Fori(0, NT) as i:
                pe.wait_ge(q_copied, i + 1)
                for h in range(H):
                    scores(i, h)
                    if h >= 2:
                        values(i, h - 2)
                    if h >= 1:
                        transpose(i, h - 1)
                values(i, H - 2)
                transpose(i, H - 1)
                values(i, H - 1)
                pe.wait_ge(o_normed, i + 1)
                for j in range(NP):
                    last = nc.tensor.transpose(S[0][:, j * P:(j + 1) * P], on[:, j * P:(j + 1) * P], ident[:, :])
                last.then_inc(oT_made, 1)
                pe.wait_ge(oT_out, 2 * i + 2)
                for j in range(NP):
                    last = nc.tensor.matmul(S[1][:, 0:D], oT[:, j * P:(j + 1) * P], w_out[:, j, :],
                                            start=(j == 0), stop=(j == NP - 1))
                last.then_inc(y_made, 1)

        @block.vector
        def _(dve):
            def biggest(i, h):
                dve.wait_ge(scores_made, i * H + h + 2)
                nc.vector.tensor_reduce(nmax[:, h:h + 1], S[h % 2][:, :], axis=AX.X, op=ALU.max,
                                        negate=True).then_inc(max_made, 1)

            def evacuate(i, h):
                dve.wait_ge(probsT_a, i * H + h + 1)
                if h >= 2:
                    dve.wait_ge(pv_made, i * H + h - 1)
                nc.vector.tensor_copy(probsT[h % 2][:, 0:BANK], Z[0][:, :]).then_inc(a_out, 1)

            dve.sem_inc(a_out, 1)
            with dve.Fori(0, NT) as i:
                dve.wait_ge(scores_made, i * H + 1)
                nc.vector.tensor_copy(qs[:, :, :], qT[:, :, bass.ts(i, P)]).then_inc(q_copied, 1)
                for h in range(H):
                    biggest(i, h)
                    if h >= 1:
                        evacuate(i, h - 1)
                evacuate(i, H - 1)
                nc.vector.reciprocal(sums[:, :], sums[:, :]).then_inc(sums_inv, 1)
                dve.wait_ge(sums_inv, i + 1)
                dve.wait_ge(pv_made, i * H + H)
                nc.vector.tensor_tensor(on[:, :].rearrange("p (h d) -> p h d", d=DH),
                                        O[:, :].rearrange("p (h d) -> p h d", d=DH),
                                        sums[:, :].unsqueeze(2).to_broadcast([P, H, DH]), op=ALU.mult).then_inc(o_normed, 1)
                dve.wait_ge(oT_made, i + 1)
                nc.vector.tensor_copy(oT[:, 0:BANK], S[0][:, 0:BANK]).then_inc(oT_out, 1)
                dve.wait_ge(y_made, i + 1)
                nc.vector.tensor_tensor(yg[:, :], S[1][:, 0:D], gate[:, b, :], op=ALU.mult).then_inc(x_step, 1)
                dve.wait_ge(x_step, i + 1)
                row = X[:, bass.ds(i + b * NT, 1), :]
                nc.vector.tensor_tensor(row, row, yg[:, :].unsqueeze(1), op=ALU.add).then_inc(x_done, 1)

        @block.scalar
        def _(act):
            def exponentiate(i, h):
                act.wait_ge(max_made, i * H + h + 1)
                if h >= 2:
                    act.wait_ge(probsT_b, i * H + h - 1)
                nc.scalar.activation(probs[h % 2][:, :], S[h % 2][:, :], ACT.Exp, bias=nmax[:, h:h + 1],
                                     accum_out=sums[:, h:h + 1]).then_inc(probs_made, 1)

            def evacuate(i, h):
                act.wait_ge(probsT_b, i * H + h + 1)
                if h >= 2:
                    act.wait_ge(pv_made, i * H + h - 1)
                nc.scalar.activation(probsT[h % 2][:, BANK:N], Z[1][:, :], ACT.Copy).then_inc(b_out, 1)

            act.sem_inc(b_out, 1)
            with act.Fori(0, NT) as i:
                for h in range(H):
                    exponentiate(i, h)
                    if h >= 1:
                        evacuate(i, h - 1)
                evacuate(i, H - 1)
                act.wait_ge(oT_made, i + 1)
                nc.scalar.activation(oT[:, BANK:INNER], S[0][:, BANK:INNER], ACT.Copy).then_inc(oT_out, 1)



def route_first(core, xT, wts_dram, ident, tri, ones):
    nc, ins = core.nc, core.ins
    (loaded, logits_made, act_step, dve_step, pick_made, counts_made, w_made, wT_made, wT_out, stored) = core.signals(
        "loaded logits_made act_step dve_step pick_made counts_made w_made wT_made wT_out stored")
    core.clear_signals()
    with ExitStack() as c:
        sb = lambda n: core.sbuf(c, n, [P, TT, E0])
        small = lambda n: core.sbuf(c, n, [P, TT])
        Wr = core.sbuf(c, "wr", [P, E0])
        rev = core.sbuf(c, "rev", [P, E0])
        reset = core.sbuf(c, "reset", [P, 2 * E0 * TT])
        p, e, q = sb("r_p"), sb("r_e"), sb("r_q")
        m, s, r, top, top2 = small("r_m"), small("r_s"), small("r_r"), small("r_t1"), small("r_t2")
        OH = core.sbuf(c, "r_oh", [P, 2 * E0, TT])
        RK = core.sbuf(c, "r_rk", [P, 2 * E0, TT])
        TO = core.sbuf(c, "r_to", [P, 2 * E0, TT])
        w = sb("r_w")
        wT = core.sbuf(c, "r_wT", [E0, T])
        psl = core.psum(c, "r_l", TT * E0)
        psc = core.psum(c, "r_c", 2 * E0 * TT)
        pst = core.psum(c, "r_tot", 2 * E0 * TT)
        psw = core.psum(c, "r_wt", T)
        block = c.enter_context(nc.Block())
        wide = lambda t: t[:, :].unsqueeze(2).to_broadcast([P, TT, E0])
        revb = rev[:, :].unsqueeze(1).to_broadcast([P, TT, E0])
        pick = lambda k: OH[:, k * E0:(k + 1) * E0, :].rearrange("p e t -> p t e")
        flat = lambda t: t[:, :, :].rearrange("p g t -> p (g t)")

        @block.sync
        def _(sp):
            sp.dma_start(Wr[:, :], ins["L0_ffn_Wr"]).then_inc(loaded, 16)
            sp.dma_start(rev[:, :], ins["const_rev"].to_broadcast([P, E0])).then_inc(loaded, 16)
            sp.dma_start(reset[:, :], ins["const_reset"][:, 0:2 * E0 * TT].to_broadcast([P, 2 * E0 * TT])).then_inc(loaded, 16)
            sp.wait_ge(wT_out, 4)
            sp.dma_start(wts_dram[0:E0, :], wT[:, :]).then_inc(stored, 16)
            sp.wait_ge(stored, 16)

        @block.tensor
        def _(pe):
            pe.wait_ge(loaded, 48)
            for t in range(TT):
                last = nc.tensor.matmul(psl[:, t * E0:(t + 1) * E0], xT[:, t * P:(t + 1) * P], Wr[:, :],
                                        start=(t == 0), stop=True, skip_group_check=True)
            last.then_inc(logits_made, 1)
            pe.wait_ge(pick_made, 2)
            nc.tensor.matmul(psc[:, :], tri[:, :], flat(OH), start=True, stop=True)
            nc.tensor.matmul(pst[:, :], ones[:, :], flat(OH), start=True, stop=True).then_inc(counts_made, 1)
            pe.wait_ge(w_made, 1)
            for t in range(TT):
                last = nc.tensor.transpose(psw[0:E0, t * P:(t + 1) * P], w[:, t, :], ident[:, :])
                if t % 4 == 3:
                    last.then_inc(wT_made, 1)

        @block.scalar
        def _(act):
            act.wait_ge(dve_step, 2)
            nc.scalar.activation(e[:, :, :], e[:, :, :], ACT.Exp).then_inc(act_step, 1)
            for j in range(4):
                act.wait_ge(wT_made, j + 1)
                nc.scalar.activation(wT[:, j * BANK:(j + 1) * BANK], psw[0:E0, j * BANK:(j + 1) * BANK],
                                     ACT.Copy).then_inc(wT_out, 1)

        @block.vector
        def _(dve):
            done = 0
            dve.wait_ge(loaded, 48)

            def then(ins_):
                nonlocal done
                ins_.then_inc(dve_step, 1)
                done += 1
                dve.wait_ge(dve_step, done)

            dve.wait_ge(logits_made, 1)
            l = psl[:, :].rearrange("p (t e) -> p t e", e=E0)
            then(nc.vector.tensor_reduce(m[:, :], l, axis=AX.X, op=ALU.max))
            then(nc.vector.tensor_tensor(e[:, :, :], l, wide(m), op=ALU.subtract))
            dve.wait_ge(act_step, 1)
            then(nc.vector.tensor_reduce(s[:, :], e[:, :, :], axis=AX.X, op=ALU.add))
            then(nc.vector.reciprocal(r[:, :], s[:, :]))
            then(nc.vector.tensor_tensor(p[:, :, :], e[:, :, :], wide(r), op=ALU.mult))
            for k, best in enumerate((top, top2)):
                then(nc.vector.tensor_reduce(best[:, :], p[:, :, :], axis=AX.X, op=ALU.max))
                then(nc.vector.tensor_tensor(q[:, :, :], p[:, :, :], wide(best), op=ALU.is_equal))
                then(nc.vector.tensor_tensor(q[:, :, :], q[:, :, :], revb, op=ALU.mult))
                then(nc.vector.tensor_reduce(m[:, :], q[:, :, :], axis=AX.X, op=ALU.max))
                then(nc.vector.tensor_tensor(pick(k), revb, wide(m), op=ALU.is_equal))
                nc.vector.sem_inc(pick_made, 1)
                if k == 0:
                    then(nc.vector.scalar_tensor_tensor(p[:, :, :], pick(k), -2.0, p[:, :, :], op0=ALU.mult, op1=ALU.add))
            then(nc.vector.tensor_tensor(s[:, :], top[:, :], top2[:, :], op=ALU.add))
            then(nc.vector.reciprocal(r[:, :], s[:, :]))
            then(nc.vector.tensor_tensor(top[:, :], top[:, :], r[:, :], op=ALU.mult))
            then(nc.vector.tensor_tensor(top2[:, :], top2[:, :], r[:, :], op=ALU.mult))
            dve.wait_ge(counts_made, 1)
            then(nc.vector.tensor_copy(flat(TO), pst[:, :]))
            then(nc.vector.tensor_tensor_scan(flat(RK), reset[:, :], flat(TO), 0.0, op0=ALU.mult, op1=ALU.add))
            then(nc.vector.tensor_tensor(flat(RK), flat(RK), flat(TO), op=ALU.subtract))
            then(nc.vector.tensor_tensor(flat(RK), flat(RK), psc[:, :], op=ALU.add))
            then(nc.vector.scalar_tensor_tensor(flat(OH), flat(RK), float(CAP0), flat(OH), op0=ALU.is_le, op1=ALU.mult))
            then(nc.vector.tensor_tensor(q[:, :, :], pick(0), wide(top), op=ALU.mult))
            then(nc.vector.tensor_tensor(w[:, :, :], pick(1), wide(top2), op=ALU.mult))
            then(nc.vector.tensor_tensor(w[:, :, :], w[:, :, :], q[:, :, :], op=ALU.add))
            nc.vector.sem_inc(w_made, 1)



def experts_first(core, X, xT, wts_dram, ident, gate_fm):
    nc, ins = core.nc, core.ins
    FC, RING = F0 // P, 4
    (base_in, w_in0, w_in1, base_made, h_made, g_made, gw_made, down_made, y_out, yT_made, x_done) = core.signals(
        "base_in w_in0 w_in1 base_made h_made g_made gw_made down_made y_out yT_made x_done")
    core.clear_signals()
    w_in = (w_in0, w_in1)
    NJ = T // BANK
    U = NJ * FC
    with ExitStack() as c:
        W1 = [core.sbuf(c, "w1", [P, F0]) for _ in range(2)]
        b1 = [core.sbuf(c, "b1", [P, FC]) for _ in range(2)]
        W2 = [core.sbuf(c, "w2", [P, FC, D]) for _ in range(2)]
        WB = [core.sbuf(c, "wb", [P, T]) for _ in range(2)]
        G = [core.sbuf(c, "g", [P, BANK]) for _ in range(RING)]
        b2 = core.sbuf(c, "b2", [E0, D])
        wT = core.sbuf(c, "wT", [E0, T])
        yT = core.sbuf(c, "yT", [P, T])
        Hp = [core.psum(c, "hp", BANK) for _ in range(RING)]
        Y = [core.psum(c, "y", BANK) for _ in range(NJ)]
        block = c.enter_context(nc.Block())

        @block.sync
        def _(sp):
            sp.dma_start(b2[:, :], ins["L0_ffn_b2"]).then_inc(base_in, 16)
            sp.dma_start(wT[:, :], wts_dram[0:E0, :]).then_inc(base_in, 16)
            with sp.Fori(0, E0 // 2) as i:
                for s in range(2):
                    e = 2 * i + s
                    sp.wait_ge(down_made, (e + 1) * U)
                    sp.dma_start(W1[s][:, :], ins["L0_ffn_W1"][bass.ds(e, 1), :, :].rearrange("e p f -> p (e f)")).then_inc(w_in[s], 16)
                    with nc.allow_non_contiguous_dma(reason="512 values"):
                        sp.dma_start(b1[s][:, :], ins["L0_ffn_b1"][bass.ds(e, 1), :].rearrange("e (c p) -> p (e c)", p=P)).then_inc(w_in[s], 16)
                    sp.dma_start(W2[s][:, :, :], ins["L0_ffn_W2"][bass.ds(e, 1), :, :].rearrange("e (c p) d -> p (e c) d", p=P)).then_inc(w_in[s], 16)
                    sp.dma_start(WB[s][:, :], wts_dram[bass.ds(e, 1), :].to_broadcast([P, T])).then_inc(w_in[s], 16)

        @block.tensor
        def _(pe):
            pe.wait_ge(base_in, 32)
            for j in range(NJ):
                nc.tensor.matmul(Y[j][:, :], b2[:, :], wT[:, j * BANK:(j + 1) * BANK], start=True, stop=False,
                                 skip_group_check=True)

            def hidden(s, k, n):
                j, f = divmod(k, FC)
                pe.wait_ge(g_made, n + k + 1)
                nc.tensor.matmul(Hp[k % RING][:, :], W1[s][:, f * P:(f + 1) * P], xT[:, j * BANK:(j + 1) * BANK],
                                 start=True, stop=True).then_inc(h_made, 1)

            def down(s, k, n):
                j, f = divmod(k, FC)
                pe.wait_ge(gw_made, n + k + 1)
                nc.tensor.matmul(Y[j][:, :], W2[s][:, f, :], G[k % RING][:, :], start=False, stop=False,
                                 skip_group_check=True).then_inc(down_made, 1)

            pe.sem_inc(down_made, 2 * U)
            with pe.Fori(0, E0 // 2) as i:
                for s in range(2):
                    pe.wait_ge(w_in[s], 64 * i + 64)
                    n = (2 * i + s) * U
                    for k in range(U + 2):
                        if k < U:
                            hidden(s, k, n)
                        if k >= 2:
                            down(s, k - 2, n)
            for j in range(NJ):
                pe.wait_ge(y_out, j + 1)
                for t in range(4):
                    at = j * BANK + t * P
                    last = nc.tensor.transpose(Hp[j][:, t * P:(t + 1) * P], yT[:, at:at + P], ident[:, :])
                last.then_inc(yT_made, 1)

        @block.scalar
        def _(act):
            act.sem_inc(g_made, RING)
            with act.Fori(0, E0 // 2) as i:
                for s in range(2):
                    act.wait_ge(w_in[s], 64 * i + 64)
                    n = (2 * i + s) * U
                    for k in range(U):
                        act.wait_ge(h_made, n + k + 1)
                        act.wait_ge(down_made, n + k + 1 - RING + 2 * U)
                        nc.scalar.activation(G[k % RING][:, :], Hp[k % RING][:, :], ACT.Gelu,
                                             bias=b1[s][:, k % FC:k % FC + 1]).then_inc(g_made, 1)

        @block.vector
        def _(dve):
            with dve.Fori(0, E0 // 2) as i:
                for s in range(2):
                    dve.wait_ge(w_in[s], 64 * i + 64)
                    n = (2 * i + s) * U
                    for k in range(U):
                        j = k // FC
                        dve.wait_ge(g_made, n + k + 1 + RING)
                        nc.vector.tensor_tensor(G[k % RING][:, :], G[k % RING][:, :], WB[s][:, j * BANK:(j + 1) * BANK],
                                                op=ALU.mult).then_inc(gw_made, 1)
            dve.wait_ge(down_made, (2 + E0) * U)
            add_transposed(nc, dve, X, Y, yT, Hp, gate_fm, y_out, yT_made, x_done)


def add_transposed(nc, dve, X, Y, yT, back, gate_fm, y_out, yT_made, x_done):
    for j in range(T // BANK):
        b = j * BANK // N
        nc.vector.tensor_scalar(yT[:, j * BANK:(j + 1) * BANK], Y[j][:, :], gate_fm[:, b:b + 1], None,
                                op0=ALU.mult).then_inc(y_out, 1)
    for j in range(T // BANK):
        dve.wait_ge(yT_made, j + 1)
        rows = X[:, 4 * j:4 * j + 4, :]
        nc.vector.tensor_tensor(rows, rows, back[j][:, :].rearrange("p (t d) -> p t d", d=D), op=ALU.add).then_inc(x_done, 1)



def prepare_second(core, ident, guT, dnT, rwT, sgT, suT, sdT):
    nc, ins = core.nc, core.ins
    loaded, banked, out_made = core.signals("loaded banked out_made")
    core.clear_signals()
    NPAIR = E1 // 2
    with ExitStack() as c:
        gu = core.sbuf(c, "gu", [P, E1, D])
        dn = core.sbuf(c, "dn", [P, E1, I1])
        rw = core.sbuf(c, "rw", [E1, D])
        sg = core.sbuf(c, "sg", [P, 2, D])
        su = core.sbuf(c, "su", [P, 2, D])
        sd = core.sbuf(c, "sd", [P, SI])
        Z = [core.psum(c, "z", BANK) for _ in range(4)]
        block = c.enter_context(nc.Block())

        batches = []
        for k in range(NPAIR // 2):
            src = [gu[:, 4 * k + e, :] for e in range(4)]
            batches.append((src, [(guT[:, 2 * k + a, s, :, :], lambda z, a=a, s=s: z[:, :].rearrange(
                "h (a e s i) -> h a e s i", a=2, e=2, s=2)[:, a, :, s, :]) for a in range(2) for s in range(2)]))
        for k in range(NPAIR // 4):
            src = [dn[:, 8 * k + 2 * e:8 * k + 2 * e + 2, :] for e in range(4)]
            batches.append((src, [(dnT[:, 4 * k:4 * k + 4, :], lambda z: z[:, :].rearrange("p (a h) -> p a h", a=4))]))
        batches.append(([sg[:, 0, :], sg[:, 1, :], su[:, 0, :], su[:, 1, :]],
                        [(sgT[:, :], lambda z: z[:, 0:SI]), (suT[:, :], lambda z: z[:, SI:2 * SI])]))
        batches.append(([sd[:, 0:P], sd[:, P:SI], rw[:, :]],
                        [(sdT[:, :, :], lambda z: z[:, 0:SI].rearrange("p (a h) -> p a h", a=2)),
                         (rwT[:, :], lambda z: z[:, SI:SI + E1])]))
        copies = [len(dst) for _, dst in batches]

        @block.sync
        def _(sp):
            sp.dma_start(gu[:, :, :], ins["L1_ffn_gate_up_proj"].rearrange("e o h -> o e h")).then_inc(loaded, 16)
            sp.dma_start(dn[:, :, :], ins["L1_ffn_down_proj"].rearrange("e h i -> h e i")).then_inc(loaded, 16)
            sp.dma_start(rw[:, :], ins["L1_ffn_router_weight"]).then_inc(loaded, 16)
            sp.dma_start(sg[:, :, :], ins["L1_ffn_shared_gate"].rearrange("(a p) h -> p a h", p=P)).then_inc(loaded, 16)
            sp.dma_start(su[:, :, :], ins["L1_ffn_shared_up"].rearrange("(a p) h -> p a h", p=P)).then_inc(loaded, 16)
            sp.dma_start(sd[:, :], ins["L1_ffn_shared_down"]).then_inc(loaded, 16)

        @block.tensor
        def _(pe):
            pe.wait_ge(loaded, 96)
            for n, (src, _) in enumerate(batches):
                if n >= 4:
                    pe.wait_ge(out_made, sum(copies[:n - 3]))
                for j, x in enumerate(src):
                    x = x.rearrange("p a i -> p (a i)") if len(x.shape) == 3 else x
                    rows = x.shape[0]
                    last = nc.tensor.transpose(Z[n % 4][:, j * P:j * P + rows], x, ident[0:rows, 0:rows])
                last.then_inc(banked, 1)

        @block.vector
        def _(dve):
            for n, (_, dst) in enumerate(batches):
                dve.wait_ge(banked, n + 1)
                for to, view in dst:
                    nc.vector.tensor_copy(to, view(Z[n % 4])).then_inc(out_made, 1)


def route_second(core, xT, wts_dram, ident, tri, ones, rwT):
    nc, ins = core.nc, core.ins
    (loaded, logits_made, act_step, dve_step, pick_made, counts_made, w_made, wT_made, wT_out, stored) = core.signals(
        "loaded logits_made act_step dve_step pick_made counts_made w_made wT_made wT_out stored")
    core.clear_signals()
    W = TT * E1
    with ExitStack() as c:
        sb = lambda n: core.sbuf(c, n, [P, TT, E1])
        small = lambda n: core.sbuf(c, n, [P, TT])
        bias = core.sbuf(c, "bias", [P, E1])
        reset_e = core.sbuf(c, "reset_e", [P, W])
        reset_t = core.sbuf(c, "reset_t", [P, W])
        score, v, gt, eq, rk = sb("score"), sb("v"), sb("gt"), sb("eq"), sb("rk")
        top = core.sbuf(c, "top", [P, TT, 8])
        room, s, r = small("room"), small("s"), small("r")
        OH, RK, TO = (core.sbuf(c, n, [P, E1, TT]) for n in ("oh", "rk", "to"))
        w = sb("w")
        wT = core.sbuf(c, "wT", [E1, T])
        psl = core.psum(c, "l", W)
        psc = core.psum(c, "c", W)
        pst = core.psum(c, "tot", W)
        psw = core.psum(c, "wt", T)
        block = c.enter_context(nc.Block())
        wide = lambda t: t[:, :].unsqueeze(2).to_broadcast([P, TT, E1])
        byt = lambda t: t[:, :, :].rearrange("p e t -> p t e")
        flat = lambda t: t[:, :, :].rearrange("p a b -> p (a b)")

        @block.sync
        def _(sp):
            sp.dma_start(bias[:, :], ins["L1_ffn_e_score_correction_bias"].rearrange("(a e) -> a e", a=1).to_broadcast([P, E1])).then_inc(loaded, 16)
            sp.dma_start(reset_t[:, :], ins["const_reset"].to_broadcast([P, W])).then_inc(loaded, 16)
            sp.dma_start(reset_e[:, :], ins["const_reset_e"].to_broadcast([P, W])).then_inc(loaded, 16)
            sp.wait_ge(wT_out, 4)
            sp.dma_start(wts_dram[:, :], wT[:, :]).then_inc(stored, 16)
            sp.wait_ge(stored, 16)

        @block.tensor
        def _(pe):
            for t in range(TT):
                last = nc.tensor.matmul(psl[:, t * E1:(t + 1) * E1], xT[:, t * P:(t + 1) * P], rwT[:, :],
                                        start=(t == 0), stop=True, skip_group_check=True)
            last.then_inc(logits_made, 1)
            pe.wait_ge(pick_made, 1)
            nc.tensor.matmul(psc[:, :], tri[:, :], flat(OH), start=True, stop=True)
            nc.tensor.matmul(pst[:, :], ones[:, :], flat(OH), start=True, stop=True).then_inc(counts_made, 1)
            pe.wait_ge(w_made, 1)
            for t in range(TT):
                last = nc.tensor.transpose(psw[0:E1, t * P:(t + 1) * P], w[:, t, :], ident[:, :])
                if t % 4 == 3:
                    last.then_inc(wT_made, 1)

        @block.scalar
        def _(act):
            act.wait_ge(logits_made, 1)
            nc.scalar.activation(flat(score), psl[:, :], ACT.Sigmoid).then_inc(act_step, 1)
            for j in range(4):
                act.wait_ge(wT_made, j + 1)
                nc.scalar.activation(wT[:, j * BANK:(j + 1) * BANK], psw[0:E1, j * BANK:(j + 1) * BANK],
                                     ACT.Copy).then_inc(wT_out, 1)

        @block.vector
        def _(dve):
            done = 0
            dve.wait_ge(loaded, 48)

            def then(ins_):
                nonlocal done
                ins_.then_inc(dve_step, 1)
                done += 1
                dve.wait_ge(dve_step, done)

            dve.wait_ge(act_step, 1)
            then(nc.vector.tensor_tensor(v[:, :, :], score[:, :, :], bias[:, :].unsqueeze(1).to_broadcast([P, TT, E1]), op=ALU.add))
            for t in range(TT):
                nc.vector.max(top[:, t, :], v[:, t, :]).then_inc(dve_step, 1)
            done += TT
            dve.wait_ge(dve_step, done)
            eighth = top[:, :, TOP1 - 1:TOP1].to_broadcast([P, TT, E1])
            then(nc.vector.tensor_tensor(gt[:, :, :], v[:, :, :], eighth, op=ALU.is_gt))
            then(nc.vector.tensor_tensor(eq[:, :, :], v[:, :, :], eighth, op=ALU.is_equal))
            then(nc.vector.tensor_reduce(room[:, :], gt[:, :, :], axis=AX.X, op=ALU.add))
            then(nc.vector.tensor_scalar(room[:, :], room[:, :], -1.0, float(TOP1), op0=ALU.mult, op1=ALU.add))
            then(nc.vector.tensor_tensor_scan(flat(rk), reset_e[:, :], flat(eq), 0.0, op0=ALU.mult, op1=ALU.add))
            then(nc.vector.tensor_tensor(rk[:, :, :], rk[:, :, :], wide(room), op=ALU.is_le))
            then(nc.vector.tensor_tensor(eq[:, :, :], eq[:, :, :], rk[:, :, :], op=ALU.mult))
            then(nc.vector.tensor_tensor(byt(OH), eq[:, :, :], gt[:, :, :], op=ALU.add))
            nc.vector.sem_inc(pick_made, 1)
            then(nc.vector.tensor_tensor(w[:, :, :], score[:, :, :], byt(OH), op=ALU.mult))
            then(nc.vector.tensor_reduce(s[:, :], w[:, :, :], axis=AX.X, op=ALU.add))
            then(nc.vector.tensor_scalar(s[:, :], s[:, :], 1e-20, None, op0=ALU.add))
            then(nc.vector.reciprocal(r[:, :], s[:, :]))
            then(nc.vector.tensor_tensor(w[:, :, :], w[:, :, :], wide(r), op=ALU.mult))
            dve.wait_ge(counts_made, 1)
            then(nc.vector.tensor_copy(flat(TO), pst[:, :]))
            then(nc.vector.tensor_tensor_scan(flat(RK), reset_t[:, :], flat(TO), 0.0, op0=ALU.mult, op1=ALU.add))
            then(nc.vector.tensor_tensor(flat(RK), flat(RK), flat(TO), op=ALU.subtract))
            then(nc.vector.tensor_tensor(flat(RK), flat(RK), psc[:, :], op=ALU.add))
            then(nc.vector.tensor_scalar(flat(RK), flat(RK), float(CAP1), 2.5, op0=ALU.is_le, op1=ALU.mult))
            then(nc.vector.tensor_tensor(w[:, :, :], w[:, :, :], byt(RK), op=ALU.mult))
            nc.vector.sem_inc(w_made, 1)


def experts_second(core, X, xT, wts_dram, ident, gate_fm, guT, dnT, sgT, suT, sdT):
    nc = core.nc
    (wb_in0, wb_in1, g_made, u_made, g_cut, u_cut, u_scaled, silu_made, prod_made, down_made, y_out, yT_made, x_done) = core.signals(
        "wb_in0 wb_in1 g_made u_made g_cut u_cut u_scaled silu_made prod_made down_made y_out yT_made x_done")
    core.clear_signals()
    wb_in = (wb_in0, wb_in1)
    NJ, NPAIR, LIMIT, R = T // BANK, E1 // 2, 7.0, 2
    with ExitStack() as c:
        WB = [core.sbuf(c, "wb", [P, T]) for _ in range(2)]
        g, a, u, h = ([core.sbuf(c, n, [P, BANK]) for _ in range(R)] for n in "gauh")
        yT = core.sbuf(c, "yT", [P, T])
        Gp = [core.psum(c, "gp", BANK) for _ in range(R)]
        Up = [core.psum(c, "up", BANK) for _ in range(R)]
        Y = [core.psum(c, "y", BANK) for _ in range(NJ)]
        block = c.enter_context(nc.Block())
        units = [(m, j) for m in range(-2, NPAIR) for j in range(NJ)]

        @block.sync
        def _(sp):
            for m in range(NPAIR):
                if m >= 2:
                    sp.wait_ge(u_scaled, (m - 1) * NJ)
                for e in range(2):
                    sp.dma_start(WB[m % 2][e * I1:(e + 1) * I1, :],
                                 wts_dram[2 * m + e:2 * m + e + 1, :].to_broadcast([I1, T])).then_inc(wb_in[m % 2], 16)

        @block.tensor
        def _(pe):
            def up(n):
                m, j = units[n]
                if n >= R:
                    pe.wait_ge(g_cut, n - R + 1)
                    pe.wait_ge(u_cut, n - R + 1)
                wg = sgT[:, (m + 2) * P:(m + 3) * P] if m < 0 else guT[:, m, 0, :, :].rearrange("h e i -> h (e i)")
                wu = suT[:, (m + 2) * P:(m + 3) * P] if m < 0 else guT[:, m, 1, :, :].rearrange("h e i -> h (e i)")
                nc.tensor.matmul(Gp[n % R][:, :], wg, xT[:, j * BANK:(j + 1) * BANK], start=True, stop=True).then_inc(g_made, 1)
                nc.tensor.matmul(Up[n % R][:, :], wu, xT[:, j * BANK:(j + 1) * BANK], start=True, stop=True).then_inc(u_made, 1)

            def down(n):
                m, j = units[n]
                pe.wait_ge(prod_made, n + 1)
                wd = sdT[:, m + 2, :] if m < 0 else dnT[:, m, :]
                nc.tensor.matmul(Y[j][:, :], wd, h[n % R][:, :], start=(m == -2), stop=(m == NPAIR - 1),
                                 skip_group_check=True).then_inc(down_made, 1)

            for n in range(len(units) + 2):
                if n < len(units):
                    up(n)
                if n >= 2:
                    down(n - 2)
            for j in range(NJ):
                pe.wait_ge(y_out, j + 1)
                for t in range(4):
                    at = j * BANK + t * P
                    last = nc.tensor.transpose((Gp + Up)[j][:, t * P:(t + 1) * P], yT[:, at:at + P], ident[:, :])
                last.then_inc(yT_made, 1)

        @block.vector
        def _(dve):
            for n, (m, j) in enumerate(units):
                dve.wait_ge(g_made, n + 1)
                if n >= R:
                    dve.wait_ge(silu_made, n - R + 1)
                if m < 0:
                    nc.vector.tensor_copy(g[n % R][:, :], Gp[n % R][:, :]).then_inc(g_cut, 1)
                else:
                    nc.vector.tensor_scalar(g[n % R][:, :], Gp[n % R][:, :], LIMIT, None, op0=ALU.min).then_inc(g_cut, 1)
                dve.wait_ge(u_made, n + 1)
                if n >= R:
                    dve.wait_ge(prod_made, n - R + 1)
                if m < 0:
                    nc.vector.tensor_copy(u[n % R][:, :], Up[n % R][:, :]).then_inc(u_cut, 1)
                else:
                    nc.vector.tensor_scalar(u[n % R][:, :], Up[n % R][:, :], LIMIT, -LIMIT, op0=ALU.min, op1=ALU.max).then_inc(u_cut, 1)
                    dve.wait_ge(u_cut, n + 1)
                    dve.wait_ge(wb_in[m % 2], 32 * (m // 2 + 1))
                    nc.vector.tensor_tensor(u[n % R][:, :], u[n % R][:, :], WB[m % 2][:, j * BANK:(j + 1) * BANK],
                                            op=ALU.mult).then_inc(u_scaled, 1)
                dve.wait_ge(u_cut, n + 1)
                if m >= 0:
                    dve.wait_ge(u_scaled, n + 1 - 2 * NJ)
                dve.wait_ge(silu_made, n + 1)
                if n >= R:
                    dve.wait_ge(down_made, n - R + 1)
                nc.vector.tensor_tensor(h[n % R][:, :], u[n % R][:, :], a[n % R][:, :], op=ALU.mult).then_inc(prod_made, 1)
            dve.wait_ge(down_made, len(units))
            add_transposed(nc, dve, X, Y, yT, Gp + Up, gate_fm, y_out, yT_made, x_done)

        @block.scalar
        def _(act):
            for n in range(len(units)):
                act.wait_ge(g_cut, n + 1)
                if n >= R:
                    act.wait_ge(prod_made, n - R + 1)
                nc.scalar.activation(a[n % R][:, :], g[n % R][:, :], ACT.Silu).then_inc(silu_made, 1)




NG = 16
QA, QQ = 2, 4
ORIGIN = N - P + P // 2 + NG
TABLE = ORIGIN + P
HID = 2 * H


def kerple_tables(core, kron1, kron2, hid_tab, score_tab, V):
    nc, ins = core.nc, core.ins
    zeroed, loaded, act_step, dve_step, tab_made, multiplied, done = core.signals(
        "zeroed loaded act_step dve_step tab_made multiplied done")
    core.clear_signals()
    with ExitStack() as c:
        w1k = core.sbuf(c, "w1k", [P, P])
        dist = core.sbuf(c, "dist", [P, TABLE])
        sign = core.sbuf(c, "sign", [P, TABLE])
        lp, la, b2 = (core.sbuf(c, n, [P, 2]) for n in ("lp", "la", "kb2"))
        b1 = core.sbuf(c, "kb1", [P, 1])
        par = core.sbuf(c, "par", [P, 2])
        ab = core.sbuf(c, "ab", [P, 2])
        ex = core.sbuf(c, "ex", [P, 2])
        ps = core.psum(c, "k", 3 * BANK)
        block = c.enter_context(nc.Block())
        zero = [kron1[0], kron1[1], kron2, w1k]

        @block.vector
        def _(dve):
            for t in zero:
                nc.vector.memset(t[:, :], 0.0).then_inc(zeroed, 1)
            nc.vector.memset(V[:, :, :, DH:DH + 1], 1.0).then_inc(zeroed, 1)
            dve.wait_ge(loaded, 16 * (5 * QQ + 3 * P // H + 2))
            nc.vector.scalar_tensor_tensor(ab[:, :], par[:, :], -1.0, par[:, :], op0=ALU.mult, op1=ALU.max).then_inc(dve_step, 1)
            dve.wait_ge(act_step, 2)
            nc.vector.scalar_tensor_tensor(par[:, :], par[:, :], 0.0, ex[:, :], op0=ALU.max, op1=ALU.add).then_inc(dve_step, 1)
            dve.wait_ge(dve_step, 2)
            nc.vector.tensor_scalar(par[:, 0:1], par[:, 0:1], -1.0, None, op0=ALU.mult).then_inc(dve_step, 1)
            dve.wait_ge(act_step, 3)
            dve.wait_ge(dve_step, 3)
            nc.vector.tensor_scalar(dist[:, :], dist[:, :], par[:, 0:1], None, op0=ALU.mult).then_inc(tab_made, 1)
            dve.wait_ge(tab_made, 1)
            nc.vector.scalar_tensor_tensor(score_tab[:, :], dist[:, :], b2[:, 0:1], sign[:, :], op0=ALU.add, op1=ALU.add).then_inc(done, 1)
            dve.wait_ge(multiplied, 1)
            nc.vector.tensor_scalar(hid_tab[:, :], ps[:, 0:TABLE], b1[:, 0:1], None, op0=ALU.add).then_inc(done, 1)

        @block.sync
        def _(sp):
            w1, w2 = ins["L1_attn_w1"], ins["L1_attn_w2"]
            sp.wait_ge(zeroed, 4)
            with nc.allow_non_contiguous_dma(reason="a few small weights"):
                for q in range(QQ):
                    cols = slice(HID * q, HID * (q + 1))
                    for a in range(QA):
                        lo = 64 * a + H * q
                        sp.dma_start(kron1[a][lo:lo + H, cols], w1[0:H, :]).then_inc(loaded, 16)
                    sp.dma_start(w1k[H * q:H * (q + 1), cols], w1[H:2 * H, :]).then_inc(loaded, 16)
                    sp.dma_start(kron2[cols, H * q:H * (q + 1)], w2).then_inc(loaded, 16)
                    sp.dma_start(b1[HID * q:HID * (q + 1), :], ins["L1_attn_b1"].rearrange("(m a) -> m a", a=1)).then_inc(loaded, 16)
                for r in range(P // H):
                    rows = slice(H * r, H * (r + 1))
                    sp.dma_start(par[rows, 0:1], ins["L1_attn_log_p"].rearrange("h a c -> h (a c)")).then_inc(loaded, 16)
                    sp.dma_start(par[rows, 1:2], ins["L1_attn_log_a"].rearrange("h a c -> h (a c)")).then_inc(loaded, 16)
                    sp.dma_start(b2[rows, 0:1], ins["L1_attn_b2"].rearrange("(h a) -> h a", a=1)).then_inc(loaded, 16)
            sp.dma_start(dist[:, :], ins["const_dist"]).then_inc(loaded, 16)
            sp.dma_start(sign[:, :], ins["const_mask"]).then_inc(loaded, 16)

        @block.scalar
        def _(act):
            act.wait_ge(dve_step, 1)
            nc.scalar.activation(ex[:, :], ab[:, :], ACT.Exp, scale=-1.0).then_inc(act_step, 1)
            act.wait_ge(act_step, 1)
            nc.scalar.activation(ex[:, :], ex[:, :], ACT.Ln, bias=1.0).then_inc(act_step, 1)
            act.wait_ge(dve_step, 2)
            nc.scalar.activation(dist[:, :], dist[:, :], ACT.Ln, scale=par[:, 1:2], bias=1.0).then_inc(act_step, 1)

        @block.tensor
        def _(pe):
            pe.wait_ge(tab_made, 1)
            for at in range(0, TABLE, BANK):
                w = min(BANK, TABLE - at)
                last = nc.tensor.matmul(ps[:, at:at + w], w1k[0:64, :], dist[0:64, at:at + w], start=True, stop=True)
            last.then_inc(multiplied, 1)



def refined_attention(core, b, X, arena, kT, V, w_out, ident, gate, q_dram, kron1, kron2, hid_tab, score_tab):
    nc = core.nc
    SLOTS = 5
    names = "f_in0 f_in1 f_in2 f_in3 f_in4"
    f_in = core.signals(names)
    (q_saved, q_in, s_made, s_out_act, s_out_dve, h_made, hid_made, gelu_made, r_made, kerple_added, f_made, max_made,
     p_made, z_made, z_out_act, z_out_dve, pv_made, o_inv, o_normed, oT_made, oT_out, y_made, x_step, x_done, o_step) = core.signals(
        "q_saved q_in s_made s_out_act s_out_dve h_made hid_made gelu_made r_made kerple_added f_made max_made "
        "p_made z_made z_out_act z_out_dve pv_made o_inv o_normed oT_made oT_out y_made x_step x_done o_step")
    core.clear_signals()
    DV = DH + 1
    OB = BANK // DV
    OBANKS = [(lo, min(OB, H - lo)) for lo in range(0, H, OB)]
    R = 4
    units = [(i, g, at, min(BANK, (i + 1) * P - at)) for i in range(NT) for g in range(NG) for at in range(0, (i + 1) * P, BANK)]
    first_unit = [next(n for n, u in enumerate(units) if u[0] == i) for i in range(NT)] + [len(units)]
    first_z = [i * (i + 1) // 2 for i in range(NT + 1)]
    with ExitStack() as c:
        qs = core.sbuf(c, "qs", [P, NP, P])
        work = core.sbuf(c, "work", [P, SLOTS, N])
        mx = core.sbuf(c, "mx", [P, 2, NG])
        nmax = core.sbuf(c, "nmax", [P, NG])
        osum = core.sbuf(c, "osum", [P, H])
        yg = core.sbuf(c, "yg", [P, D])
        PS = core.psum(c, "ps", 8 * BANK)
        bank = lambda n: PS[:, n * BANK:(n + 1) * BANK]
        block = c.enter_context(nc.Block())
        F = arena[:, :].rearrange("p (g j) -> p g j", g=NG)
        hs = lambda n: work[:, n % R, :]
        pT = lambda m: work[:, 2 * (m % 2):2 * (m % 2) + 2, :].rearrange("p a b -> p (a b)")
        on = work[:, 4, :]
        oT = work[:, 0, :]
        z_in = lambda k: bank(k).rearrange("p (g r h) -> p g r h", g=4, h=H)
        z_to = lambda m, k: pT(m).rearrange("p (h r g) -> p g r h", h=H, g=NG)[:, 4 * k:4 * k + 4, :, :]
        hp = lambda n, a: bank(2 * (n % 2) + a)
        rp = lambda n: bank(4 + n % 2)
        O = lambda k: bank(4 + k)
        y = bank(7)

        @block.sync
        def _(sp):
            sp.dma_start(q_dram[:, :], arena[:, 0:NP * N]).then_inc(q_saved, 16)
            sp.wait_ge(q_saved, 16)
            for i in range(NT):
                L = (i + 1) * P
                if i:
                    sp.wait_ge(s_made, H * i)
                sp.dma_start(qs[:, :, :], q_dram.rearrange("p (a n) -> p a n", a=NP)[:, :, i * P:(i + 1) * P]).then_inc(q_in, 16)
                if i:
                    sp.wait_ge(z_made, 4 * first_z[i])
                for h in range(H):
                    n = H * i + h
                    if h % 2 == 0:
                        sp.wait_ge(s_out_act, n // 2 + 1)
                    else:
                        sp.wait_ge(s_out_dve, n // 2 + 1)
                    sp.dma_start(F[h:h + P - H + 1:H, :, 0:L], work[:, n % SLOTS, 0:L]).then_inc(f_in[n % SLOTS], 16)

        def rows_wait(eng, n):
            if n >= SLOTS:
                eng.wait_ge(f_in[n % SLOTS], 16 * (n // SLOTS))

        @block.tensor
        def _(pe):
            def hidden(n):
                i, g, at, w = units[n]
                if n >= 2:
                    pe.wait_ge(hid_made, 2 * (n - 1))
                for a in range(QA):
                    last = nc.tensor.matmul(hp(n, a)[:, 0:w], kron1[a][:, :], F[:, g, at:at + w], start=True, stop=True)
                last.then_inc(h_made, 1)

            def refine(n):
                i, g, at, w = units[n]
                pe.wait_ge(gelu_made, n + 1)
                if n >= 2:
                    pe.wait_ge(f_made, n - 1)
                for a in range(QA):
                    last = nc.tensor.matmul(rp(n)[64 * a:64 * a + 64, 0:w], kron2[:, 0:64], hs(n)[:, a * BANK:a * BANK + w],
                                            start=True, stop=True)
                last.then_inc(r_made, 1)

            def transpose(m, i, jb):
                for k in range(4):
                    if jb == 0:
                        pe.wait_ge(p_made, NG * i + 4 * k + 4)
                    if m and k % 2:
                        pe.wait_ge(z_out_act, 2 * (m - 1) + k // 2 + 1)
                    elif m:
                        pe.wait_ge(z_out_dve, 2 * (m - 1) + k // 2 + 1)
                    for g in range(4 * k, 4 * k + 4):
                        last = nc.tensor.transpose(bank(k)[:, (g % 4) * P:(g % 4 + 1) * P], F[:, g, jb * P:(jb + 1) * P], ident[:, :])
                    last.then_inc(z_made, 1)

            def values(m, i, jb):
                pe.wait_ge(z_out_dve, 2 * m + 2)
                pe.wait_ge(z_out_act, 2 * m + 2)
                for k, (lo, cnt) in enumerate(OBANKS):
                    for h in range(lo, lo + cnt):
                        last = nc.tensor.matmul(O(k)[:, (h - lo) * DV:(h - lo + 1) * DV], pT(m)[:, h * P:(h + 1) * P], V[:, jb, h, :],
                                                start=(jb == 0 and h == lo), stop=(jb == i), skip_group_check=True)
                last.then_inc(pv_made, 1)

            for i in range(NT):
                L = (i + 1) * P
                pe.wait_ge(q_in, 16 * (i + 1))
                for h in range(H):
                    n = H * i + h
                    if h >= 2:
                        if h % 2 == 0:
                            pe.wait_ge(s_out_act, n // 2)
                        else:
                            pe.wait_ge(s_out_dve, n // 2)
                    r = slice(DH * (h % 2), DH * (h % 2) + DH)
                    for at in range(0, L, BANK):
                        w = min(BANK, L - at)
                        last = nc.tensor.matmul(bank(2 * (h % 2) + at // BANK)[:, 0:w], qs[r, h // 2, :],
                                                kT[r, h // 2, at:at + w], start=True, stop=True)
                    last.then_inc(s_made, 1)
                for s in range(SLOTS):
                    uses = (H * (i + 1) - s + SLOTS - 1) // SLOTS
                    pe.wait_ge(f_in[s], 16 * uses)
                lo, hi = first_unit[i], first_unit[i + 1]
                for n in range(lo, hi + 2):
                    if n < hi:
                        hidden(n)
                    if n - 2 >= lo:
                        refine(n - 2)
                lo, hi = first_z[i], first_z[i + 1]
                for m in range(lo, hi + 1):
                    if m < hi:
                        transpose(m, i, m - lo)
                    if m > lo:
                        values(m - 1, i, m - 1 - lo)
                pe.wait_ge(o_normed, i + 1)
                for j in range(NP):
                    last = nc.tensor.transpose(bank(j // 4)[:, (j % 4) * P:(j % 4 + 1) * P], on[:, j * P:(j + 1) * P], ident[:, :])
                last.then_inc(oT_made, 1)
                pe.wait_ge(oT_out, 2 * i + 2)
                for j in range(NP):
                    last = nc.tensor.matmul(y[:, 0:D], oT[:, j * P:(j + 1) * P], w_out[:, j, :], start=(j == 0), stop=(j == NP - 1))
                last.then_inc(y_made, 1)

        @block.scalar
        def _(act):
            for i in range(NT):
                L = (i + 1) * P
                for h in range(0, H, 2):
                    n = H * i + h
                    act.wait_ge(s_made, n + 1)
                    rows_wait(act, n)
                    nc.scalar.activation(work[:, n % SLOTS, 0:L], PS[:, 0:L], ACT.Copy, scale=DH ** -0.5).then_inc(s_out_act, 1)
                for n in range(first_unit[i], first_unit[i + 1]):
                    w = units[n][3]
                    act.wait_ge(hid_made, 2 * n + 2)
                    h2 = hs(n).rearrange("p (a w) -> p a w", a=QA)[:, :, 0:w]
                    nc.scalar.activation(h2, h2, ACT.Gelu).then_inc(gelu_made, 1)
                act.wait_ge(max_made, i + 1)
                for g in range(NG):
                    nc.scalar.activation(F[:, g, 0:L], F[:, g, 0:L], ACT.Exp, bias=nmax[:, g:g + 1]).then_inc(p_made, 1)
                for m in range(first_z[i], first_z[i + 1]):
                    for k in (1, 3):
                        act.wait_ge(z_made, 4 * m + k + 1)
                        if m - 2 >= 0:
                            act.wait_ge(pv_made, m - 1)
                        nc.scalar.activation(z_to(m, k), z_in(k), ACT.Copy).then_inc(z_out_act, 1)
                act.wait_ge(oT_made, i + 1)
                nc.scalar.activation(oT[:, BANK:2 * BANK], bank(1), ACT.Copy).then_inc(oT_out, 1)

        @block.gpsimd
        def _(pool):
            for n, (i, g, at, w) in enumerate(units):
                pool.wait_ge(h_made, n + 1)
                start = ORIGIN - (i * P + g) + at
                nc.gpsimd.tensor_tensor(F[:, g, at:at + w], F[:, g, at:at + w], score_tab[:, start:start + w],
                                        op=ALU.add).then_inc(kerple_added, 1)

        @block.vector
        def _(dve):
            def hidden(n):
                i, g, at, w = units[n]
                dve.wait_ge(h_made, n + 1)
                if n >= R:
                    dve.wait_ge(r_made, n - R + 1)
                for a in range(QA):
                    start = ORIGIN - (i * P + g + 64 * a) + at
                    nc.vector.tensor_tensor(hs(n)[:, a * BANK:a * BANK + w], hp(n, a)[:, 0:w], hid_tab[:, start:start + w],
                                            op=ALU.add).then_inc(hid_made, 1)

            def refined(n):
                i, g, at, w = units[n]
                dve.wait_ge(r_made, n + 1)
                dve.wait_ge(kerple_added, n + 1)
                row = F[:, g, at:at + w]
                nc.vector.tensor_tensor_reduce(out=row, in0=rp(n)[:, 0:w], in1=row, scale=1.0, scalar=2 * NEG,
                                               op0=ALU.add, op1=ALU.max,
                                               accum_out=mx[:, at // BANK, g:g + 1]).then_inc(f_made, 1)

            for i in range(NT):
                L = (i + 1) * P
                for h in range(1, H, 2):
                    n = H * i + h
                    dve.wait_ge(s_made, n + 1)
                    rows_wait(dve, n)
                    nc.vector.tensor_scalar(work[:, n % SLOTS, 0:L], PS[:, 2 * BANK:2 * BANK + L], DH ** -0.5, None,
                                            op0=ALU.mult).then_inc(s_out_dve, 1)
                lo, hi = first_unit[i], first_unit[i + 1]
                for n in range(lo, hi + 2):
                    if n < hi:
                        hidden(n)
                    if n - 2 >= lo:
                        refined(n - 2)
                dve.wait_ge(f_made, hi)
                if L <= BANK:
                    nc.vector.tensor_scalar(nmax[:, :], mx[:, 0, :], -1.0, None, op0=ALU.mult).then_inc(max_made, 1)
                else:
                    nc.vector.tensor_tensor(mx[:, 0, :], mx[:, 0, :], mx[:, 1, :], op=ALU.max).then_inc(o_step, 1)
                    dve.wait_ge(o_step, i + 1 - NT // 2)
                    nc.vector.tensor_scalar(nmax[:, :], mx[:, 0, :], -1.0, None, op0=ALU.mult).then_inc(max_made, 1)
                for m in range(first_z[i], first_z[i + 1]):
                    for k in (0, 2):
                        dve.wait_ge(z_made, 4 * m + k + 1)
                        if m - 2 >= 0:
                            dve.wait_ge(pv_made, m - 1)
                        nc.vector.tensor_copy(z_to(m, k), z_in(k)).then_inc(z_out_dve, 1)
                dve.wait_ge(pv_made, first_z[i + 1])
                for k, (lo, cnt) in enumerate(OBANKS):
                    o = O(k)[:, 0:cnt * DV].rearrange("p (h d) -> p h d", d=DV)
                    nc.vector.reciprocal(osum[:, lo:lo + cnt], o[:, :, DH]).then_inc(o_inv, 1)
                dve.wait_ge(o_inv, len(OBANKS) * (i + 1))
                for k, (lo, cnt) in enumerate(OBANKS):
                    o = O(k)[:, 0:cnt * DV].rearrange("p (h d) -> p h d", d=DV)
                    last = nc.vector.tensor_tensor(on[:, lo * DH:(lo + cnt) * DH].rearrange("p (h d) -> p h d", d=DH), o[:, :, 0:DH],
                                                   osum[:, lo:lo + cnt].unsqueeze(2).to_broadcast([P, cnt, DH]), op=ALU.mult)
                last.then_inc(o_normed, 1)
                dve.wait_ge(oT_made, i + 1)
                nc.vector.tensor_copy(oT[:, 0:BANK], bank(0)).then_inc(oT_out, 1)
                dve.wait_ge(y_made, i + 1)
                nc.vector.tensor_tensor(yg[:, :], y[:, 0:D], gate[:, b, :], op=ALU.mult).then_inc(x_step, 1)
                dve.wait_ge(x_step, i + 1)
                row = X[:, i + b * NT, :]
                nc.vector.tensor_tensor(row, row, yg[:, :], op=ALU.add).then_inc(x_done, 1)



def host_constants():
    reset = np.ones((1, E1 * TT), np.float32)
    reset[:, ::TT] = 0.0
    reset_e = np.ones((1, E1 * TT), np.float32)
    reset_e[:, ::E1] = 0.0
    behind = (np.arange(P) // H * NG).reshape(P, 1) + ORIGIN - np.arange(TABLE)[None]
    freq = (np.float32(1.0) / np.float32(10000.0) ** (np.arange(0, DH, 2, dtype=np.float32) / np.float32(DH))).astype(np.float32)
    angle = np.outer(np.arange(N, dtype=np.float32), freq).astype(np.float32)
    tiles = lambda t: np.ascontiguousarray(t.reshape(NT, P, DH // 2).transpose(1, 0, 2).astype(np.float32))
    return {
        "const_dist": np.abs(behind).astype(np.float32),
        "const_mask": np.where(behind < 0, NEG, 0.0).astype(np.float32),
        "const_cos": tiles(np.cos(angle)),
        "const_sin": tiles(np.sin(angle)),
        "const_reset_e": reset_e,
        "const_ident": np.eye(P, dtype=np.float32),
        "const_tri": np.triu(np.ones((P, P), np.float32)),
        "const_reset": reset,
        "const_rev": np.arange(E0, 0, -1, dtype=np.float32)[None],
    }


def program(nc, ins, out, stages="01234"):
    with ExitStack() as ctx:
        core = Core(nc, ctx, ins)
        sb = lambda n, s: core.sbuf(ctx, n, s)
        X = sb("X", [P, TT, D])
        xT = sb("xT", [P, T])
        ident = sb("ident", [P, P])
        expo = sb("expo", [P, 1])
        mod = sb("mod", [P, 6, B])
        gate_a = sb("gate_a", [P, B, D])
        gate_b = sb("gate_b", [P, B, D])
        rows = sb("rows", [P, B, D])
        tri, ones = sb("tri", [P, P]), sb("ones", [P, P])
        q_dram = nc.dram_tensor("queries", (P, NP * N), F32, kind="Internal").ap()
        wts_dram = nc.dram_tensor("expert_weights", (E1, T), F32, kind="Internal").ap()
        loaded, const_made = core.signals("loaded const_made")
        core.clear_signals()
        with nc.Block() as block:
            @block.sync
            def _(sp):
                sp.dma_start(X[:, :, :], ins["L0_attn_x"].rearrange("b (t p) d -> p (b t) d", p=P)).then_inc(loaded, 16)
                sp.dma_start(ident[:, :], ins["const_ident"]).then_inc(loaded, 16)
                sp.dma_start(tri[:, :], ins["const_tri"]).then_inc(loaded, 16)
                sp.wait_ge(loaded, 48)

            @block.vector
            def _(dve):
                nc.vector.memset(ones[:, :], 1.0).then_inc(const_made, 1)
                nc.vector.memset(expo[:, :], -0.5).then_inc(const_made, 1)
                dve.wait_ge(const_made, 2)

        if "0" in stages:
            modulation(core, "L0", ident, mod, gate_a, gate_b, None)
            bias, staged = core.signals("bias staged")
            core.clear_signals()
            with nc.Block() as block:
                @block.sync
                def _(sp):
                    sp.dma_start(rows[:, 0, :], ins["L0_attn_b_out"].rearrange("(a d) -> a d", a=1).to_broadcast([P, D])).then_inc(bias, 16)
                    sp.wait_ge(bias, 16)

                @block.vector
                def _(dve):
                    dve.wait_ge(bias, 16)
                    nc.vector.tensor_tensor(rows[:, 1, :], rows[:, 0, :], gate_a[:, 1, :], op=ALU.mult).then_inc(staged, 1)
                    dve.wait_ge(staged, 1)
                    nc.vector.tensor_tensor(rows[:, 0, :], rows[:, 0, :], gate_a[:, 0, :], op=ALU.mult).then_inc(staged, 1)
            layer_norm(core, X, xT, ident, expo, mod[:, 0, :], mod[:, 1, :], rows)
            with ExitStack() as c:
                sc = lambda n, s: core.sbuf(c, n, s)
                w_qkv = sc("w_qkv", [P, 3 * INNER])
                w_out = sc("w_out", [P, NP, D])
                hscale = sc("hscale", [P, H])
                qT, kT, V = sc("qT", [P, NP, N]), sc("kT", [P, NP, N]), sc("V", [P, NT, H, DH])
                scaled, = core.signals("scaled")
                core.clear_signals()
                with nc.Block() as block:
                    @block.sync
                    def _(sp):
                        sp.dma_start(w_qkv[:, :], ins["L0_attn_w_qkv"]).then_inc(loaded, 16)
                        sp.dma_start(w_out[:, :, :], ins["L0_attn_w_out"].rearrange("(j p) d -> p j d", p=P)).then_inc(loaded, 16)
                        sp.dma_start(hscale[:, :], ins["L0_attn_logit_scale"].rearrange("h a c -> (a c) h").to_broadcast([P, H])).then_inc(loaded, 16)
                        sp.wait_ge(loaded, 48)

                    @block.vector
                    def _(dve):
                        dve.wait_ge(loaded, 48)
                        nc.vector.tensor_scalar(hscale[:, :], hscale[:, :], float(np.float32(np.log(1.0 / 0.01))), None, op0=ALU.min).then_inc(scaled, 1)

                    @block.scalar
                    def _(act):
                        act.wait_ge(scaled, 1)
                        nc.scalar.activation(hscale[:, :], hscale[:, :], ACT.Exp).then_inc(scaled, 1)
                for b in range(B):
                    project_qkv(core, 0, b, xT, w_qkv, qT, kT, V, ident, expo, hscale)
                    cosine_attention(core, b, X, qT, kT, V, w_out, ident, gate_a)

        if "1" in stages:
            if "0" not in stages:
                modulation(core, "L0", ident, mod, gate_a, gate_b, None)
            layer_norm(core, X, xT, ident, expo, mod[:, 3, :], mod[:, 4, :], None)
            route_first(core, xT, wts_dram, ident, tri, ones)
            experts_first(core, X, xT, wts_dram, ident, mod[:, 5, :])

        if "2" in stages:
            modulation(core, "L1", ident, mod, gate_a, gate_b, None)
            layer_norm(core, X, xT, ident, expo, mod[:, 0, :], mod[:, 1, :], None)
            with ExitStack() as c:
                arena = core.sbuf(c, "arena", [P, NG * N])
                kT = core.sbuf(c, "kT", [P, NP, N])
                V = core.sbuf(c, "V", [P, NT, H, DH + 1])
                w_out = core.sbuf(c, "w_out", [P, NP, D])
                kron1 = [core.sbuf(c, "kron1", [P, P]) for _ in range(QA)]
                kron2 = core.sbuf(c, "kron2", [P, 64])
                hid_tab = core.sbuf(c, "hid_tab", [P, TABLE])
                score_tab = core.sbuf(c, "score_tab", [P, TABLE])
                qT = arena[:, 0:NP * N].rearrange("p (a n) -> p a n", a=NP)
                w_qkv = arena[:, NP * N:NP * N + 3 * INNER]
                kerple_tables(core, kron1, kron2, hid_tab, score_tab, V)
                for b in range(B):
                    with ExitStack() as c2:
                        cos = core.sbuf(c2, "cos", [P, NT, DH // 2])
                        sin = core.sbuf(c2, "sin", [P, NT, DH // 2])
                        core.clear_signals()
                        with nc.Block() as block:
                            @block.sync
                            def _(sp):
                                sp.dma_start(w_qkv[:, :], ins["L1_attn_w_qkv"]).then_inc(loaded, 16)
                                sp.dma_start(cos[:, :, :], ins["const_cos"]).then_inc(loaded, 16)
                                sp.dma_start(sin[:, :, :], ins["const_sin"]).then_inc(loaded, 16)
                                sp.dma_start(w_out[:, :, :], ins["L1_attn_w_o"].rearrange("(j p) d -> p j d", p=P)).then_inc(loaded, 16)
                                sp.wait_ge(loaded, 64)
                        project_qkv(core, 1, b, xT, w_qkv, qT, kT, V, ident, expo, (cos, sin))
                    refined_attention(core, b, X, arena, kT, V, w_out, ident, gate_a, q_dram, kron1, kron2, hid_tab, score_tab)

        if "3" in stages:
            if "2" not in stages:
                modulation(core, "L1", ident, mod, gate_a, gate_b, None)
            layer_norm(core, X, xT, ident, expo, mod[:, 3, :], mod[:, 4, :], None)
            with ExitStack() as c:
                guT = core.sbuf(c, "guT", [P, E1 // 2, 2, 2, I1])
                dnT = core.sbuf(c, "dnT", [P, E1 // 2, D])
                rwT = core.sbuf(c, "rwT", [P, E1])
                sgT, suT = core.sbuf(c, "sgT", [P, SI]), core.sbuf(c, "suT", [P, SI])
                sdT = core.sbuf(c, "sdT", [P, 2, D])
                prepare_second(core, ident, guT, dnT, rwT, sgT, suT, sdT)
                route_second(core, xT, wts_dram, ident, tri, ones, rwT)
                experts_second(core, X, xT, wts_dram, ident, mod[:, 5, :], guT, dnT, sgT, suT, sdT)

        stored, = core.signals("stored")
        core.clear_signals()
        with nc.Block() as block:
            @block.sync
            def _(sp):
                sp.dma_start(out.rearrange("b (t p) d -> p (b t) d", p=P), X[:, :, :]).then_inc(stored, 16)
                sp.wait_ge(stored, 16)


def kernel(**inputs):
    import concourse.bacc as bacc
    from concourse.bass_utils import run_bass_kernel_spmd

    nc = bacc.Bacc("TRN2", target_bir_lowering=False, num_devices=1)
    arrays = {name: np.ascontiguousarray(a) for name, a in {**inputs, **host_constants()}.items()}
    ins = {name: nc.dram_tensor(name, a.shape, mybir.dt.from_np(a.dtype), kind="ExternalInput").ap()
           for name, a in arrays.items()}
    out = nc.dram_tensor("out", (B, N, D), F32, kind="ExternalOutput").ap()
    program(nc, ins, out)
    return run_bass_kernel_spmd(nc, [arrays], core_ids=[0]).results[0]["out"]
```

```python
from contextlib import ExitStack

import concourse.bass as bass
import numpy as np
from concourse import mybir

F32 = mybir.dt.float32
F16 = mybir.dt.float16
ALU = mybir.AluOpType
ACT = mybir.ActivationFunctionType
AX = mybir.AxisListType

P = 128
B = 2
N = 1024
D = 128
H = 16
DH = 64
NT = N // P
TT = B * NT
T = B * N
NP = H // 2
INNER = H * DH
BANK = 512
Q_UP, K_UP = 2.0 ** 5, 2.0 ** 8
NEG = -1.0e30

E0, F0, CAP0 = 8, 512, int(T * 1.25 / 8)
E1, I1, SI, CAP1, TOP1 = 32, 64, 256, 256, 8


class Core:

    def __init__(self, nc, ctx, ins):
        self.nc, self.ctx, self.ins, self.named, self.count = nc, ctx, ins, {}, 0

    def sbuf(self, c, name, shape, dtype=F32):
        self.count += 1
        return c.enter_context(self.nc.sbuf_tensor(f"{name}_{self.count}", shape, dtype))

    def psum(self, c, name, width, dtype=F32):
        self.count += 1
        return c.enter_context(self.nc.psum_tensor(f"{name}_{self.count}", [P, width], dtype))

    def signals(self, names):
        out = []
        for n in names.split():
            if n not in self.named:
                self.named[n] = self.ctx.enter_context(self.nc.semaphore(n))
            out.append(self.named[n])
        return out

    def clear_signals(self):
        nums = sorted(s.num for s in self.named.values())
        if not nums:
            return
        with self.nc.Block() as block:
            @block.sync
            def _(sp):
                sp.sem_clear(range(nums[0], nums[-1] + 1))



def modulation(core, name, ident, mod, gate_a, gate_b, bias_row):
    nc, ins = core.nc, core.ins
    cond_in, trans_ready, condT_ready, modulated, gates_done, act_step, dve_step = core.signals(
        "cond_in trans_ready condT_ready modulated gates_done act_step dve_step")
    core.clear_signals()
    with ExitStack() as c:
        sb = lambda n, s: core.sbuf(c, n, s)
        W = sb("mod_w", [P, 6 * D])
        cT = sb("mod_cT", [P, B])
        e = sb("mod_e", [P, B])
        cb = sb("mod_cb", [P, B, P])
        t1 = sb("mod_t1", [P, 2 * B * D])
        t2 = sb("mod_t2", [P, 2 * B * D])
        t3 = sb("mod_t3", [P, 2 * B * D])
        ps_m = core.psum(c, "mod_pm", 6 * B)
        ps_g = core.psum(c, "mod_pg", 2 * B * D)
        block = c.enter_context(nc.Block())

        @block.sync
        def _(sp):
            sp.dma_start(W[:, :], ins[name + "_wmod"]).then_inc(cond_in, 16)
            with nc.allow_non_contiguous_dma(reason="256 values"):
                for b in range(B):
                    sp.dma_start(cT[:, b:b + 1], ins[name + "_c"][b, :].rearrange("(d a) -> d a", a=1)).then_inc(cond_in, 16)

        @block.scalar
        def _(act):
            act.wait_ge(cond_in, 48)
            nc.scalar.activation(e[:, :], cT[:, :], ACT.Exp, scale=-1.0).then_inc(act_step, 1)

        @block.vector
        def _(dve):
            dve.wait_ge(act_step, 1)
            nc.vector.tensor_scalar(e[:, :], e[:, :], 1.0, None, op0=ALU.add).then_inc(dve_step, 1)
            dve.wait_ge(dve_step, 1)
            nc.vector.reciprocal(e[:, :], e[:, :]).then_inc(dve_step, 1)
            dve.wait_ge(dve_step, 2)
            nc.vector.tensor_tensor(cT[:, :], cT[:, :], e[:, :], op=ALU.mult).then_inc(dve_step, 1)
            dve.wait_ge(dve_step, 3)
            nc.vector.tensor_copy(cb[:, :, :], cT[:, :].unsqueeze(2).to_broadcast([P, B, P])).then_inc(condT_ready, 1)
            dve.wait_ge(modulated, 1)
            nc.vector.tensor_copy(mod[:, :, :], ps_m[:, :].rearrange("p (k b) -> p k b", b=B)).then_inc(dve_step, 1)
            dve.wait_ge(dve_step, 4)
            for k in (1, 4):
                nc.vector.tensor_scalar(mod[:, k, :], mod[:, k, :], 1.0, None, op0=ALU.add).then_inc(dve_step, 1)
            count = 6

            def gate(x, a, size):
                nonlocal count
                nc.vector.tensor_scalar(a, x, 0.0, 2.0, op0=ALU.is_ge, op1=ALU.mult).then_inc(dve_step, 1)
                nc.vector.scalar_tensor_tensor(size, x, -1.0, x, op0=ALU.mult, op1=ALU.max).then_inc(dve_step, 1)
                count += 2
                dve.wait_ge(dve_step, count)
                nc.vector.tensor_scalar(size, size, 0.25, None, op0=ALU.max).then_inc(dve_step, 1)
                count += 1
                dve.wait_ge(dve_step, count)
                nc.vector.scalar_tensor_tensor(x, a, -1.0, size, op0=ALU.add, op1=ALU.mult).then_inc(dve_step, 1)
                count += 1
                dve.wait_ge(dve_step, count)

            for k in (2, 5):
                gate(mod[:, k, :], t2[:, 0:B], t3[:, 0:B])
            nc.vector.tensor_copy(t1[:, :], ps_g[:, :]).then_inc(dve_step, 1)
            count += 1
            dve.wait_ge(dve_step, count)
            gate(t1[:, :], t2[:, :], t3[:, :])
            half = B * D
            nc.vector.tensor_copy(gate_a[:, :, :], t1[:, 0:half].rearrange("p (b d) -> p b d", b=B)).then_inc(dve_step, 1)
            nc.vector.tensor_copy(gate_b[:, :, :], t1[:, half:2 * half].rearrange("p (b d) -> p b d", b=B)).then_inc(dve_step, 1)

        @block.tensor
        def _(pe):
            pe.wait_ge(condT_ready, 1)
            for k in range(6):
                nc.tensor.matmul(ps_m[:, B * k:B * k + B], W[:, D * k:D * k + D], cT[:, :], start=(k == 0), stop=True,
                                 skip_group_check=True)
            for g, k in enumerate((2, 5)):
                for b in range(B):
                    at = (g * B + b) * D
                    last = nc.tensor.matmul(ps_g[:, at:at + D], cb[:, b, :], W[:, D * k:D * k + D],
                                            start=(g == 0 and b == 0), stop=True, skip_group_check=True)
            last.then_inc(modulated, 1)



def layer_norm(core, X, xT, ident, expo, shift, scale, bias_row):
    nc = core.nc
    dve_step, powered, normed, xhatT, evac = core.signals("dve_step powered normed xhatT evac")
    core.clear_signals()
    with ExitStack() as c:
        xc = core.sbuf(c, "ln_xc", [P, TT, D])
        sq = core.sbuf(c, "ln_sq", [P, TT, D])
        m = core.sbuf(c, "ln_m", [P, TT])
        v = core.sbuf(c, "ln_v", [P, TT])
        ps = [core.psum(c, f"ln_ps{i}", BANK) for i in range(TT // 4)]
        block = c.enter_context(nc.Block())

        @block.vector
        def _(dve):
            nc.vector.tensor_reduce(m[:, :], X[:, :, :], axis=AX.X, op=ALU.add).then_inc(dve_step, 1)
            dve.wait_ge(dve_step, 1)
            nc.vector.tensor_scalar(m[:, :], m[:, :], 1.0 / D, None, op0=ALU.mult).then_inc(dve_step, 1)
            dve.wait_ge(dve_step, 2)
            nc.vector.tensor_tensor(xc[:, :, :], X[:, :, :], m[:, :].unsqueeze(2).to_broadcast([P, TT, D]),
                                    op=ALU.subtract).then_inc(dve_step, 1)
            dve.wait_ge(dve_step, 3)
            nc.vector.tensor_tensor(sq[:, :, :], xc[:, :, :], xc[:, :, :], op=ALU.mult).then_inc(dve_step, 1)
            dve.wait_ge(dve_step, 4)
            nc.vector.tensor_reduce(v[:, :], sq[:, :, :], axis=AX.X, op=ALU.add).then_inc(dve_step, 1)
            dve.wait_ge(dve_step, 5)
            nc.vector.tensor_scalar(v[:, :], v[:, :], 1.0 / D, 1e-5, op0=ALU.mult, op1=ALU.add).then_inc(dve_step, 1)
            dve.wait_ge(powered, 1)
            nc.vector.tensor_tensor(xc[:, :, :], xc[:, :, :], v[:, :].unsqueeze(2).to_broadcast([P, TT, D]),
                                    op=ALU.mult).then_inc(normed, 1)
            if bias_row is not None:
                for b in range(B):
                    rows = X[:, b * NT:(b + 1) * NT, :]
                    nc.vector.tensor_tensor(rows, rows, bias_row[:, b, :].unsqueeze(1).to_broadcast([P, NT, D]),
                                            op=ALU.add).then_inc(dve_step, 1)
            for i in range(0, TT // 4, 2):
                dve.wait_ge(xhatT, i + 1)
                b = i * 4 // NT
                nc.vector.tensor_scalar(xT[:, i * BANK:(i + 1) * BANK], ps[i][:, :], scale[:, b:b + 1], shift[:, b:b + 1],
                                        op0=ALU.mult, op1=ALU.add).then_inc(evac, 1)

        @block.gpsimd
        def _(pool):
            pool.wait_ge(dve_step, 6)
            nc.gpsimd.tensor_tensor(v[:, :], v[:, :], expo[:, 0:1].to_broadcast([P, TT]), op=ALU.pow).then_inc(powered, 1)

        @block.tensor
        def _(pe):
            pe.wait_ge(normed, 1)
            for i in range(TT // 4):
                for j in range(4):
                    last = nc.tensor.transpose(ps[i][:, j * P:(j + 1) * P], xc[:, 4 * i + j, :], ident[:, :])
                last.then_inc(xhatT, 1)

        @block.scalar
        def _(act):
            for i in range(1, TT // 4, 2):
                act.wait_ge(xhatT, i + 1)
                b = i * 4 // NT
                nc.scalar.activation(xT[:, i * BANK:(i + 1) * BANK], ps[i][:, :], ACT.Identity,
                                     scale=scale[:, b:b + 1], bias=shift[:, b:b + 1]).then_inc(evac, 1)



def project_qkv(core, layer, b, xT, w_qkv, qT, kT, V, ident, extra, q_dram=None, ident16=None):
    nc = core.nc
    (x_copied, q_made, k_made, v_made, v_out, squared_q, squared_k, dve_step, inverted, rooted, product,
     q_ready, k_ready, q_high, k_high, q_split, k_split, qT_made, kT_made, qT_out, kT_out, q_stored) = core.signals(
        "x_copied q_made k_made v_made v_out squared_q squared_k dve_step inverted rooted product "
        "q_ready k_ready q_high k_high q_split k_split qT_made kT_made qT_out kT_out q_stored")
    core.clear_signals()
    with ExitStack() as c:
        sb = lambda n, s: core.sbuf(c, n, s)
        xs = sb("qkv_x", [P, P])
        sq = [sb("qkv_sq", [P, INNER]) for _ in range(2)]
        qk = [sb("qkv_qk", [P, INNER]) for _ in range(2)]
        rn = [sb("qkv_rn", [P, H]) for _ in range(2)]
        U = [core.psum(c, "qkv_u", INNER) for _ in range(2)]
        Vp = core.psum(c, "qkv_v", INNER)
        parts = [core.sbuf(c, "qkv_parts", [P, H, 2, DH], F16) for _ in range(2 - 2 * layer)]
        Z = core.psum(c, "qkv_z", 2 * INNER, F16) if layer == 0 else core.psum(c, "qkv_z", INNER)
        made, squared, ready = (q_made, k_made), (squared_q, squared_k), (q_ready, k_ready)
        T_made, T_out, dst = (qT_made, kT_made), (qT_out, kT_out), (qT, kT)
        block = c.enter_context(nc.Block())
        heads = lambda t: t[:, :].rearrange("p (h d) -> p h d", d=DH)
        halves = lambda t: t[:, :].rearrange("p (h s d) -> p h s d", s=2, d=DH // 2)

        if layer == 1:
            @block.sync
            def _(sp):
                for t in range(NT):
                    sp.wait_ge(qT_out, 2 * t + 2)
                    sp.dma_start(q_dram[:, :, t * P:(t + 1) * P], qT[:, :, t * P:(t + 1) * P]).then_inc(q_stored, 16)
                sp.wait_ge(q_stored, 16 * NT)

        high, split = (q_high, k_high), (q_split, k_split)

        @block.gpsimd
        def _(pool):
            def low_parts(t, j, first):
                pool.wait_ge(high[j], t + 1)
                if not first:
                    pool.wait_ge(T_made[j], t)
                nc.gpsimd.tensor_tensor(parts[j][:, :, 1, :], heads(qk[j]), parts[j][:, :, 0, :],
                                        op=ALU.subtract).then_inc(split[j], 1)

            if layer == 1:
                pool.sem_inc(q_ready, 1)
                pool.sem_inc(k_ready, 1)
                with pool.Fori(0, NT) as t:
                    for j in range(2):
                        pool.wait_ge(product, 6 * t + 3 * j + 3)
                        nc.gpsimd.tensor_tensor(qk[j][:, :], qk[j][:, :], sq[j][:, :], op=ALU.add).then_inc(ready[j], 1)
            else:
                low_parts(0, 0, True)
                low_parts(0, 1, True)
                with pool.Fori(1, NT) as t:
                    low_parts(t, 0, False)
                    low_parts(t, 1, False)

        @block.tensor
        def _(pe):
            def project(t, j):
                pe.wait_ge(ready[j], t + 1)
                for h in range(2):
                    at = j * INNER + h * BANK
                    last = nc.tensor.matmul(U[j][:, h * BANK:(h + 1) * BANK], xs[:, :], w_qkv[:, at:at + BANK],
                                            start=True, stop=True)
                last.then_inc(made[j], 1)

            def project_v(t):
                pe.wait_ge(v_out, 2 * t + 2)
                for h in range(2):
                    at = 2 * INNER + h * BANK
                    last = nc.tensor.matmul(Vp[:, h * BANK:(h + 1) * BANK], xs[:, :], w_qkv[:, at:at + BANK],
                                            start=True, stop=True)
                last.then_inc(v_made, 1)

            def transpose(t, j):
                if j == 0:
                    pe.wait_ge(kT_out, 2 * t + 2)
                else:
                    pe.wait_ge(qT_out, 2 * t + 2)
                if layer == 0:
                    pe.wait_ge(split[j], t + 1)
                    for h in range(H):
                        last = nc.tensor.transpose(Z[:, h * P:(h + 1) * P], parts[j][:, h, :, :].rearrange("p s d -> p (s d)"),
                                                   ident16[:, :])
                else:
                    pe.wait_ge(ready[j], t + 2)
                    for a in range(NP):
                        last = nc.tensor.transpose(Z[:, a * P:(a + 1) * P], qk[j][:, a * P:(a + 1) * P], ident[:, :])
                last.then_inc(T_made[j], 1)

            pe.wait_ge(x_copied, 1)
            project(0, 0)
            project_v(0)
            project(0, 1)
            with pe.Fori(1, NT) as t:
                pe.wait_ge(x_copied, t + 1)
                project(t, 0)
                transpose(t - 1, 0)
                project_v(t)
                project(t, 1)
                transpose(t - 1, 1)
            transpose(NT - 1, 0)
            transpose(NT - 1, 1)

        @block.scalar
        def _(act):
            def square(t, j):
                act.wait_ge(made[j], t + 1)
                act.wait_ge(ready[j], t + 1)
                nc.scalar.activation(sq[j][:, :], U[j][:, :], ACT.Square).then_inc(squared[j], 1)

            def root(t, j):
                act.wait_ge(inverted, 2 * t + j + 1)
                nc.scalar.activation(rn[j][:, :], rn[j][:, :], ACT.Sqrt).then_inc(rooted, 1)

            def move_v(t):
                act.wait_ge(v_made, t + 1)
                for j in range(2):
                    nc.scalar.activation(V[:, bass.ds(t, 1), j * (H // 2):(j + 1) * (H // 2), :],
                                         Vp[:, j * BANK:(j + 1) * BANK].rearrange("p (a h d) -> p a h d", a=1, d=DH),
                                         ACT.Copy).then_inc(v_out, 1)

            def move_T(t, j):
                act.wait_ge(T_made[j], t + 1)
                z = Z[:, :].rearrange("p (a q) -> p a q", q=P)
                half = z.shape[1] // 2
                for s in range(2):
                    nc.scalar.activation(dst[j][:, half * s:half * s + half, bass.ts(t, P)], z[:, half * s:half * s + half, :],
                                         ACT.Copy).then_inc(T_out[j], 1)

            def high_parts(t, j, follows):
                act.wait_ge(ready[j], t + 2)
                if follows:
                    act.wait_ge(T_made[j], t)
                nc.scalar.activation(parts[j][:, :, 0, :], heads(qk[j]), ACT.Copy).then_inc(high[j], 1)

            def tile(t, follows):
                if layer == 0:
                    square(t, 0)
                if follows:
                    move_T(t - 1, 0)
                if layer == 0:
                    root(t, 0)
                move_v(t)
                if layer == 0:
                    square(t, 1)
                    high_parts(t, 0, follows)
                if follows:
                    move_T(t - 1, 1)
                if layer == 0:
                    root(t, 1)
                    high_parts(t, 1, follows)

            act.sem_inc(v_out, 2)
            act.sem_inc(kT_out, 2)
            tile(0, False)
            with act.Fori(1, NT) as t:
                tile(t, True)
            move_T(NT - 1, 0)
            move_T(NT - 1, 1)

        @block.vector
        def _(dve):
            def normalize(t, j, first):
                n = 2 * t + j
                dve.wait_ge(squared[j], t + 1)
                nc.vector.tensor_reduce(rn[j][:, :], heads(sq[j]), axis=AX.X, op=ALU.add).then_inc(dve_step, 1)
                dve.wait_ge(dve_step, 5 * t + 3 * j + 1)
                nc.vector.tensor_scalar(rn[j][:, :], rn[j][:, :], 1e-24, (Q_UP, K_UP)[j] ** -2.0, op0=ALU.max,
                                        op1=ALU.mult).then_inc(dve_step, 1)
                dve.wait_ge(dve_step, 5 * t + 3 * j + 2)
                if j == 0:
                    nc.vector.reciprocal(rn[j][:, :], rn[j][:, :]).then_inc(dve_step, 1)
                    dve.wait_ge(dve_step, 5 * t + 3)
                    nc.vector.tensor_tensor(rn[j][:, :], rn[j][:, :], extra[:, :], op=ALU.mult).then_inc(inverted, 1)
                else:
                    nc.vector.reciprocal(rn[j][:, :], rn[j][:, :]).then_inc(inverted, 1)
                dve.wait_ge(rooted, n + 1)
                if not first:
                    dve.wait_ge(split[j], t)
                nc.vector.tensor_tensor(heads(qk[j]), heads(U[j]), rn[j][:, :].unsqueeze(2).to_broadcast([P, H, DH]),
                                        op=ALU.mult).then_inc(ready[j], 1)

            def rotate(t, j, first):
                cos, sin = extra
                dve.wait_ge(made[j], t + 1)
                if not first:
                    dve.wait_ge(ready[j], t + 1)
                u, s, o = halves(U[j]), halves(sq[j]), halves(qk[j])
                half = DH // 2
                tab = lambda x: x[:, bass.ds(t, 1), :].to_broadcast([P, H, half])
                nc.vector.scalar_tensor_tensor(s[:, :, 0, :], u[:, :, 1, :], -1.0, tab(sin), op0=ALU.mult, op1=ALU.mult).then_inc(product, 1)
                nc.vector.tensor_tensor(s[:, :, 1, :], u[:, :, 0, :], tab(sin), op=ALU.mult).then_inc(product, 1)
                if not first:
                    dve.wait_ge(T_made[j], t)
                nc.vector.tensor_tensor(heads(qk[j]).rearrange("p h (s d) -> p h s d", s=2), u,
                                        cos[:, bass.ds(t, 1), :].unsqueeze(1).to_broadcast([P, H, 2, half]),
                                        op=ALU.mult).then_inc(product, 1)

            def copy_x(t):
                nc.vector.tensor_copy(xs[:, :], xT[:, bass.ts(t + b * NT, P)]).then_inc(x_copied, 1)

            def tile(t, first, last):
                step = normalize if layer == 0 else rotate
                step(t, 0, first)
                if not last:
                    dve.wait_ge(k_made, t + 1)
                    copy_x(t + 1)
                step(t, 1, first)

            copy_x(0)
            if layer == 0:
                dve.sem_inc(q_ready, 1)
                dve.sem_inc(k_ready, 1)
            tile(0, True, False)
            with dve.Fori(1, NT - 1) as t:
                tile(t, False, False)
            tile(NT - 1, False, True)



def cosine_attention(core, b, X, qT, kT, V, w_out, ident, gate):
    nc = core.nc
    (q_copied, scores_made, max_found, max_made, exp_made, sum_inv, probs_made, probsT_a, probsT_b, a_out, b_out, pv_made,
     oT_out, y_made, x_step, x_done) = core.signals(
        "q_copied scores_made max_found max_made exp_made sum_inv probs_made probsT_a probsT_b a_out b_out pv_made "
        "oT_out y_made x_step x_done")
    q_in = core.signals("q_in_first q_in_last")
    core.clear_signals()
    with ExitStack() as c:
        sb = lambda n, s: core.sbuf(c, n, s)
        pb = lambda n, w: core.psum(c, n, w)
        q_parts, q_swapped = (core.sbuf(c, n, [P, H, P], F16) for n in ("ca_q", "ca_qs"))
        probs = [sb(f"ca_p{i}", [P, N]) for i in range(4)]
        probsT = [sb(f"ca_pT{i}", [P, N]) for i in range(4)]
        nmax = sb("ca_nmax", [P, H])
        sums = sb("ca_sum", [P, H])
        oT = sb("ca_oT", [P, INNER])
        yg = sb("ca_yg", [P, D])
        S = [pb(f"ca_s{i}", N) for i in range(2)]
        Z = [pb(f"ca_z{i}", BANK) for i in range(2)]
        O = [pb(f"ca_o{i}", BANK) for i in range(2)]
        block = c.enter_context(nc.Block())

        def query_copies(i, part):
            heads, high, low = slice(part * H // 2, (part + 1) * H // 2), slice(0, DH), slice(DH, P)
            return [(to[rows, heads, :], qT[from_rows, heads, bass.ts(i, P)])
                    for to, rows, from_rows in ((q_parts, slice(0, P), slice(0, P)), (q_swapped, high, low), (q_swapped, low, high))]

        Y_AT = 6

        @block.tensor
        def _(pe):
            def scores(i, h, follows):
                if h >= 2 or follows:
                    pe.wait_ge(exp_made, i * H + h - 1)
                for q in (q_parts, q_swapped):
                    for j in range(2):
                        last = nc.tensor.matmul(S[h % 2][:, j * BANK:(j + 1) * BANK], q[:, h, :],
                                                kT[:, h, j * BANK:(j + 1) * BANK], start=(q is q_parts), stop=(q is q_swapped))
                last.then_inc(scores_made, 1)

            def transpose(i, h):
                pe.wait_ge(probs_made, i * H + h + 1)
                for half, done, out in ((0, probsT_a, a_out), (1, probsT_b, b_out)):
                    pe.wait_ge(out, i * H + h + 1)
                    for j in range(4):
                        at = (4 * half + j) * P
                        last = nc.tensor.transpose(Z[half][:, j * P:(j + 1) * P], probs[h % 4][:, at:at + P], ident[:, :])
                    last.then_inc(done, 1)

            def values(i, pair, part):
                h = 2 * pair
                pe.wait_ge(a_out, i * H + h + 3)
                pe.wait_ge(b_out, i * H + h + 3)
                if pair % 4 == 0:
                    pe.wait_ge(oT_out, 2 * i + pair // 4 + 1)
                for j in range(part * NT // 2, (part + 1) * NT // 2):
                    for s in range(2):
                        last = nc.tensor.matmul(O[pair // 4][DH * s:DH * s + DH, (pair % 4) * P:(pair % 4 + 1) * P],
                                                V[:, j, h + s, 0:DH], probsT[(h + s) % 4][:, j * P:(j + 1) * P],
                                                start=(j == 0), stop=(j == NT - 1))
                if part == 1:
                    last.then_inc(pv_made, 1)

            def project(i, heads_before):
                pe.wait_ge(oT_out, 2 * i + 4)
                pe.wait_ge(a_out, heads_before + 1)
                for j in range(NP):
                    last = nc.tensor.matmul(Z[0][:, 0:D], oT[:, j * P:(j + 1) * P], w_out[:, j, :],
                                            start=(j == 0), stop=(j == NP - 1))
                last.then_inc(y_made, 1)

            def tile(i, follows):
                for h in range(H):
                    if h % (H // 2) == 0 and follows:
                        pe.wait_ge(q_in[2 * h // H], 48 * i)
                    elif h % (H // 2) == 0:
                        pe.wait_ge(q_copied, 3 + 6 * h // H)
                    scores(i, h, follows)
                    if h >= 2:
                        transpose(i, h - 2)
                    elif follows:
                        transpose(i - 1, H - 2 + h)
                    if h >= 4:
                        values(i, (h - 4) // 2, h % 2)
                    elif follows:
                        values(i - 1, (h + H - 4) // 2, h % 2)
                    if follows and h == Y_AT:
                        project(i - 1, i * H + h - 1)
                        pe.wait_ge(x_step, i)

            tile(0, False)
            with pe.Fori(1, NT) as i:
                tile(i, True)
            transpose(NT - 1, H - 2)
            values(NT - 1, NP - 2, 0)
            transpose(NT - 1, H - 1)
            values(NT - 1, NP - 2, 1)
            values(NT - 1, NP - 1, 0)
            values(NT - 1, NP - 1, 1)
            project(NT - 1, NT * H)

        @block.sync
        def _(sp):
            with sp.Fori(1, NT) as i:
                for part in range(2):
                    sp.wait_ge(scores_made, i * H - H + (part + 1) * H // 2)
                    for to, from_ in query_copies(i, part):
                        sp.dma_start(to, from_).then_inc(q_in[part], 16)

        @block.vector
        def _(dve):
            def biggest(i, h):
                dve.wait_ge(scores_made, i * H + h + 1)
                nc.vector.tensor_reduce(nmax[:, h:h + 1], S[h % 2][:, :], axis=AX.X, op=ALU.max,
                                        negate=True).then_inc(max_found, 1)
                dve.wait_ge(max_found, i * H + h + 1)
                nc.vector.tensor_scalar(nmax[:, h:h + 1], nmax[:, h:h + 1], 1.0 / (Q_UP * K_UP), None,
                                        op0=ALU.mult).then_inc(max_made, 1)

            def normalize(i, h):
                dve.wait_ge(exp_made, i * H + h + 1)
                nc.vector.reciprocal(sums[:, h:h + 1], sums[:, h:h + 1]).then_inc(sum_inv, 1)
                dve.wait_ge(sum_inv, i * H + h + 1)
                nc.vector.tensor_scalar(probs[h % 4][:, :], probs[h % 4][:, :], sums[:, h:h + 1], None,
                                        op0=ALU.mult).then_inc(probs_made, 1)

            def evacuate(i, h, follows):
                dve.wait_ge(probsT_a, i * H + h + 1)
                if h >= 4 or follows:
                    dve.wait_ge(pv_made, i * NP + h // 2 - 1)
                nc.vector.tensor_copy(probsT[h % 4][:, 0:BANK], Z[0][:, :]).then_inc(a_out, 1)

            def evacuate_out(i, k, follows):
                dve.wait_ge(pv_made, i * NP + 4 * k + 4)
                if follows:
                    dve.wait_ge(y_made, i)
                nc.vector.tensor_copy(oT[:, k * BANK:(k + 1) * BANK], O[k][:, :]).then_inc(oT_out, 1)

            def add_to_x(i):
                dve.wait_ge(y_made, i + 1)
                nc.vector.tensor_tensor(yg[:, :], Z[0][:, 0:D], gate[:, b, :], op=ALU.mult).then_inc(x_step, 1)
                dve.wait_ge(x_step, i + 1)
                row = X[:, bass.ds(i + b * NT, 1), :]
                nc.vector.tensor_tensor(row, row, yg[:, :].unsqueeze(1), op=ALU.add).then_inc(x_done, 1)

            def tile(i, follows):
                for h in range(H):
                    biggest(i, h)
                    if h >= 1:
                        normalize(i, h - 1)
                    elif follows:
                        normalize(i - 1, H - 1)
                    if h >= 2:
                        evacuate(i, h - 2, follows)
                    elif follows:
                        evacuate(i - 1, H - 2 + h, True)
                    if follows and h == 4:
                        evacuate_out(i - 1, 1, True)
                    if follows and h == Y_AT:
                        add_to_x(i - 1)
                    if h == 12:
                        evacuate_out(i, 0, follows)

            dve.sem_inc(a_out, 1)
            dve.sem_inc(oT_out, 2)
            for part in range(2):
                for to, from_ in query_copies(0, part):
                    nc.vector.tensor_copy(to, from_).then_inc(q_copied, 1)
            tile(0, False)
            with dve.Fori(1, NT) as i:
                tile(i, True)
            normalize(NT - 1, H - 1)
            evacuate(NT - 1, H - 2, True)
            evacuate(NT - 1, H - 1, True)
            evacuate_out(NT - 1, 1, True)
            add_to_x(NT - 1)

        @block.scalar
        def _(act):
            def exponentiate(i, h, follows):
                act.wait_ge(max_made, i * H + h + 1)
                if h >= 4 or follows:
                    act.wait_ge(probsT_b, i * H + h - 3)
                nc.scalar.activation(probs[h % 4][:, :], S[h % 2][:, :], ACT.Exp, bias=nmax[:, h:h + 1], scale=1.0 / (Q_UP * K_UP),
                                     accum_out=sums[:, h:h + 1]).then_inc(exp_made, 1)

            def evacuate(i, h, follows):
                act.wait_ge(probsT_b, i * H + h + 1)
                if h >= 4 or follows:
                    act.wait_ge(pv_made, i * NP + h // 2 - 1)
                nc.scalar.activation(probsT[h % 4][:, BANK:N], Z[1][:, :], ACT.Copy).then_inc(b_out, 1)

            def tile(i, follows):
                for h in range(H):
                    if h >= 2:
                        evacuate(i, h - 2, follows)
                    elif follows:
                        evacuate(i - 1, H - 2 + h, True)
                    exponentiate(i, h, follows)

            act.sem_inc(b_out, 1)
            tile(0, False)
            with act.Fori(1, NT) as i:
                tile(i, True)
            evacuate(NT - 1, H - 2, True)
            evacuate(NT - 1, H - 1, True)



def route_first(core, xT, wts_dram, ident, tri, ones):
    nc, ins = core.nc, core.ins
    (loaded, logits_made, act_step, dve_step, pick_made, counts_made, w_made, wT_made, wT_out, stored) = core.signals(
        "loaded logits_made act_step dve_step pick_made counts_made w_made wT_made wT_out stored")
    core.clear_signals()
    with ExitStack() as c:
        sb = lambda n: core.sbuf(c, n, [P, TT, E0])
        small = lambda n: core.sbuf(c, n, [P, TT])
        Wr = core.sbuf(c, "wr", [P, E0])
        rev = core.sbuf(c, "rev", [P, E0])
        reset = core.sbuf(c, "reset", [P, 2 * E0 * TT])
        p, e, q = sb("r_p"), sb("r_e"), sb("r_q")
        m, s, r, top, top2 = small("r_m"), small("r_s"), small("r_r"), small("r_t1"), small("r_t2")
        OH = core.sbuf(c, "r_oh", [P, 2 * E0, TT])
        RK = core.sbuf(c, "r_rk", [P, 2 * E0, TT])
        TO = core.sbuf(c, "r_to", [P, 2 * E0, TT])
        w = sb("r_w")
        wT = core.sbuf(c, "r_wT", [E0, T])
        psl = core.psum(c, "r_l", TT * E0)
        psc = core.psum(c, "r_c", 2 * E0 * TT)
        pst = core.psum(c, "r_tot", 2 * E0 * TT)
        psw = core.psum(c, "r_wt", T)
        block = c.enter_context(nc.Block())
        wide = lambda t: t[:, :].unsqueeze(2).to_broadcast([P, TT, E0])
        revb = rev[:, :].unsqueeze(1).to_broadcast([P, TT, E0])
        pick = lambda k: OH[:, k * E0:(k + 1) * E0, :].rearrange("p e t -> p t e")
        flat = lambda t: t[:, :, :].rearrange("p g t -> p (g t)")

        @block.sync
        def _(sp):
            sp.dma_start(Wr[:, :], ins["L0_ffn_Wr"]).then_inc(loaded, 16)
            sp.dma_start(rev[:, :], ins["const_rev"].to_broadcast([P, E0])).then_inc(loaded, 16)
            sp.dma_start(reset[:, :], ins["const_reset"][:, 0:2 * E0 * TT].to_broadcast([P, 2 * E0 * TT])).then_inc(loaded, 16)
            sp.wait_ge(wT_out, 4)
            sp.dma_start(wts_dram[0:E0, :], wT[:, :]).then_inc(stored, 16)
            sp.wait_ge(stored, 16)

        @block.tensor
        def _(pe):
            pe.wait_ge(loaded, 48)
            for t in range(TT):
                last = nc.tensor.matmul(psl[:, t * E0:(t + 1) * E0], xT[:, t * P:(t + 1) * P], Wr[:, :],
                                        start=(t == 0), stop=True, skip_group_check=True)
            last.then_inc(logits_made, 1)
            pe.wait_ge(pick_made, 2)
            nc.tensor.matmul(psc[:, :], tri[:, :], flat(OH), start=True, stop=True)
            nc.tensor.matmul(pst[:, :], ones[:, :], flat(OH), start=True, stop=True).then_inc(counts_made, 1)
            pe.wait_ge(w_made, 1)
            for t in range(TT):
                last = nc.tensor.transpose(psw[0:E0, t * P:(t + 1) * P], w[:, t, :], ident[:, :])
                if t % 4 == 3:
                    last.then_inc(wT_made, 1)

        @block.scalar
        def _(act):
            act.wait_ge(dve_step, 2)
            nc.scalar.activation(e[:, :, :], e[:, :, :], ACT.Exp).then_inc(act_step, 1)
            for j in range(4):
                act.wait_ge(wT_made, j + 1)
                nc.scalar.activation(wT[:, j * BANK:(j + 1) * BANK], psw[0:E0, j * BANK:(j + 1) * BANK],
                                     ACT.Copy).then_inc(wT_out, 1)

        @block.vector
        def _(dve):
            done = 0
            dve.wait_ge(loaded, 48)

            def then(ins_):
                nonlocal done
                ins_.then_inc(dve_step, 1)
                done += 1
                dve.wait_ge(dve_step, done)

            dve.wait_ge(logits_made, 1)
            l = psl[:, :].rearrange("p (t e) -> p t e", e=E0)
            then(nc.vector.tensor_reduce(m[:, :], l, axis=AX.X, op=ALU.max))
            then(nc.vector.tensor_tensor(e[:, :, :], l, wide(m), op=ALU.subtract))
            dve.wait_ge(act_step, 1)
            then(nc.vector.tensor_reduce(s[:, :], e[:, :, :], axis=AX.X, op=ALU.add))
            then(nc.vector.reciprocal(r[:, :], s[:, :]))
            then(nc.vector.tensor_tensor(p[:, :, :], e[:, :, :], wide(r), op=ALU.mult))
            for k, best in enumerate((top, top2)):
                then(nc.vector.tensor_reduce(best[:, :], p[:, :, :], axis=AX.X, op=ALU.max))
                then(nc.vector.tensor_tensor(q[:, :, :], p[:, :, :], wide(best), op=ALU.is_equal))
                then(nc.vector.tensor_tensor(q[:, :, :], q[:, :, :], revb, op=ALU.mult))
                then(nc.vector.tensor_reduce(m[:, :], q[:, :, :], axis=AX.X, op=ALU.max))
                then(nc.vector.tensor_tensor(pick(k), revb, wide(m), op=ALU.is_equal))
                nc.vector.sem_inc(pick_made, 1)
                if k == 0:
                    then(nc.vector.scalar_tensor_tensor(p[:, :, :], pick(k), -2.0, p[:, :, :], op0=ALU.mult, op1=ALU.add))
            then(nc.vector.tensor_tensor(s[:, :], top[:, :], top2[:, :], op=ALU.add))
            then(nc.vector.reciprocal(r[:, :], s[:, :]))
            then(nc.vector.tensor_tensor(top[:, :], top[:, :], r[:, :], op=ALU.mult))
            then(nc.vector.tensor_tensor(top2[:, :], top2[:, :], r[:, :], op=ALU.mult))
            dve.wait_ge(counts_made, 1)
            then(nc.vector.tensor_copy(flat(TO), pst[:, :]))
            then(nc.vector.tensor_tensor_scan(flat(RK), reset[:, :], flat(TO), 0.0, op0=ALU.mult, op1=ALU.add))
            then(nc.vector.tensor_tensor(flat(RK), flat(RK), flat(TO), op=ALU.subtract))
            then(nc.vector.tensor_tensor(flat(RK), flat(RK), psc[:, :], op=ALU.add))
            then(nc.vector.scalar_tensor_tensor(flat(OH), flat(RK), float(CAP0), flat(OH), op0=ALU.is_le, op1=ALU.mult))
            then(nc.vector.tensor_tensor(q[:, :, :], pick(0), wide(top), op=ALU.mult))
            then(nc.vector.tensor_tensor(w[:, :, :], pick(1), wide(top2), op=ALU.mult))
            then(nc.vector.tensor_tensor(w[:, :, :], w[:, :, :], q[:, :, :], op=ALU.add))
            nc.vector.sem_inc(w_made, 1)



def experts_first(core, X, xT, wts_dram, ident, gate_fm):
    nc, ins = core.nc, core.ins
    FC, RING = F0 // P, 4
    (base_in, w_in0, w_in1, base_made, h_made, g_made, gw_made, down_made, y_out, yT_made, x_done) = core.signals(
        "base_in w_in0 w_in1 base_made h_made g_made gw_made down_made y_out yT_made x_done")
    core.clear_signals()
    w_in = (w_in0, w_in1)
    NJ = T // BANK
    U = NJ * FC
    with ExitStack() as c:
        W1 = [core.sbuf(c, "w1", [P, F0]) for _ in range(2)]
        b1 = [core.sbuf(c, "b1", [P, FC]) for _ in range(2)]
        W2 = [core.sbuf(c, "w2", [P, FC, D]) for _ in range(2)]
        WB = [core.sbuf(c, "wb", [P, T]) for _ in range(2)]
        G = [core.sbuf(c, "g", [P, BANK]) for _ in range(RING)]
        b2 = core.sbuf(c, "b2", [E0, D])
        wT = core.sbuf(c, "wT", [E0, T])
        yT = core.sbuf(c, "yT", [P, T])
        Hp = [core.psum(c, "hp", BANK) for _ in range(RING)]
        Y = [core.psum(c, "y", BANK) for _ in range(NJ)]
        block = c.enter_context(nc.Block())

        @block.sync
        def _(sp):
            sp.dma_start(b2[:, :], ins["L0_ffn_b2"]).then_inc(base_in, 16)
            sp.dma_start(wT[:, :], wts_dram[0:E0, :]).then_inc(base_in, 16)
            with sp.Fori(0, E0 // 2) as i:
                for s in range(2):
                    e = 2 * i + s
                    sp.wait_ge(down_made, (e + 1) * U)
                    sp.dma_start(W1[s][:, :], ins["L0_ffn_W1"][bass.ds(e, 1), :, :].rearrange("e p f -> p (e f)")).then_inc(w_in[s], 16)
                    with nc.allow_non_contiguous_dma(reason="512 values"):
                        sp.dma_start(b1[s][:, :], ins["L0_ffn_b1"][bass.ds(e, 1), :].rearrange("e (c p) -> p (e c)", p=P)).then_inc(w_in[s], 16)
                    sp.dma_start(W2[s][:, :, :], ins["L0_ffn_W2"][bass.ds(e, 1), :, :].rearrange("e (c p) d -> p (e c) d", p=P)).then_inc(w_in[s], 16)
                    sp.dma_start(WB[s][:, :], wts_dram[bass.ds(e, 1), :].to_broadcast([P, T])).then_inc(w_in[s], 16)

        @block.tensor
        def _(pe):
            pe.wait_ge(base_in, 32)
            for j in range(NJ):
                nc.tensor.matmul(Y[j][:, :], b2[:, :], wT[:, j * BANK:(j + 1) * BANK], start=True, stop=False,
                                 skip_group_check=True)

            def hidden(s, k, n):
                j, f = divmod(k, FC)
                pe.wait_ge(g_made, n + k + 1)
                nc.tensor.matmul(Hp[k % RING][:, :], W1[s][:, f * P:(f + 1) * P], xT[:, j * BANK:(j + 1) * BANK],
                                 start=True, stop=True).then_inc(h_made, 1)

            def down(s, k, n):
                j, f = divmod(k, FC)
                pe.wait_ge(gw_made, n + k + 1)
                nc.tensor.matmul(Y[j][:, :], W2[s][:, f, :], G[k % RING][:, :], start=False, stop=False,
                                 skip_group_check=True).then_inc(down_made, 1)

            pe.sem_inc(down_made, 2 * U)
            with pe.Fori(0, E0 // 2) as i:
                for s in range(2):
                    pe.wait_ge(w_in[s], 64 * i + 64)
                    n = (2 * i + s) * U
                    for k in range(U + 2):
                        if k < U:
                            hidden(s, k, n)
                        if k >= 2:
                            down(s, k - 2, n)
            for j in range(NJ):
                pe.wait_ge(y_out, j + 1)
                for t in range(4):
                    at = j * BANK + t * P
                    last = nc.tensor.transpose(Hp[j][:, t * P:(t + 1) * P], yT[:, at:at + P], ident[:, :])
                last.then_inc(yT_made, 1)

        @block.scalar
        def _(act):
            act.sem_inc(g_made, RING)
            with act.Fori(0, E0 // 2) as i:
                for s in range(2):
                    act.wait_ge(w_in[s], 64 * i + 64)
                    n = (2 * i + s) * U
                    for k in range(U):
                        act.wait_ge(h_made, n + k + 1)
                        act.wait_ge(down_made, n + k + 1 - RING + 2 * U)
                        nc.scalar.activation(G[k % RING][:, :], Hp[k % RING][:, :], ACT.Gelu,
                                             bias=b1[s][:, k % FC:k % FC + 1]).then_inc(g_made, 1)

        @block.vector
        def _(dve):
            with dve.Fori(0, E0 // 2) as i:
                for s in range(2):
                    dve.wait_ge(w_in[s], 64 * i + 64)
                    n = (2 * i + s) * U
                    for k in range(U):
                        j = k // FC
                        dve.wait_ge(g_made, n + k + 1 + RING)
                        nc.vector.tensor_tensor(G[k % RING][:, :], G[k % RING][:, :], WB[s][:, j * BANK:(j + 1) * BANK],
                                                op=ALU.mult).then_inc(gw_made, 1)
            dve.wait_ge(down_made, (2 + E0) * U)
            add_transposed(nc, dve, X, Y, yT, Hp, gate_fm, y_out, yT_made, x_done)


def add_transposed(nc, dve, X, Y, yT, back, gate_fm, y_out, yT_made, x_done):
    for j in range(T // BANK):
        b = j * BANK // N
        nc.vector.tensor_scalar(yT[:, j * BANK:(j + 1) * BANK], Y[j][:, :], gate_fm[:, b:b + 1], None,
                                op0=ALU.mult).then_inc(y_out, 1)
    for j in range(T // BANK):
        dve.wait_ge(yT_made, j + 1)
        rows = X[:, 4 * j:4 * j + 4, :]
        nc.vector.tensor_tensor(rows, rows, back[j][:, :].rearrange("p (t d) -> p t d", d=D), op=ALU.add).then_inc(x_done, 1)



def prepare_second(core, ident, guT, dnT, rwT, sgT, suT, sdT):
    nc, ins = core.nc, core.ins
    loaded, banked, out_made = core.signals("loaded banked out_made")
    core.clear_signals()
    NPAIR = E1 // 2
    with ExitStack() as c:
        gu = core.sbuf(c, "gu", [P, E1, D])
        dn = core.sbuf(c, "dn", [P, E1, I1])
        rw = core.sbuf(c, "rw", [E1, D])
        sg = core.sbuf(c, "sg", [P, 2, D])
        su = core.sbuf(c, "su", [P, 2, D])
        sd = core.sbuf(c, "sd", [P, SI])
        Z = [core.psum(c, "z", BANK) for _ in range(4)]
        block = c.enter_context(nc.Block())

        batches = []
        for k in range(NPAIR // 2):
            src = [gu[:, 4 * k + e, :] for e in range(4)]
            batches.append((src, [(guT[:, 2 * k + a, s, :, :], lambda z, a=a, s=s: z[:, :].rearrange(
                "h (a e s i) -> h a e s i", a=2, e=2, s=2)[:, a, :, s, :]) for a in range(2) for s in range(2)]))
        for k in range(NPAIR // 4):
            src = [dn[:, 8 * k + 2 * e:8 * k + 2 * e + 2, :] for e in range(4)]
            batches.append((src, [(dnT[:, 4 * k:4 * k + 4, :], lambda z: z[:, :].rearrange("p (a h) -> p a h", a=4))]))
        batches.append(([sg[:, 0, :], sg[:, 1, :], su[:, 0, :], su[:, 1, :]],
                        [(sgT[:, :], lambda z: z[:, 0:SI]), (suT[:, :], lambda z: z[:, SI:2 * SI])]))
        batches.append(([sd[:, 0:P], sd[:, P:SI], rw[:, :]],
                        [(sdT[:, :, :], lambda z: z[:, 0:SI].rearrange("p (a h) -> p a h", a=2)),
                         (rwT[:, :], lambda z: z[:, SI:SI + E1])]))
        copies = [len(dst) for _, dst in batches]

        @block.sync
        def _(sp):
            sp.dma_start(gu[:, :, :], ins["L1_ffn_gate_up_proj"].rearrange("e o h -> o e h")).then_inc(loaded, 16)
            sp.dma_start(dn[:, :, :], ins["L1_ffn_down_proj"].rearrange("e h i -> h e i")).then_inc(loaded, 16)
            sp.dma_start(rw[:, :], ins["L1_ffn_router_weight"]).then_inc(loaded, 16)
            sp.dma_start(sg[:, :, :], ins["L1_ffn_shared_gate"].rearrange("(a p) h -> p a h", p=P)).then_inc(loaded, 16)
            sp.dma_start(su[:, :, :], ins["L1_ffn_shared_up"].rearrange("(a p) h -> p a h", p=P)).then_inc(loaded, 16)
            sp.dma_start(sd[:, :], ins["L1_ffn_shared_down"]).then_inc(loaded, 16)

        @block.tensor
        def _(pe):
            pe.wait_ge(loaded, 96)
            for n, (src, _) in enumerate(batches):
                if n >= 4:
                    pe.wait_ge(out_made, sum(copies[:n - 3]))
                for j, x in enumerate(src):
                    x = x.rearrange("p a i -> p (a i)") if len(x.shape) == 3 else x
                    rows = x.shape[0]
                    last = nc.tensor.transpose(Z[n % 4][:, j * P:j * P + rows], x, ident[0:rows, 0:rows])
                last.then_inc(banked, 1)

        @block.vector
        def _(dve):
            for n, (_, dst) in enumerate(batches):
                dve.wait_ge(banked, n + 1)
                for to, view in dst:
                    nc.vector.tensor_copy(to, view(Z[n % 4])).then_inc(out_made, 1)


def route_second(core, xT, wts_dram, ident, tri, ones, rwT):
    nc, ins = core.nc, core.ins
    (loaded, logits_made, act_step, dve_step, pick_made, counts_made, w_made, wT_made, wT_out, stored) = core.signals(
        "loaded logits_made act_step dve_step pick_made counts_made w_made wT_made wT_out stored")
    core.clear_signals()
    W = TT * E1
    with ExitStack() as c:
        sb = lambda n: core.sbuf(c, n, [P, TT, E1])
        small = lambda n: core.sbuf(c, n, [P, TT])
        bias = core.sbuf(c, "bias", [P, E1])
        reset_e = core.sbuf(c, "reset_e", [P, W])
        reset_t = core.sbuf(c, "reset_t", [P, W])
        score, v, gt, eq, rk = sb("score"), sb("v"), sb("gt"), sb("eq"), sb("rk")
        top = core.sbuf(c, "top", [P, TT, 8])
        room, s, r = small("room"), small("s"), small("r")
        OH, RK, TO = (core.sbuf(c, n, [P, E1, TT]) for n in ("oh", "rk", "to"))
        w = sb("w")
        wT = core.sbuf(c, "wT", [E1, T])
        psl = core.psum(c, "l", W)
        psc = core.psum(c, "c", W)
        pst = core.psum(c, "tot", W)
        psw = core.psum(c, "wt", T)
        block = c.enter_context(nc.Block())
        wide = lambda t: t[:, :].unsqueeze(2).to_broadcast([P, TT, E1])
        byt = lambda t: t[:, :, :].rearrange("p e t -> p t e")
        flat = lambda t: t[:, :, :].rearrange("p a b -> p (a b)")

        @block.sync
        def _(sp):
            sp.dma_start(bias[:, :], ins["L1_ffn_e_score_correction_bias"].rearrange("(a e) -> a e", a=1).to_broadcast([P, E1])).then_inc(loaded, 16)
            sp.dma_start(reset_t[:, :], ins["const_reset"].to_broadcast([P, W])).then_inc(loaded, 16)
            sp.dma_start(reset_e[:, :], ins["const_reset_e"].to_broadcast([P, W])).then_inc(loaded, 16)
            sp.wait_ge(wT_out, 4)
            sp.dma_start(wts_dram[:, :], wT[:, :]).then_inc(stored, 16)
            sp.wait_ge(stored, 16)

        @block.tensor
        def _(pe):
            for t in range(TT):
                last = nc.tensor.matmul(psl[:, t * E1:(t + 1) * E1], xT[:, t * P:(t + 1) * P], rwT[:, :],
                                        start=(t == 0), stop=True, skip_group_check=True)
            last.then_inc(logits_made, 1)
            pe.wait_ge(pick_made, 1)
            nc.tensor.matmul(psc[:, :], tri[:, :], flat(OH), start=True, stop=True)
            nc.tensor.matmul(pst[:, :], ones[:, :], flat(OH), start=True, stop=True).then_inc(counts_made, 1)
            pe.wait_ge(w_made, 1)
            for t in range(TT):
                last = nc.tensor.transpose(psw[0:E1, t * P:(t + 1) * P], w[:, t, :], ident[:, :])
                if t % 4 == 3:
                    last.then_inc(wT_made, 1)

        @block.scalar
        def _(act):
            act.wait_ge(logits_made, 1)
            nc.scalar.activation(flat(score), psl[:, :], ACT.Sigmoid).then_inc(act_step, 1)
            for j in range(4):
                act.wait_ge(wT_made, j + 1)
                nc.scalar.activation(wT[:, j * BANK:(j + 1) * BANK], psw[0:E1, j * BANK:(j + 1) * BANK],
                                     ACT.Copy).then_inc(wT_out, 1)

        @block.vector
        def _(dve):
            done = 0
            dve.wait_ge(loaded, 48)

            def then(ins_):
                nonlocal done
                ins_.then_inc(dve_step, 1)
                done += 1
                dve.wait_ge(dve_step, done)

            dve.wait_ge(act_step, 1)
            then(nc.vector.tensor_tensor(v[:, :, :], score[:, :, :], bias[:, :].unsqueeze(1).to_broadcast([P, TT, E1]), op=ALU.add))
            for t in range(TT):
                nc.vector.max(top[:, t, :], v[:, t, :]).then_inc(dve_step, 1)
            done += TT
            dve.wait_ge(dve_step, done)
            eighth = top[:, :, TOP1 - 1:TOP1].to_broadcast([P, TT, E1])
            then(nc.vector.tensor_tensor(gt[:, :, :], v[:, :, :], eighth, op=ALU.is_gt))
            then(nc.vector.tensor_tensor(eq[:, :, :], v[:, :, :], eighth, op=ALU.is_equal))
            then(nc.vector.tensor_reduce(room[:, :], gt[:, :, :], axis=AX.X, op=ALU.add))
            then(nc.vector.tensor_scalar(room[:, :], room[:, :], -1.0, float(TOP1), op0=ALU.mult, op1=ALU.add))
            then(nc.vector.tensor_tensor_scan(flat(rk), reset_e[:, :], flat(eq), 0.0, op0=ALU.mult, op1=ALU.add))
            then(nc.vector.tensor_tensor(rk[:, :, :], rk[:, :, :], wide(room), op=ALU.is_le))
            then(nc.vector.tensor_tensor(eq[:, :, :], eq[:, :, :], rk[:, :, :], op=ALU.mult))
            then(nc.vector.tensor_tensor(byt(OH), eq[:, :, :], gt[:, :, :], op=ALU.add))
            nc.vector.sem_inc(pick_made, 1)
            then(nc.vector.tensor_tensor(w[:, :, :], score[:, :, :], byt(OH), op=ALU.mult))
            then(nc.vector.tensor_reduce(s[:, :], w[:, :, :], axis=AX.X, op=ALU.add))
            then(nc.vector.tensor_scalar(s[:, :], s[:, :], 1e-20, None, op0=ALU.add))
            then(nc.vector.reciprocal(r[:, :], s[:, :]))
            then(nc.vector.tensor_tensor(w[:, :, :], w[:, :, :], wide(r), op=ALU.mult))
            dve.wait_ge(counts_made, 1)
            then(nc.vector.tensor_copy(flat(TO), pst[:, :]))
            then(nc.vector.tensor_tensor_scan(flat(RK), reset_t[:, :], flat(TO), 0.0, op0=ALU.mult, op1=ALU.add))
            then(nc.vector.tensor_tensor(flat(RK), flat(RK), flat(TO), op=ALU.subtract))
            then(nc.vector.tensor_tensor(flat(RK), flat(RK), psc[:, :], op=ALU.add))
            then(nc.vector.tensor_scalar(flat(RK), flat(RK), float(CAP1), 2.5, op0=ALU.is_le, op1=ALU.mult))
            then(nc.vector.tensor_tensor(w[:, :, :], w[:, :, :], byt(RK), op=ALU.mult))
            nc.vector.sem_inc(w_made, 1)


def experts_second(core, X, xT, wts_dram, ident, gate_fm, guT, dnT, sgT, suT, sdT):
    nc = core.nc
    (wb_in0, wb_in1, g_made, u_made, g_cut, u_cut, u_scaled, silu_made, prod_made, down_made, y_out, yT_made, x_done) = core.signals(
        "wb_in0 wb_in1 g_made u_made g_cut u_cut u_scaled silu_made prod_made down_made y_out yT_made x_done")
    core.clear_signals()
    wb_in = (wb_in0, wb_in1)
    NJ, NPAIR, LIMIT, R = T // BANK, E1 // 2, 7.0, 2
    with ExitStack() as c:
        WB = [core.sbuf(c, "wb", [P, T]) for _ in range(2)]
        g, a, u, h = ([core.sbuf(c, n, [P, BANK]) for _ in range(R)] for n in "gauh")
        yT = core.sbuf(c, "yT", [P, T])
        Gp = [core.psum(c, "gp", BANK) for _ in range(R)]
        Up = [core.psum(c, "up", BANK) for _ in range(R)]
        Y = [core.psum(c, "y", BANK) for _ in range(NJ)]
        block = c.enter_context(nc.Block())
        units = [(m, j) for m in range(-2, NPAIR) for j in range(NJ)]

        @block.sync
        def _(sp):
            for m in range(NPAIR):
                if m >= 2:
                    sp.wait_ge(u_scaled, (m - 1) * NJ)
                for e in range(2):
                    sp.dma_start(WB[m % 2][e * I1:(e + 1) * I1, :],
                                 wts_dram[2 * m + e:2 * m + e + 1, :].to_broadcast([I1, T])).then_inc(wb_in[m % 2], 16)

        @block.tensor
        def _(pe):
            def up(n):
                m, j = units[n]
                if n >= R:
                    pe.wait_ge(g_cut, n - R + 1)
                    pe.wait_ge(u_cut, n - R + 1)
                wg = sgT[:, (m + 2) * P:(m + 3) * P] if m < 0 else guT[:, m, 0, :, :].rearrange("h e i -> h (e i)")
                wu = suT[:, (m + 2) * P:(m + 3) * P] if m < 0 else guT[:, m, 1, :, :].rearrange("h e i -> h (e i)")
                nc.tensor.matmul(Gp[n % R][:, :], wg, xT[:, j * BANK:(j + 1) * BANK], start=True, stop=True).then_inc(g_made, 1)
                nc.tensor.matmul(Up[n % R][:, :], wu, xT[:, j * BANK:(j + 1) * BANK], start=True, stop=True).then_inc(u_made, 1)

            def down(n):
                m, j = units[n]
                pe.wait_ge(prod_made, n + 1)
                wd = sdT[:, m + 2, :] if m < 0 else dnT[:, m, :]
                nc.tensor.matmul(Y[j][:, :], wd, h[n % R][:, :], start=(m == -2), stop=(m == NPAIR - 1),
                                 skip_group_check=True).then_inc(down_made, 1)

            for n in range(len(units) + 2):
                if n < len(units):
                    up(n)
                if n >= 2:
                    down(n - 2)
            for j in range(NJ):
                pe.wait_ge(y_out, j + 1)
                for t in range(4):
                    at = j * BANK + t * P
                    last = nc.tensor.transpose((Gp + Up)[j][:, t * P:(t + 1) * P], yT[:, at:at + P], ident[:, :])
                last.then_inc(yT_made, 1)

        @block.vector
        def _(dve):
            for n, (m, j) in enumerate(units):
                dve.wait_ge(g_made, n + 1)
                if n >= R:
                    dve.wait_ge(silu_made, n - R + 1)
                if m < 0:
                    nc.vector.tensor_copy(g[n % R][:, :], Gp[n % R][:, :]).then_inc(g_cut, 1)
                else:
                    nc.vector.tensor_scalar(g[n % R][:, :], Gp[n % R][:, :], LIMIT, None, op0=ALU.min).then_inc(g_cut, 1)
                dve.wait_ge(u_made, n + 1)
                if n >= R:
                    dve.wait_ge(prod_made, n - R + 1)
                if m < 0:
                    nc.vector.tensor_copy(u[n % R][:, :], Up[n % R][:, :]).then_inc(u_cut, 1)
                else:
                    nc.vector.tensor_scalar(u[n % R][:, :], Up[n % R][:, :], LIMIT, -LIMIT, op0=ALU.min, op1=ALU.max).then_inc(u_cut, 1)
                    dve.wait_ge(u_cut, n + 1)
                    dve.wait_ge(wb_in[m % 2], 32 * (m // 2 + 1))
                    nc.vector.tensor_tensor(u[n % R][:, :], u[n % R][:, :], WB[m % 2][:, j * BANK:(j + 1) * BANK],
                                            op=ALU.mult).then_inc(u_scaled, 1)
                dve.wait_ge(u_cut, n + 1)
                if m >= 0:
                    dve.wait_ge(u_scaled, n + 1 - 2 * NJ)
                dve.wait_ge(silu_made, n + 1)
                if n >= R:
                    dve.wait_ge(down_made, n - R + 1)
                nc.vector.tensor_tensor(h[n % R][:, :], u[n % R][:, :], a[n % R][:, :], op=ALU.mult).then_inc(prod_made, 1)
            dve.wait_ge(down_made, len(units))
            add_transposed(nc, dve, X, Y, yT, Gp + Up, gate_fm, y_out, yT_made, x_done)

        @block.scalar
        def _(act):
            for n in range(len(units)):
                act.wait_ge(g_cut, n + 1)
                if n >= R:
                    act.wait_ge(prod_made, n - R + 1)
                nc.scalar.activation(a[n % R][:, :], g[n % R][:, :], ACT.Silu).then_inc(silu_made, 1)




NG = 16
QA, QQ = 2, 4
ORIGIN = N - P + P // 2 + NG
TABLE = ORIGIN + P
HID = 2 * H
QR = P // NG
ROW = N + P


def kerple_tables(core, kron1, kron2, hid_tab, score_tab):
    nc, ins = core.nc, core.ins
    zeroed, loaded, act_step, dve_step, tab_made, multiplied, done = core.signals(
        "zeroed loaded act_step dve_step tab_made multiplied done")
    core.clear_signals()
    with ExitStack() as c:
        w1k = core.sbuf(c, "w1k", [P, P])
        dist = core.sbuf(c, "dist", [P, TABLE])
        sign = core.sbuf(c, "sign", [P, TABLE])
        lp, la, b2 = (core.sbuf(c, n, [P, 2]) for n in ("lp", "la", "kb2"))
        b1 = core.sbuf(c, "kb1", [P, 1])
        par = core.sbuf(c, "par", [P, 2])
        ab = core.sbuf(c, "ab", [P, 2])
        ex = core.sbuf(c, "ex", [P, 2])
        ps = core.psum(c, "k", 3 * BANK)
        block = c.enter_context(nc.Block())
        zero = [kron1[0], kron1[1], kron2, w1k]

        @block.vector
        def _(dve):
            for t in zero:
                nc.vector.memset(t[:, :], 0.0).then_inc(zeroed, 1)
            dve.wait_ge(loaded, 16 * (5 * QQ + 3 * P // H + 2))
            nc.vector.scalar_tensor_tensor(ab[:, :], par[:, :], -1.0, par[:, :], op0=ALU.mult, op1=ALU.max).then_inc(dve_step, 1)
            dve.wait_ge(act_step, 2)
            nc.vector.scalar_tensor_tensor(par[:, :], par[:, :], 0.0, ex[:, :], op0=ALU.max, op1=ALU.add).then_inc(dve_step, 1)
            dve.wait_ge(dve_step, 2)
            nc.vector.tensor_scalar(par[:, 0:1], par[:, 0:1], -1.0, None, op0=ALU.mult).then_inc(dve_step, 1)
            dve.wait_ge(act_step, 3)
            dve.wait_ge(dve_step, 3)
            nc.vector.tensor_scalar(dist[:, :], dist[:, :], par[:, 0:1], None, op0=ALU.mult).then_inc(tab_made, 1)
            dve.wait_ge(tab_made, 1)
            nc.vector.scalar_tensor_tensor(score_tab[:, :], dist[:, :], b2[:, 0:1], sign[:, :], op0=ALU.add, op1=ALU.add).then_inc(done, 1)
            dve.wait_ge(multiplied, 1)
            nc.vector.tensor_scalar(hid_tab[:, :], ps[:, 0:TABLE], b1[:, 0:1], None, op0=ALU.add).then_inc(done, 1)

        @block.sync
        def _(sp):
            w1, w2 = ins["L1_attn_w1"], ins["L1_attn_w2"]
            sp.wait_ge(zeroed, 4)
            with nc.allow_non_contiguous_dma(reason="a few small weights"):
                for q in range(QQ):
                    cols = slice(HID * q, HID * (q + 1))
                    for a in range(QA):
                        lo = 64 * a + H * q
                        sp.dma_start(kron1[a][lo:lo + H, cols], w1[0:H, :]).then_inc(loaded, 16)
                    sp.dma_start(w1k[H * q:H * (q + 1), cols], w1[H:2 * H, :]).then_inc(loaded, 16)
                    sp.dma_start(kron2[cols, H * q:H * (q + 1)], w2).then_inc(loaded, 16)
                    sp.dma_start(b1[HID * q:HID * (q + 1), :], ins["L1_attn_b1"].rearrange("(m a) -> m a", a=1)).then_inc(loaded, 16)
                for r in range(P // H):
                    rows = slice(H * r, H * (r + 1))
                    sp.dma_start(par[rows, 0:1], ins["L1_attn_log_p"].rearrange("h a c -> h (a c)")).then_inc(loaded, 16)
                    sp.dma_start(par[rows, 1:2], ins["L1_attn_log_a"].rearrange("h a c -> h (a c)")).then_inc(loaded, 16)
                    sp.dma_start(b2[rows, 0:1], ins["L1_attn_b2"].rearrange("(h a) -> h a", a=1)).then_inc(loaded, 16)
            sp.dma_start(dist[:, :], ins["const_dist"]).then_inc(loaded, 16)
            sp.dma_start(sign[:, :], ins["const_mask"]).then_inc(loaded, 16)

        @block.scalar
        def _(act):
            act.wait_ge(dve_step, 1)
            nc.scalar.activation(ex[:, :], ab[:, :], ACT.Exp, scale=-1.0).then_inc(act_step, 1)
            act.wait_ge(act_step, 1)
            nc.scalar.activation(ex[:, :], ex[:, :], ACT.Ln, bias=1.0).then_inc(act_step, 1)
            act.wait_ge(dve_step, 2)
            nc.scalar.activation(dist[:, :], dist[:, :], ACT.Ln, scale=par[:, 1:2], bias=1.0).then_inc(act_step, 1)

        @block.tensor
        def _(pe):
            pe.wait_ge(tab_made, 1)
            for at in range(0, TABLE, BANK):
                w = min(BANK, TABLE - at)
                last = nc.tensor.matmul(ps[:, at:at + w], w1k[0:64, :], dist[0:64, at:at + w], start=True, stop=True)
            last.then_inc(multiplied, 1)



def refined_attention(core, b, X, arena, kT, V, w_out, ident, gate, q_dram, kron1, kron2, hid_tab, score_tab):
    nc = core.nc
    SLOTS = 5
    LAG = 3
    f_in = core.signals("f_in0 f_in1 f_in2 f_in3 f_in4")
    (q_in, s_made, s_out_act, s_out_dve, h_made, hid_made, gelu_made, r_made, kerple_added, f_made, max_step,
     max_made, p_made, inverted, p_normed, z_made, z_out, pv_made, oT_out, y_made, x_step, x_done) = core.signals(
        "q_in s_made s_out_act s_out_dve h_made hid_made gelu_made r_made kerple_added f_made max_step "
        "max_made p_made inverted p_normed z_made z_out pv_made oT_out y_made x_step x_done")
    core.clear_signals()
    tiles = [i for m in range(NT // 2) for i in (NT // 2 - 1 - m, NT // 2 + m)]
    length = [(i + 1) * P for i in tiles]
    base = [0 if k % 2 == 0 else ROW - length[k] for k in range(NT)]
    units = [(k, g, at, min(BANK, length[k] - at)) for k in range(NT) for g in range(NG) for at in range(0, length[k], BANK)]
    first_unit = [next(n for n, u in enumerate(units) if u[0] == k) for k in range(NT)] + [len(units)]
    per_batch = [NG // 4 if length[k] > BANK else NG // 2 if length[k] > BANK // 2 else NG for k in range(NT)]
    batch_units = [per_batch[k] * -(-length[k] // BANK) for k in range(NT)]
    z_lag = [batch_units[k] + LAG + 3 for k in range(NT)]
    last_batch = [first_unit[k + 1] - batch_units[k] for k in range(NT)]
    with ExitStack() as c:
        qs = core.sbuf(c, "qs", [P, NP, P])
        work = core.sbuf(c, "work", [P, SLOTS, N])
        oT = core.sbuf(c, "oT", [P, NP, P])
        mx = core.sbuf(c, "mx", [P, 2, NG])
        nmax = core.sbuf(c, "nmax", [P, NG])
        esum = core.sbuf(c, "esum", [P, NG])
        yg = core.sbuf(c, "yg", [P, D])
        PS = core.psum(c, "ps", 8 * BANK)
        bank = lambda n: PS[:, n * BANK:(n + 1) * BANK]
        block = c.enter_context(nc.Block())
        rows = arena[:, :].rearrange("p (g j) -> p g j", g=NG)

        def F(n):
            k, g, at, w = units[n]
            return rows[:, g, base[k] + at:base[k] + at + w]

        row = lambda k, g: rows[:, g, base[k]:base[k] + length[k]]
        hs = lambda n: work[:, n % SLOTS, :]
        hp = lambda n, a: bank(2 * (n % 2) + a)
        rp = lambda n: bank(4 + n % 2)
        O = lambda half: bank(4 + half)
        zp = lambda n: bank(6 + n % 2)
        y = bank(6)

        def batch_done(k, n):
            m = n - first_unit[k] + 1
            if m <= 0 or m % batch_units[k]:
                return []
            q = m // batch_units[k]
            return list(range((q - 1) * per_batch[k], q * per_batch[k]))

        def rows_wait(eng, n):
            if n >= SLOTS:
                eng.wait_ge(f_in[n % SLOTS], 16 * (n // SLOTS))

        @block.sync
        def _(sp):
            for k in range(NT):
                i = tiles[k]
                if k:
                    sp.wait_ge(s_made, H * k)
                sp.dma_start(qs[:, :, :], q_dram[:, :, i * P:(i + 1) * P]).then_inc(q_in, 16)
                if k >= 2:
                    sp.wait_ge(pv_made, k - 1)
                for h in range(H):
                    n = H * k + h
                    if h % 2 == 0:
                        sp.wait_ge(s_out_act, n // 2 + 1)
                    else:
                        sp.wait_ge(s_out_dve, n // 2 + 1)
                    sp.dma_start(rows[h:h + P - H + 1:H, :, base[k]:base[k] + length[k]],
                                 work[:, n % SLOTS, 0:length[k]]).then_inc(f_in[n % SLOTS], 16)

        @block.tensor
        def _(pe):
            def scores(k):
                pe.wait_ge(q_in, 16 * (k + 1))
                if k:
                    pe.wait_ge(hid_made, 2 * first_unit[k])
                for h in range(H):
                    n = H * k + h
                    if h >= 2:
                        if h % 2 == 0:
                            pe.wait_ge(s_out_act, n // 2)
                        else:
                            pe.wait_ge(s_out_dve, n // 2)
                    r = slice(DH * (h % 2), DH * (h % 2) + DH)
                    for at in range(0, length[k], BANK):
                        w = min(BANK, length[k] - at)
                        last = nc.tensor.matmul(bank(2 * (h % 2) + at // BANK)[:, 0:w], qs[r, h // 2, :],
                                                kT[r, h // 2, at:at + w], start=True, stop=True)
                    last.then_inc(s_made, 1)

            def hidden(n):
                w = units[n][3]
                if n >= 2:
                    pe.wait_ge(hid_made, 2 * (n - 1))
                for a in range(QA):
                    last = nc.tensor.matmul(hp(n, a)[:, 0:w], kron1[a][:, :], F(n), start=True, stop=True)
                last.then_inc(h_made, 1)

            def refine(n):
                w = units[n][3]
                pe.wait_ge(gelu_made, n + 1)
                if n >= 2:
                    pe.wait_ge(f_made, n - 1)
                for a in range(QA):
                    last = nc.tensor.matmul(rp(n)[64 * a:64 * a + 64, 0:w], kron2[:, 0:64], hs(n)[:, a * BANK:a * BANK + w],
                                            start=True, stop=True)
                last.then_inc(r_made, 1)

            def transpose(n):
                k, g, at, w = units[n]
                pe.wait_ge(p_normed, NG * k + g + 1)
                if n >= 2:
                    pe.wait_ge(z_out, n - 1)
                for c in range(0, w, P):
                    last = nc.tensor.transpose(zp(n)[:, c:c + P], F(n)[:, c:c + P], ident[:, :])
                last.then_inc(z_made, 1)

            def values(k):
                pe.wait_ge(z_out, first_unit[k + 1])
                pe.wait_ge(f_made, first_unit[k + 1])
                blocks = length[k] // P
                for jb in range(blocks):
                    at = base[k] + jb * P
                    for h in range(H):
                        j = h // 2
                        last = nc.tensor.matmul(O(j // 4)[DH * (h % 2):DH * (h % 2) + DH, (j % 4) * P:(j % 4 + 1) * P],
                                                V[:, jb, h, :], rows[:, :, at + QR * h:at + QR * (h + 1)],
                                                start=(jb == 0 and j % 4 == 0), stop=(jb == blocks - 1), skip_group_check=True)
                last.then_inc(pv_made, 1)

            def project(k):
                pe.wait_ge(oT_out, 2 * k + 2)
                for j in range(NP):
                    last = nc.tensor.matmul(y[:, 0:D], oT[:, j, :], w_out[:, j, :], start=(j == 0), stop=(j == NP - 1))
                last.then_inc(y_made, 1)

            scores(0)
            for k in range(NT):
                lo, hi = first_unit[k], first_unit[k + 1]
                for s in range(SLOTS):
                    pe.wait_ge(f_in[s], 16 * ((H * (k + 1) - s + SLOTS - 1) // SLOTS))
                for n in range(lo, hi + LAG):
                    if n < hi:
                        hidden(n)
                    if k and n == lo + 1:
                        project(k - 1)
                    if k and n == lo + LAG:
                        pe.wait_ge(oT_out, 2 * k)
                        pe.wait_ge(x_step, k)
                    if n >= lo + LAG:
                        refine(n - LAG)
                    if lo <= n - z_lag[k] < last_batch[k]:
                        transpose(n - z_lag[k])
                for n in range(max(lo, hi + LAG - z_lag[k]), last_batch[k]):
                    transpose(n)
                if k + 1 < NT:
                    scores(k + 1)
                for n in range(last_batch[k], hi):
                    transpose(n)
                values(k)
            project(NT - 1)

        @block.scalar
        def _(act):
            def score_out(n):
                L = length[n // H]
                act.wait_ge(s_made, n + 1)
                if n >= H:
                    act.wait_ge(r_made, first_unit[n // H])
                rows_wait(act, n)
                nc.scalar.activation(work[:, n % SLOTS, 0:L], PS[:, 0:L], ACT.Copy, scale=DH ** -0.5).then_inc(s_out_act, 1)

            def gelu(n):
                w = units[n][3]
                act.wait_ge(hid_made, 2 * n + 2)
                h2 = hs(n).rearrange("p (a w) -> p a w", a=QA)[:, :, 0:w]
                nc.scalar.activation(h2, h2, ACT.Gelu).then_inc(gelu_made, 1)

            def exponentials(k, groups):
                for g in groups:
                    act.wait_ge(max_made, NG * k + g + 1)
                    nc.scalar.activation(row(k, g), row(k, g), ACT.Exp, bias=nmax[:, g:g + 1],
                                         accum_out=esum[:, g:g + 1]).then_inc(p_made, 1)

            def transposed_out(n):
                w = units[n][3]
                act.wait_ge(z_made, n + 1)
                nc.scalar.activation(F(n).rearrange("p (c h r) -> p c h r", h=H, r=QR),
                                     zp(n)[:, 0:w].rearrange("p (c r h) -> p c h r", h=H, r=QR), ACT.Copy).then_inc(z_out, 1)

            for h in range(0, H, 2):
                score_out(h)
            for k in range(NT):
                lo, hi = first_unit[k], first_unit[k + 1]
                for n in range(lo, hi + LAG):
                    if n < hi:
                        gelu(n)
                        exponentials(k, batch_done(k, n - LAG))
                    if lo <= n - z_lag[k] < last_batch[k]:
                        transposed_out(n - z_lag[k])
                for n in range(max(lo, hi + LAG - z_lag[k]), last_batch[k]):
                    transposed_out(n)
                groups = batch_done(k, hi - 1)
                each = -(-len(groups) // NP)
                for j in range(NP):
                    exponentials(k, groups[j * each:(j + 1) * each])
                    if k + 1 < NT:
                        score_out(H * (k + 1) + 2 * j)
                for n in range(last_batch[k], hi):
                    transposed_out(n)
                act.wait_ge(pv_made, k + 1)
                if k:
                    act.wait_ge(y_made, k)
                nc.scalar.activation(oT[:, 0:4, :].rearrange("p j (r g) -> p j r g", g=NG),
                                     O(0).rearrange("p (j g r) -> p j r g", g=NG, r=QR), ACT.Copy).then_inc(oT_out, 1)

        @block.gpsimd
        def _(pool):
            for n, (k, g, at, w) in enumerate(units):
                pool.wait_ge(h_made, n + 1)
                start = ORIGIN - (tiles[k] * P + g) + at
                nc.gpsimd.tensor_tensor(F(n), F(n), score_tab[:, start:start + w], op=ALU.add).then_inc(kerple_added, 1)

        @block.vector
        def _(dve):
            max_steps = 0

            def score_out(n):
                L = length[n // H]
                dve.wait_ge(s_made, n + 1)
                if n >= H:
                    dve.wait_ge(r_made, first_unit[n // H])
                rows_wait(dve, n)
                nc.vector.tensor_scalar(work[:, n % SLOTS, 0:L], PS[:, 2 * BANK:2 * BANK + L], DH ** -0.5, None,
                                        op0=ALU.mult).then_inc(s_out_dve, 1)

            def hidden(n):
                k, g, at, w = units[n]
                dve.wait_ge(h_made, n + 1)
                if n >= SLOTS:
                    dve.wait_ge(r_made, n - SLOTS + 1)
                for a in range(QA):
                    start = ORIGIN - (tiles[k] * P + g + 64 * a) + at
                    nc.vector.tensor_tensor(hs(n)[:, a * BANK:a * BANK + w], hp(n, a)[:, 0:w], hid_tab[:, start:start + w],
                                            op=ALU.add).then_inc(hid_made, 1)

            def refined(n):
                k, g, at, w = units[n]
                dve.wait_ge(r_made, n + 1)
                dve.wait_ge(kerple_added, n + 1)
                nc.vector.tensor_tensor_reduce(out=F(n), in0=rp(n)[:, 0:w], in1=F(n), scale=1.0, scalar=2 * NEG,
                                               op0=ALU.add, op1=ALU.max,
                                               accum_out=mx[:, at // BANK, g:g + 1]).then_inc(f_made, 1)

            def maxima(k, n):
                nonlocal max_steps
                groups = batch_done(k, n)
                if not groups:
                    return
                gs = slice(groups[0], groups[-1] + 1)
                dve.wait_ge(f_made, n + 1)
                if length[k] > BANK:
                    nc.vector.tensor_tensor(mx[:, 0, gs], mx[:, 0, gs], mx[:, 1, gs], op=ALU.max).then_inc(max_step, 1)
                    max_steps += 1
                    dve.wait_ge(max_step, max_steps)
                nc.vector.tensor_scalar(nmax[:, gs], mx[:, 0, gs], -1.0, None, op0=ALU.mult).then_inc(max_made, len(groups))

            def normalize(k, groups):
                for g in groups:
                    n = NG * k + g
                    dve.wait_ge(p_made, n + 1)
                    nc.vector.reciprocal(esum[:, g:g + 1], esum[:, g:g + 1]).then_inc(inverted, 1)
                    dve.wait_ge(inverted, n + 1)
                    nc.vector.tensor_scalar(row(k, g), row(k, g), esum[:, g:g + 1], None, op0=ALU.mult).then_inc(p_normed, 1)

            def residual(k):
                dve.wait_ge(y_made, k + 1)
                if k:
                    dve.wait_ge(x_done, k)
                nc.vector.tensor_tensor(yg[:, :], y[:, 0:D], gate[:, b, :], op=ALU.mult).then_inc(x_step, 1)
                dve.wait_ge(x_step, k + 1)
                x = X[:, tiles[k] + b * NT, :]
                nc.vector.tensor_tensor(x, x, yg[:, :], op=ALU.add).then_inc(x_done, 1)

            for h in range(1, H, 2):
                score_out(h)
            for k in range(NT):
                lo, hi = first_unit[k], first_unit[k + 1]
                for n in range(lo, hi + LAG):
                    if n < hi:
                        hidden(n)
                    if k and n == lo + 2:
                        residual(k - 1)
                    if n >= lo + LAG:
                        refined(n - LAG)
                        maxima(k, n - LAG)
                    done = batch_done(k, n - LAG - 2)
                    normalize(k, done[:len(done) // 2])
                    done = batch_done(k, n - LAG - 3)
                    normalize(k, done[len(done) // 2:])
                groups = batch_done(k, hi - 1)
                each = -(-len(groups) // NP)
                for j in range(NP):
                    if k + 1 < NT:
                        score_out(H * (k + 1) + 2 * j + 1)
                    normalize(k, groups[j * each:(j + 1) * each])
                dve.wait_ge(pv_made, k + 1)
                if k:
                    dve.wait_ge(y_made, k)
                nc.vector.tensor_copy(oT[:, 4:8, :].rearrange("p j (r g) -> p j r g", g=NG),
                                      O(1).rearrange("p (j g r) -> p j r g", g=NG, r=QR)).then_inc(oT_out, 1)
            residual(NT - 1)



def host_constants():
    reset = np.ones((1, E1 * TT), np.float32)
    reset[:, ::TT] = 0.0
    reset_e = np.ones((1, E1 * TT), np.float32)
    reset_e[:, ::E1] = 0.0
    behind = (np.arange(P) // H * NG).reshape(P, 1) + ORIGIN - np.arange(TABLE)[None]
    freq = (np.float32(1.0) / np.float32(10000.0) ** (np.arange(0, DH, 2, dtype=np.float32) / np.float32(DH))).astype(np.float32)
    angle = np.outer(np.arange(N, dtype=np.float32), freq).astype(np.float32)
    tiles = lambda t: np.ascontiguousarray(t.reshape(NT, P, DH // 2).transpose(1, 0, 2).astype(np.float32))
    return {
        "const_dist": np.abs(behind).astype(np.float32),
        "const_mask": np.where(behind < 0, NEG, 0.0).astype(np.float32),
        "const_cos": tiles(np.cos(angle)),
        "const_sin": tiles(np.sin(angle)),
        "const_reset_e": reset_e,
        "const_ident": np.eye(P, dtype=np.float32),
        "const_tri": np.triu(np.ones((P, P), np.float32)),
        "const_reset": reset,
        "const_rev": np.arange(E0, 0, -1, dtype=np.float32)[None],
    }


def program(nc, ins, out, stages="01234"):
    with ExitStack() as ctx:
        core = Core(nc, ctx, ins)
        sb = lambda n, s: core.sbuf(ctx, n, s)
        X = sb("X", [P, TT, D])
        xT = sb("xT", [P, T])
        ident = sb("ident", [P, P])
        expo = sb("expo", [P, 1])
        mod = sb("mod", [P, 6, B])
        gate_a = sb("gate_a", [P, B, D])
        gate_b = sb("gate_b", [P, B, D])
        rows = sb("rows", [P, B, D])
        tri, ones = sb("tri", [P, P]), sb("ones", [P, P])
        q_dram = nc.dram_tensor("queries", (P, NP, N), F32, kind="Internal").ap()
        wts_dram = nc.dram_tensor("expert_weights", (E1, T), F32, kind="Internal").ap()
        loaded, const_made = core.signals("loaded const_made")
        core.clear_signals()
        with nc.Block() as block:
            @block.sync
            def _(sp):
                sp.dma_start(X[:, :, :], ins["L0_attn_x"].rearrange("b (t p) d -> p (b t) d", p=P)).then_inc(loaded, 16)
                sp.dma_start(ident[:, :], ins["const_ident"]).then_inc(loaded, 16)
                sp.dma_start(tri[:, :], ins["const_tri"]).then_inc(loaded, 16)
                sp.wait_ge(loaded, 48)

            @block.vector
            def _(dve):
                nc.vector.memset(ones[:, :], 1.0).then_inc(const_made, 1)
                nc.vector.memset(expo[:, :], -0.5).then_inc(const_made, 1)
                dve.wait_ge(const_made, 2)

        if "0" in stages:
            modulation(core, "L0", ident, mod, gate_a, gate_b, None)
            bias, staged = core.signals("bias staged")
            core.clear_signals()
            with nc.Block() as block:
                @block.sync
                def _(sp):
                    sp.dma_start(rows[:, 0, :], ins["L0_attn_b_out"].rearrange("(a d) -> a d", a=1).to_broadcast([P, D])).then_inc(bias, 16)
                    sp.wait_ge(bias, 16)

                @block.vector
                def _(dve):
                    dve.wait_ge(bias, 16)
                    nc.vector.tensor_tensor(rows[:, 1, :], rows[:, 0, :], gate_a[:, 1, :], op=ALU.mult).then_inc(staged, 1)
                    dve.wait_ge(staged, 1)
                    nc.vector.tensor_tensor(rows[:, 0, :], rows[:, 0, :], gate_a[:, 0, :], op=ALU.mult).then_inc(staged, 1)
            layer_norm(core, X, xT, ident, expo, mod[:, 0, :], mod[:, 1, :], rows)
            with ExitStack() as c:
                sc = lambda n, s: core.sbuf(c, n, s)
                w_qkv = sc("w_qkv", [P, 3 * INNER])
                w_out = sc("w_out", [P, NP, D])
                hscale = sc("hscale", [P, H])
                qT, kT = (core.sbuf(c, n, [P, H, N], F16) for n in ("qT", "kT"))
                V = sc("V", [P, NT, H, DH])
                ident16 = core.sbuf(c, "ident16", [P, P], F16)
                scaled, copied = core.signals("scaled copied")
                core.clear_signals()
                with nc.Block() as block:
                    @block.sync
                    def _(sp):
                        sp.dma_start(w_qkv[:, :], ins["L0_attn_w_qkv"]).then_inc(loaded, 16)
                        sp.dma_start(w_out[:, :, :], ins["L0_attn_w_out"].rearrange("(j p) d -> p j d", p=P)).then_inc(loaded, 16)
                        sp.dma_start(hscale[:, :], ins["L0_attn_logit_scale"].rearrange("h a c -> (a c) h").to_broadcast([P, H])).then_inc(loaded, 16)
                        sp.wait_ge(loaded, 48)

                    @block.vector
                    def _(dve):
                        dve.wait_ge(loaded, 48)
                        nc.vector.tensor_copy(ident16[:, :], ident[:, :]).then_inc(copied, 1)
                        nc.vector.tensor_scalar(hscale[:, :], hscale[:, :], float(np.float32(np.log(1.0 / 0.01))), None, op0=ALU.min).then_inc(scaled, 1)

                    @block.scalar
                    def _(act):
                        act.wait_ge(scaled, 1)
                        nc.scalar.activation(hscale[:, :], hscale[:, :], ACT.Exp, scale=2.0).then_inc(scaled, 1)
                for b in range(B):
                    project_qkv(core, 0, b, xT, w_qkv, qT, kT, V, ident, hscale, ident16=ident16)
                    cosine_attention(core, b, X, qT, kT, V, w_out, ident, gate_a)

        if "1" in stages:
            if "0" not in stages:
                modulation(core, "L0", ident, mod, gate_a, gate_b, None)
            layer_norm(core, X, xT, ident, expo, mod[:, 3, :], mod[:, 4, :], None)
            route_first(core, xT, wts_dram, ident, tri, ones)
            experts_first(core, X, xT, wts_dram, ident, mod[:, 5, :])

        if "2" in stages:
            modulation(core, "L1", ident, mod, gate_a, gate_b, None)
            layer_norm(core, X, xT, ident, expo, mod[:, 0, :], mod[:, 1, :], None)
            with ExitStack() as c:
                arena = core.sbuf(c, "arena", [P, NG * ROW])
                kT = core.sbuf(c, "kT", [P, NP, N])
                V = core.sbuf(c, "V", [P, NT, H, DH])
                w_out = core.sbuf(c, "w_out", [P, NP, D])
                kron1 = [core.sbuf(c, "kron1", [P, P]) for _ in range(QA)]
                kron2 = core.sbuf(c, "kron2", [P, 64])
                hid_tab = core.sbuf(c, "hid_tab", [P, TABLE])
                score_tab = core.sbuf(c, "score_tab", [P, TABLE])
                qT = arena[:, 0:NP * N].rearrange("p (a n) -> p a n", a=NP)
                w_qkv = arena[:, NP * N:NP * N + 3 * INNER]
                kerple_tables(core, kron1, kron2, hid_tab, score_tab)
                for b in range(B):
                    with ExitStack() as c2:
                        cos = core.sbuf(c2, "cos", [P, NT, DH // 2])
                        sin = core.sbuf(c2, "sin", [P, NT, DH // 2])
                        core.clear_signals()
                        with nc.Block() as block:
                            @block.sync
                            def _(sp):
                                sp.dma_start(w_qkv[:, :], ins["L1_attn_w_qkv"]).then_inc(loaded, 16)
                                sp.dma_start(cos[:, :, :], ins["const_cos"]).then_inc(loaded, 16)
                                sp.dma_start(sin[:, :, :], ins["const_sin"]).then_inc(loaded, 16)
                                sp.dma_start(w_out[:, :, :], ins["L1_attn_w_o"].rearrange("(j p) d -> p j d", p=P)).then_inc(loaded, 16)
                                sp.wait_ge(loaded, 64)
                        project_qkv(core, 1, b, xT, w_qkv, qT, kT, V, ident, (cos, sin), q_dram)
                    refined_attention(core, b, X, arena, kT, V, w_out, ident, gate_a, q_dram, kron1, kron2, hid_tab, score_tab)

        if "3" in stages:
            if "2" not in stages:
                modulation(core, "L1", ident, mod, gate_a, gate_b, None)
            layer_norm(core, X, xT, ident, expo, mod[:, 3, :], mod[:, 4, :], None)
            with ExitStack() as c:
                guT = core.sbuf(c, "guT", [P, E1 // 2, 2, 2, I1])
                dnT = core.sbuf(c, "dnT", [P, E1 // 2, D])
                rwT = core.sbuf(c, "rwT", [P, E1])
                sgT, suT = core.sbuf(c, "sgT", [P, SI]), core.sbuf(c, "suT", [P, SI])
                sdT = core.sbuf(c, "sdT", [P, 2, D])
                prepare_second(core, ident, guT, dnT, rwT, sgT, suT, sdT)
                route_second(core, xT, wts_dram, ident, tri, ones, rwT)
                experts_second(core, X, xT, wts_dram, ident, mod[:, 5, :], guT, dnT, sgT, suT, sdT)

        stored, = core.signals("stored")
        core.clear_signals()
        with nc.Block() as block:
            @block.sync
            def _(sp):
                sp.dma_start(out.rearrange("b (t p) d -> p (b t) d", p=P), X[:, :, :]).then_inc(stored, 16)
                sp.wait_ge(stored, 16)


def kernel(**inputs):
    import concourse.bacc as bacc
    from concourse.bass_utils import run_bass_kernel_spmd

    nc = bacc.Bacc("TRN2", target_bir_lowering=False, num_devices=1)
    arrays = {name: np.ascontiguousarray(a) for name, a in {**inputs, **host_constants()}.items()}
    ins = {name: nc.dram_tensor(name, a.shape, mybir.dt.from_np(a.dtype), kind="ExternalInput").ap()
           for name, a in arrays.items()}
    out = nc.dram_tensor("out", (B, N, D), F32, kind="ExternalOutput").ap()
    program(nc, ins, out)
    return run_bass_kernel_spmd(nc, [arrays], core_ids=[0]).results[0]["out"]
```

```python
from contextlib import ExitStack

import concourse.bass as bass
import numpy as np
from concourse import mybir

F32 = mybir.dt.float32
F16 = mybir.dt.float16
ALU = mybir.AluOpType
ACT = mybir.ActivationFunctionType
AX = mybir.AxisListType

P = 128
B = 2
N = 1024
D = 128
H = 16
DH = 64
NT = N // P
TT = B * NT
T = B * N
NP = H // 2
INNER = H * DH
BANK = 512
Q_UP, K_UP = 2.0 ** 5, 2.0 ** 8
NEG = -1.0e30

E0, F0, CAP0 = 8, 512, int(T * 1.25 / 8)
E1, I1, SI, CAP1, TOP1 = 32, 64, 256, 256, 8


class Core:

    def __init__(self, nc, ctx, ins):
        self.nc, self.ctx, self.ins, self.named, self.count = nc, ctx, ins, {}, 0

    def sbuf(self, c, name, shape, dtype=F32):
        self.count += 1
        return c.enter_context(self.nc.sbuf_tensor(f"{name}_{self.count}", shape, dtype))

    def psum(self, c, name, width, dtype=F32):
        self.count += 1
        return c.enter_context(self.nc.psum_tensor(f"{name}_{self.count}", [P, width], dtype))

    def signals(self, names):
        out = []
        for n in names.split():
            if n not in self.named:
                self.named[n] = self.ctx.enter_context(self.nc.semaphore(n))
            out.append(self.named[n])
        return out

    def clear_signals(self):
        nums = sorted(s.num for s in self.named.values())
        if not nums:
            return
        with self.nc.Block() as block:
            @block.sync
            def _(sp):
                sp.sem_clear(range(nums[0], nums[-1] + 1))



def modulation(core, X, ident, tri, ones, expo, mod, gate, rows):
    nc, ins = core.nc, core.ins
    cond_in, rest_in, ones_made, condT_ready, modulated, act_step, dve_step = core.signals(
        "cond_in rest_in ones_made condT_ready modulated act_step dve_step")
    core.clear_signals()
    LB = 2 * B
    with ExitStack() as c:
        sb = lambda n, s: core.sbuf(c, n, s)
        W = sb("mod_w", [P, 2, 6 * D])
        cT = sb("mod_cT", [P, LB])
        e = sb("mod_e", [P, LB])
        cb = sb("mod_cb", [P, LB, P])
        t2 = sb("mod_t2", [P, LB * D])
        t3 = sb("mod_t3", [P, LB * D])
        ps_m = core.psum(c, "mod_pm", 12 * B)
        ps_g = core.psum(c, "mod_pg", LB * D)
        block = c.enter_context(nc.Block())

        @block.sync
        def _(sp):
            with nc.allow_non_contiguous_dma(reason="512 values"):
                for l, name in enumerate(("L0", "L1")):
                    sp.dma_start(cT[:, l * B:(l + 1) * B], ins[name + "_c"].rearrange("b d -> d b")).then_inc(cond_in, 16)
            for l, name in enumerate(("L0", "L1")):
                sp.dma_start(W[:, l, :], ins[name + "_wmod"]).then_inc(cond_in, 16)
            sp.dma_start(rows[:, 0, :], ins["L0_attn_b_out"].rearrange("(a d) -> a d", a=1).to_broadcast([P, D])).then_inc(rest_in, 16)
            sp.dma_start(X[:, :, :], ins["L0_attn_x"].rearrange("b (t p) d -> p (b t) d", p=P)).then_inc(rest_in, 16)
            sp.dma_start(ident[:, :], ins["const_ident"]).then_inc(rest_in, 16)
            sp.dma_start(tri[:, :], ins["const_tri"]).then_inc(rest_in, 16)
            sp.wait_ge(rest_in, 64)

        @block.gpsimd
        def _(pool):
            nc.gpsimd.memset(ones[:, :], 1.0).then_inc(ones_made, 1)
            nc.gpsimd.memset(expo[:, :], -0.5).then_inc(ones_made, 1)
            pool.wait_ge(ones_made, 2)

        @block.scalar
        def _(act):
            act.wait_ge(cond_in, 64)
            nc.scalar.activation(e[:, :], cT[:, :], ACT.Exp, scale=-1.0).then_inc(act_step, 1)

        @block.vector
        def _(dve):
            count = 0

            def then(ins_):
                nonlocal count
                ins_.then_inc(dve_step, 1)
                count += 1
                dve.wait_ge(dve_step, count)

            dve.wait_ge(act_step, 1)
            then(nc.vector.tensor_scalar(e[:, :], e[:, :], 1.0, None, op0=ALU.add))
            then(nc.vector.reciprocal(e[:, :], e[:, :]))
            then(nc.vector.tensor_tensor(cT[:, :], cT[:, :], e[:, :], op=ALU.mult))
            nc.vector.tensor_copy(cb[:, :, :], cT[:, :].unsqueeze(2).to_broadcast([P, LB, P])).then_inc(condT_ready, 1)

            def push(x, g, a, size):
                nc.vector.tensor_scalar(a, x, 0.0, 2.0, op0=ALU.is_ge, op1=ALU.mult).then_inc(dve_step, 1)
                then(nc.vector.scalar_tensor_tensor(size, x, -1.0, g, op0=ALU.mult, op1=ALU.max))
                then(nc.vector.tensor_scalar(size, size, 0.25, None, op0=ALU.max))
                then(nc.vector.scalar_tensor_tensor(g, a, -1.0, size, op0=ALU.add, op1=ALU.mult))

            dve.wait_ge(modulated, 1)
            nc.vector.tensor_copy(mod[:, :, :, :], ps_m[:, :].rearrange("p (l k b) -> p l k b", l=2, b=B)).then_inc(dve_step, 1)
            count += 1
            flat = gate[:, :, :, :].rearrange("p l b d -> p (l b d)")
            then(nc.vector.tensor_copy(flat, ps_g[:, :]))
            for k in (1, 4):
                nc.vector.tensor_scalar(mod[:, :, k, :], mod[:, :, k, :], 1.0, None, op0=ALU.add).then_inc(dve_step, 1)
            count += 2
            for k in (2, 5):
                x = mod[:, :, k, :]
                count += 1
                push(x, x, t2[:, 0:LB].rearrange("p (l b) -> p l b", b=B), t3[:, 0:LB].rearrange("p (l b) -> p l b", b=B))
            count += 1
            push(flat, flat, t2[:, :], t3[:, :])
            dve.wait_ge(rest_in, 64)
            then(nc.vector.tensor_tensor(rows[:, 1, :], rows[:, 0, :], gate[:, 0, 1, :], op=ALU.mult))
            then(nc.vector.tensor_tensor(rows[:, 0, :], rows[:, 0, :], gate[:, 0, 0, :], op=ALU.mult))

        @block.tensor
        def _(pe):
            pe.wait_ge(condT_ready, 1)
            for l in range(2):
                for k in range(6):
                    at = (6 * l + k) * B
                    nc.tensor.matmul(ps_m[:, at:at + B], W[:, l, D * k:D * k + D], cT[:, l * B:(l + 1) * B],
                                     start=(l + k == 0), stop=True, skip_group_check=True)
            for n in range(LB):
                last = nc.tensor.matmul(ps_g[:, n * D:(n + 1) * D], cb[:, n, :], W[:, n // B, 2 * D:3 * D],
                                        start=(n == 0), stop=True, skip_group_check=True)
            last.then_inc(modulated, 1)



def layer_norm(core, X, xT, ident, expo, shift, scale, bias_row=None, loads=None):
    nc = core.nc
    summed, averaged, centered, squared, sq_summed, powered, normed, biased, xhatT, evac = core.signals(
        "summed averaged centered squared sq_summed powered normed biased xhatT evac")
    core.clear_signals()
    with ExitStack() as c:
        xc = core.sbuf(c, "ln_xc", [P, TT, D])
        sq = core.sbuf(c, "ln_sq", [P, TT, D])
        m = core.sbuf(c, "ln_m", [P, TT])
        v = core.sbuf(c, "ln_v", [P, TT])
        ps = [core.psum(c, f"ln_ps{i}", BANK) for i in range(TT // 4)]
        block = c.enter_context(nc.Block())
        of = lambda b: slice(b * NT, (b + 1) * NT)

        if loads is not None:
            @block.sync
            def _(sp):
                loads(sp)

        @block.vector
        def _(dve):
            wide = lambda t, b: t[:, of(b)].unsqueeze(2).to_broadcast([P, NT, D])
            for b in range(B):
                nc.vector.tensor_reduce(m[:, of(b)], X[:, of(b), :], axis=AX.X, op=ALU.add).then_inc(summed, 1)
            for b in range(B):
                dve.wait_ge(summed, b + 1)
                nc.vector.tensor_scalar(m[:, of(b)], m[:, of(b)], 1.0 / D, None, op0=ALU.mult).then_inc(averaged, 1)
                dve.wait_ge(averaged, b + 1)
                nc.vector.tensor_tensor(xc[:, of(b), :], X[:, of(b), :], wide(m, b), op=ALU.subtract).then_inc(centered, 1)
            for b in range(B):
                dve.wait_ge(squared, b + 1)
                nc.vector.tensor_reduce(v[:, of(b)], sq[:, of(b), :], axis=AX.X, op=ALU.add).then_inc(sq_summed, 1)
                dve.wait_ge(sq_summed, 2 * b + 1)
                nc.vector.tensor_scalar(v[:, of(b)], v[:, of(b)], 1.0 / D, 1e-5, op0=ALU.mult, op1=ALU.add).then_inc(sq_summed, 1)
            for b in range(B):
                dve.wait_ge(powered, b + 1)
                nc.vector.tensor_tensor(xc[:, of(b), :], xc[:, of(b), :], wide(v, b), op=ALU.mult).then_inc(normed, 1)
            dve.wait_ge(xhatT, 3)
            nc.vector.tensor_scalar(xT[:, 2 * BANK:3 * BANK], ps[2][:, :], scale[:, 1:2], shift[:, 1:2],
                                    op0=ALU.mult, op1=ALU.add).then_inc(evac, 1)
            if bias_row is not None:
                for b in range(B):
                    nc.vector.tensor_tensor(X[:, of(b), :], X[:, of(b), :], bias_row[:, b, :].unsqueeze(1).to_broadcast([P, NT, D]),
                                            op=ALU.add).then_inc(biased, 1)

        @block.gpsimd
        def _(pool):
            for b in range(B):
                pool.wait_ge(sq_summed, 2 * b + 2)
                nc.gpsimd.tensor_tensor(v[:, of(b)], v[:, of(b)], expo[:, 0:1].to_broadcast([P, NT]), op=ALU.pow).then_inc(powered, 1)

        @block.tensor
        def _(pe):
            for i in range(TT // 4):
                pe.wait_ge(normed, 4 * i // NT + 1)
                for j in range(4):
                    last = nc.tensor.transpose(ps[i][:, j * P:(j + 1) * P], xc[:, 4 * i + j, :], ident[:, :])
                last.then_inc(xhatT, 1)

        @block.scalar
        def _(act):
            for b in range(B):
                act.wait_ge(centered, b + 1)
                nc.scalar.activation(sq[:, of(b), :], xc[:, of(b), :], ACT.Square).then_inc(squared, 1)
            for i in (0, 1, 3):
                act.wait_ge(xhatT, i + 1)
                b = i * 4 // NT
                nc.scalar.activation(xT[:, i * BANK:(i + 1) * BANK], ps[i][:, :], ACT.Identity,
                                     scale=scale[:, b:b + 1], bias=shift[:, b:b + 1]).then_inc(evac, 1)



def project_qkv(core, layer, b, xT, w_qkv, qT, kT, V, ident, extra, q_dram=None, ident16=None,
                load=None, weights=None, q_stored=None, qs=None):
    nc = core.nc
    (x_copied, q_made, k_made, v_made, v_out, squared_q, squared_k, dve_step, inverted, rooted, product,
     q_ready, k_ready, q_high, k_high, q_split, k_split, qT_made, kT_made, qT_out, kT_out, q_copied) = core.signals(
        "x_copied q_made k_made v_made v_out squared_q squared_k dve_step inverted rooted product "
        "q_ready k_ready q_high k_high q_split k_split qT_made kT_made qT_out kT_out q_copied")
    core.clear_signals()
    with ExitStack() as c:
        sb = lambda n, s: core.sbuf(c, n, s)
        xs = sb("qkv_x", [P, P])
        sq = [sb("qkv_sq", [P, INNER]) for _ in range(2)]
        qk = [sb("qkv_qk", [P, INNER]) for _ in range(2)]
        rn = [sb("qkv_rn", [P, H]) for _ in range(2)]
        U = [core.psum(c, "qkv_u", INNER) for _ in range(2)]
        Vp = core.psum(c, "qkv_v", INNER)
        parts = [core.sbuf(c, "qkv_parts", [P, H, 2, DH], F16) for _ in range(2 - 2 * layer)]
        Z = core.psum(c, "qkv_z", 2 * INNER, F16) if layer == 0 else core.psum(c, "qkv_z", INNER)
        made, squared, ready = (q_made, k_made), (squared_q, squared_k), (q_ready, k_ready)
        T_made, T_out, dst = (qT_made, kT_made), (qT_out, kT_out), (qT, kT)
        block = c.enter_context(nc.Block())
        heads = lambda t: t[:, :].rearrange("p (h d) -> p h d", d=DH)
        halves = lambda t: t[:, :].rearrange("p (h s d) -> p h s d", s=2, d=DH // 2)

        if layer == 1:
            @block.sync
            def _(sp):
                if load is not None:
                    load(sp)
                for t in range(NT):
                    sp.wait_ge(qT_out, 2 * t + 2)
                    sp.dma_start(q_dram[:, :, t * P:(t + 1) * P], qT[:, :, t * P:(t + 1) * P]).then_inc(q_stored, 16)

        high, split = (q_high, k_high), (q_split, k_split)

        @block.gpsimd
        def _(pool):
            def low_parts(t, j, first):
                pool.wait_ge(high[j], t + 1)
                if not first:
                    pool.wait_ge(T_made[j], t)
                nc.gpsimd.tensor_tensor(parts[j][:, :, 1, :], heads(qk[j]), parts[j][:, :, 0, :],
                                        op=ALU.subtract).then_inc(split[j], 1)

            if layer == 1:
                pool.sem_inc(q_ready, 1)
                pool.sem_inc(k_ready, 1)
                with pool.Fori(0, NT) as t:
                    for j in range(2):
                        pool.wait_ge(product, 6 * t + 3 * j + 3)
                        nc.gpsimd.tensor_tensor(qk[j][:, :], qk[j][:, :], sq[j][:, :], op=ALU.add).then_inc(ready[j], 1)
            else:
                low_parts(0, 0, True)
                low_parts(0, 1, True)
                with pool.Fori(1, NT) as t:
                    low_parts(t, 0, False)
                    low_parts(t, 1, False)

        @block.tensor
        def _(pe):
            def project(t, j):
                pe.wait_ge(ready[j], t + 1)
                for h in range(2):
                    at = j * INNER + h * BANK
                    last = nc.tensor.matmul(U[j][:, h * BANK:(h + 1) * BANK], xs[:, :], w_qkv[:, at:at + BANK],
                                            start=True, stop=True)
                last.then_inc(made[j], 1)

            def project_v(t):
                pe.wait_ge(v_out, 2 * t + 2)
                for h in range(2):
                    at = 2 * INNER + h * BANK
                    last = nc.tensor.matmul(Vp[:, h * BANK:(h + 1) * BANK], xs[:, :], w_qkv[:, at:at + BANK],
                                            start=True, stop=True)
                last.then_inc(v_made, 1)

            def transpose(t, j):
                if j == 0:
                    pe.wait_ge(kT_out, 2 * t + 2)
                else:
                    pe.wait_ge(qT_out, 2 * t + 2)
                if layer == 0:
                    pe.wait_ge(split[j], t + 1)
                    for h in range(H):
                        last = nc.tensor.transpose(Z[:, h * P:(h + 1) * P], parts[j][:, h, :, :].rearrange("p s d -> p (s d)"),
                                                   ident16[:, :])
                else:
                    pe.wait_ge(ready[j], t + 2)
                    for a in range(NP):
                        last = nc.tensor.transpose(Z[:, a * P:(a + 1) * P], qk[j][:, a * P:(a + 1) * P], ident[:, :])
                last.then_inc(T_made[j], 1)

            if layer == 1:
                pe.wait_ge(*weights)
            pe.wait_ge(x_copied, 1)
            project(0, 0)
            project_v(0)
            project(0, 1)
            with pe.Fori(1, NT) as t:
                pe.wait_ge(x_copied, t + 1)
                project(t, 0)
                transpose(t - 1, 0)
                project_v(t)
                project(t, 1)
                transpose(t - 1, 1)
            transpose(NT - 1, 0)
            transpose(NT - 1, 1)

        @block.scalar
        def _(act):
            def square(t, j):
                act.wait_ge(made[j], t + 1)
                act.wait_ge(ready[j], t + 1)
                nc.scalar.activation(sq[j][:, :], U[j][:, :], ACT.Square).then_inc(squared[j], 1)

            def root(t, j):
                act.wait_ge(inverted, 2 * t + j + 1)
                nc.scalar.activation(rn[j][:, :], rn[j][:, :], ACT.Sqrt).then_inc(rooted, 1)

            def move_v(t):
                act.wait_ge(v_made, t + 1)
                for j in range(2):
                    nc.scalar.activation(V[:, bass.ds(t, 1), j * (H // 2):(j + 1) * (H // 2), :],
                                         Vp[:, j * BANK:(j + 1) * BANK].rearrange("p (a h d) -> p a h d", a=1, d=DH),
                                         ACT.Copy).then_inc(v_out, 1)

            def move_T(t, j):
                act.wait_ge(T_made[j], t + 1)
                z = Z[:, :].rearrange("p (a q) -> p a q", q=P)
                half = z.shape[1] // 2
                for s in range(2):
                    nc.scalar.activation(dst[j][:, half * s:half * s + half, bass.ts(t, P)], z[:, half * s:half * s + half, :],
                                         ACT.Copy).then_inc(T_out[j], 1)

            def high_parts(t, j, follows):
                act.wait_ge(ready[j], t + 2)
                if follows:
                    act.wait_ge(T_made[j], t)
                nc.scalar.activation(parts[j][:, :, 0, :], heads(qk[j]), ACT.Copy).then_inc(high[j], 1)

            def tile(t, follows):
                if layer == 0:
                    square(t, 0)
                if follows:
                    move_T(t - 1, 0)
                if layer == 0:
                    root(t, 0)
                move_v(t)
                if layer == 0:
                    square(t, 1)
                    high_parts(t, 0, follows)
                if follows:
                    move_T(t - 1, 1)
                if layer == 0:
                    root(t, 1)
                    high_parts(t, 1, follows)

            act.sem_inc(v_out, 2)
            act.sem_inc(kT_out, 2)
            tile(0, False)
            with act.Fori(1, NT) as t:
                tile(t, True)
            move_T(NT - 1, 0)
            move_T(NT - 1, 1)

        @block.vector
        def _(dve):
            def normalize(t, j, first):
                n = 2 * t + j
                dve.wait_ge(squared[j], t + 1)
                nc.vector.tensor_reduce(rn[j][:, :], heads(sq[j]), axis=AX.X, op=ALU.add).then_inc(dve_step, 1)
                dve.wait_ge(dve_step, 5 * t + 3 * j + 1)
                nc.vector.tensor_scalar(rn[j][:, :], rn[j][:, :], 1e-24, (Q_UP, K_UP)[j] ** -2.0, op0=ALU.max,
                                        op1=ALU.mult).then_inc(dve_step, 1)
                dve.wait_ge(dve_step, 5 * t + 3 * j + 2)
                if j == 0:
                    nc.vector.reciprocal(rn[j][:, :], rn[j][:, :]).then_inc(dve_step, 1)
                    dve.wait_ge(dve_step, 5 * t + 3)
                    nc.vector.tensor_tensor(rn[j][:, :], rn[j][:, :], extra[:, :], op=ALU.mult).then_inc(inverted, 1)
                else:
                    nc.vector.reciprocal(rn[j][:, :], rn[j][:, :]).then_inc(inverted, 1)
                dve.wait_ge(rooted, n + 1)
                if not first:
                    dve.wait_ge(split[j], t)
                nc.vector.tensor_tensor(heads(qk[j]), heads(U[j]), rn[j][:, :].unsqueeze(2).to_broadcast([P, H, DH]),
                                        op=ALU.mult).then_inc(ready[j], 1)

            def rotate(t, j, first):
                cos, sin = extra
                dve.wait_ge(made[j], t + 1)
                if not first:
                    dve.wait_ge(ready[j], t + 1)
                u, s, o = halves(U[j]), halves(sq[j]), halves(qk[j])
                half = DH // 2
                tab = lambda x: x[:, bass.ds(t, 1), :].to_broadcast([P, H, half])
                nc.vector.scalar_tensor_tensor(s[:, :, 0, :], u[:, :, 1, :], -1.0, tab(sin), op0=ALU.mult, op1=ALU.mult).then_inc(product, 1)
                nc.vector.tensor_tensor(s[:, :, 1, :], u[:, :, 0, :], tab(sin), op=ALU.mult).then_inc(product, 1)
                if not first:
                    dve.wait_ge(T_made[j], t)
                nc.vector.tensor_tensor(heads(qk[j]).rearrange("p h (s d) -> p h s d", s=2), u,
                                        cos[:, bass.ds(t, 1), :].unsqueeze(1).to_broadcast([P, H, 2, half]),
                                        op=ALU.mult).then_inc(product, 1)

            def copy_x(t):
                nc.vector.tensor_copy(xs[:, :], xT[:, bass.ts(t + b * NT, P)]).then_inc(x_copied, 1)

            def tile(t, first, last):
                step = normalize if layer == 0 else rotate
                step(t, 0, first)
                if not last:
                    dve.wait_ge(k_made, t + 1)
                    copy_x(t + 1)
                step(t, 1, first)

            copy_x(0)
            if layer == 0:
                dve.sem_inc(q_ready, 1)
                dve.sem_inc(k_ready, 1)
            tile(0, True, False)
            with dve.Fori(1, NT - 1) as t:
                tile(t, False, False)
            tile(NT - 1, False, True)
            if layer == 1:
                i = TILES[0]
                dve.wait_ge(qT_out, 2 * i + 2)
                nc.vector.tensor_copy(qs[:, :, :], qT[:, :, i * P:(i + 1) * P]).then_inc(q_copied, 1)



def cosine_attention(core, b, X, qT, kT, V, w_out, ident, gate):
    nc = core.nc
    (q_copied, scores_made, max_found, max_made, exp_made, sum_inv, probs_made, probsT_a, probsT_b, a_out, b_out, pv_made,
     oT_out, y_made, x_step, x_done) = core.signals(
        "q_copied scores_made max_found max_made exp_made sum_inv probs_made probsT_a probsT_b a_out b_out pv_made "
        "oT_out y_made x_step x_done")
    q_in = core.signals("q_in_first q_in_last")
    core.clear_signals()
    with ExitStack() as c:
        sb = lambda n, s: core.sbuf(c, n, s)
        pb = lambda n, w: core.psum(c, n, w)
        q_parts, q_swapped = (core.sbuf(c, n, [P, H, P], F16) for n in ("ca_q", "ca_qs"))
        probs = [sb(f"ca_p{i}", [P, N]) for i in range(4)]
        probsT = [sb(f"ca_pT{i}", [P, N]) for i in range(4)]
        nmax = sb("ca_nmax", [P, H])
        sums = sb("ca_sum", [P, H])
        oT = sb("ca_oT", [P, INNER])
        yg = sb("ca_yg", [P, D])
        S = [pb(f"ca_s{i}", N) for i in range(2)]
        Z = [pb(f"ca_z{i}", BANK) for i in range(2)]
        O = [pb(f"ca_o{i}", BANK) for i in range(2)]
        block = c.enter_context(nc.Block())

        def query_copies(i, part):
            heads, high, low = slice(part * H // 2, (part + 1) * H // 2), slice(0, DH), slice(DH, P)
            return [(to[rows, heads, :], qT[from_rows, heads, bass.ts(i, P)])
                    for to, rows, from_rows in ((q_parts, slice(0, P), slice(0, P)), (q_swapped, high, low), (q_swapped, low, high))]

        Y_AT = 6

        @block.tensor
        def _(pe):
            def scores(i, h, follows):
                if h >= 2 or follows:
                    pe.wait_ge(exp_made, i * H + h - 1)
                for q in (q_parts, q_swapped):
                    for j in range(2):
                        last = nc.tensor.matmul(S[h % 2][:, j * BANK:(j + 1) * BANK], q[:, h, :],
                                                kT[:, h, j * BANK:(j + 1) * BANK], start=(q is q_parts), stop=(q is q_swapped))
                last.then_inc(scores_made, 1)

            def transpose(i, h):
                pe.wait_ge(probs_made, i * H + h + 1)
                for half, done, out in ((0, probsT_a, a_out), (1, probsT_b, b_out)):
                    pe.wait_ge(out, i * H + h + 1)
                    for j in range(4):
                        at = (4 * half + j) * P
                        last = nc.tensor.transpose(Z[half][:, j * P:(j + 1) * P], probs[h % 4][:, at:at + P], ident[:, :])
                    last.then_inc(done, 1)

            def values(i, pair, part):
                h = 2 * pair
                pe.wait_ge(a_out, i * H + h + 3)
                pe.wait_ge(b_out, i * H + h + 3)
                if pair % 4 == 0:
                    pe.wait_ge(oT_out, 2 * i + pair // 4 + 1)
                for j in range(part * NT // 2, (part + 1) * NT // 2):
                    for s in range(2):
                        last = nc.tensor.matmul(O[pair // 4][DH * s:DH * s + DH, (pair % 4) * P:(pair % 4 + 1) * P],
                                                V[:, j, h + s, 0:DH], probsT[(h + s) % 4][:, j * P:(j + 1) * P],
                                                start=(j == 0), stop=(j == NT - 1))
                if part == 1:
                    last.then_inc(pv_made, 1)

            def project(i, heads_before):
                pe.wait_ge(oT_out, 2 * i + 4)
                pe.wait_ge(a_out, heads_before + 1)
                for j in range(NP):
                    last = nc.tensor.matmul(Z[0][:, 0:D], oT[:, j * P:(j + 1) * P], w_out[:, j, :],
                                            start=(j == 0), stop=(j == NP - 1))
                last.then_inc(y_made, 1)

            def tile(i, follows):
                for h in range(H):
                    if h % (H // 2) == 0 and follows:
                        pe.wait_ge(q_in[2 * h // H], 48 * i)
                    elif h % (H // 2) == 0:
                        pe.wait_ge(q_copied, 3 + 6 * h // H)
                    scores(i, h, follows)
                    if h >= 2:
                        transpose(i, h - 2)
                    elif follows:
                        transpose(i - 1, H - 2 + h)
                    if h >= 4:
                        values(i, (h - 4) // 2, h % 2)
                    elif follows:
                        values(i - 1, (h + H - 4) // 2, h % 2)
                    if follows and h == Y_AT:
                        project(i - 1, i * H + h - 1)
                        pe.wait_ge(x_step, i)

            tile(0, False)
            with pe.Fori(1, NT) as i:
                tile(i, True)
            transpose(NT - 1, H - 2)
            values(NT - 1, NP - 2, 0)
            transpose(NT - 1, H - 1)
            values(NT - 1, NP - 2, 1)
            values(NT - 1, NP - 1, 0)
            values(NT - 1, NP - 1, 1)
            project(NT - 1, NT * H)

        @block.sync
        def _(sp):
            with sp.Fori(1, NT) as i:
                for part in range(2):
                    sp.wait_ge(scores_made, i * H - H + (part + 1) * H // 2)
                    for to, from_ in query_copies(i, part):
                        sp.dma_start(to, from_).then_inc(q_in[part], 16)

        @block.vector
        def _(dve):
            def biggest(i, h):
                dve.wait_ge(scores_made, i * H + h + 1)
                nc.vector.tensor_reduce(nmax[:, h:h + 1], S[h % 2][:, :], axis=AX.X, op=ALU.max,
                                        negate=True).then_inc(max_found, 1)
                dve.wait_ge(max_found, i * H + h + 1)
                nc.vector.tensor_scalar(nmax[:, h:h + 1], nmax[:, h:h + 1], 1.0 / (Q_UP * K_UP), None,
                                        op0=ALU.mult).then_inc(max_made, 1)

            def normalize(i, h):
                dve.wait_ge(exp_made, i * H + h + 1)
                nc.vector.reciprocal(sums[:, h:h + 1], sums[:, h:h + 1]).then_inc(sum_inv, 1)
                dve.wait_ge(sum_inv, i * H + h + 1)
                nc.vector.tensor_scalar(probs[h % 4][:, :], probs[h % 4][:, :], sums[:, h:h + 1], None,
                                        op0=ALU.mult).then_inc(probs_made, 1)

            def evacuate_out(i, k, follows):
                dve.wait_ge(pv_made, i * NP + 4 * k + 4)
                if follows:
                    dve.wait_ge(y_made, i)
                nc.vector.tensor_copy(oT[:, k * BANK:(k + 1) * BANK], O[k][:, :]).then_inc(oT_out, 1)

            def add_to_x(i):
                dve.wait_ge(y_made, i + 1)
                nc.vector.tensor_tensor(yg[:, :], Z[0][:, 0:D], gate[:, b, :], op=ALU.mult).then_inc(x_step, 1)
                dve.wait_ge(x_step, i + 1)
                row = X[:, bass.ds(i + b * NT, 1), :]
                nc.vector.tensor_tensor(row, row, yg[:, :].unsqueeze(1), op=ALU.add).then_inc(x_done, 1)

            def tile(i, follows):
                for h in range(H):
                    biggest(i, h)
                    if h >= 1:
                        normalize(i, h - 1)
                    elif follows:
                        normalize(i - 1, H - 1)
                    if follows and h == 4:
                        evacuate_out(i - 1, 1, True)
                    if follows and h == Y_AT:
                        add_to_x(i - 1)
                    if h == 12:
                        evacuate_out(i, 0, follows)

            dve.sem_inc(oT_out, 2)
            for part in range(2):
                for to, from_ in query_copies(0, part):
                    nc.vector.tensor_copy(to, from_).then_inc(q_copied, 1)
            tile(0, False)
            with dve.Fori(1, NT) as i:
                tile(i, True)
            normalize(NT - 1, H - 1)
            evacuate_out(NT - 1, 1, True)
            add_to_x(NT - 1)

        @block.scalar
        def _(act):
            def exponentiate(i, h, follows):
                act.wait_ge(max_made, i * H + h + 1)
                if h >= 4 or follows:
                    act.wait_ge(probsT_b, i * H + h - 3)
                nc.scalar.activation(probs[h % 4][:, :], S[h % 2][:, :], ACT.Exp, bias=nmax[:, h:h + 1], scale=1.0 / (Q_UP * K_UP),
                                     accum_out=sums[:, h:h + 1]).then_inc(exp_made, 1)

            def evacuate(i, h, follows):
                act.wait_ge(probsT_a, i * H + h + 1)
                if h >= 4 or follows:
                    act.wait_ge(pv_made, i * NP + h // 2 - 1)
                nc.scalar.activation(probsT[h % 4][:, 0:BANK], Z[0][:, :], ACT.Copy).then_inc(a_out, 1)
                act.wait_ge(probsT_b, i * H + h + 1)
                nc.scalar.activation(probsT[h % 4][:, BANK:N], Z[1][:, :], ACT.Copy).then_inc(b_out, 1)

            def tile(i, follows):
                for h in range(H):
                    if h >= 2:
                        evacuate(i, h - 2, follows)
                    elif follows:
                        evacuate(i - 1, H - 2 + h, True)
                    exponentiate(i, h, follows)

            act.sem_inc(a_out, 1)
            act.sem_inc(b_out, 1)
            tile(0, False)
            with act.Fori(1, NT) as i:
                tile(i, True)
            evacuate(NT - 1, H - 2, True)
            evacuate(NT - 1, H - 1, True)



def route_first(core, xT, wts_dram, ident, tri, ones):
    nc, ins = core.nc, core.ins
    (loaded, logits_made, act_step, dve_step, pick_made, counts_made, w_made, wT_made, wT_out, stored) = core.signals(
        "loaded logits_made act_step dve_step pick_made counts_made w_made wT_made wT_out stored")
    core.clear_signals()
    with ExitStack() as c:
        sb = lambda n: core.sbuf(c, n, [P, TT, E0])
        small = lambda n: core.sbuf(c, n, [P, TT])
        Wr = core.sbuf(c, "wr", [P, E0])
        rev = core.sbuf(c, "rev", [P, E0])
        reset = core.sbuf(c, "reset", [P, 2 * E0 * TT])
        p, e, q = sb("r_p"), sb("r_e"), sb("r_q")
        m, s, r, top, top2 = small("r_m"), small("r_s"), small("r_r"), small("r_t1"), small("r_t2")
        OH = core.sbuf(c, "r_oh", [P, 2 * E0, TT])
        RK = core.sbuf(c, "r_rk", [P, 2 * E0, TT])
        TO = core.sbuf(c, "r_to", [P, 2 * E0, TT])
        w = sb("r_w")
        wT = core.sbuf(c, "r_wT", [E0, T])
        psl = core.psum(c, "r_l", TT * E0)
        psc = core.psum(c, "r_c", 2 * E0 * TT)
        pst = core.psum(c, "r_tot", 2 * E0 * TT)
        psw = core.psum(c, "r_wt", T)
        block = c.enter_context(nc.Block())
        wide = lambda t: t[:, :].unsqueeze(2).to_broadcast([P, TT, E0])
        revb = rev[:, :].unsqueeze(1).to_broadcast([P, TT, E0])
        pick = lambda k: OH[:, k * E0:(k + 1) * E0, :].rearrange("p e t -> p t e")
        flat = lambda t: t[:, :, :].rearrange("p g t -> p (g t)")

        @block.sync
        def _(sp):
            sp.dma_start(Wr[:, :], ins["L0_ffn_Wr"]).then_inc(loaded, 16)
            sp.dma_start(rev[:, :], ins["const_rev"].to_broadcast([P, E0])).then_inc(loaded, 16)
            sp.dma_start(reset[:, :], ins["const_reset"][:, 0:2 * E0 * TT].to_broadcast([P, 2 * E0 * TT])).then_inc(loaded, 16)
            sp.wait_ge(wT_out, 4)
            sp.dma_start(wts_dram[0:E0, :], wT[:, :]).then_inc(stored, 16)
            sp.wait_ge(stored, 16)

        @block.tensor
        def _(pe):
            pe.wait_ge(loaded, 48)
            for t in range(TT):
                last = nc.tensor.matmul(psl[:, t * E0:(t + 1) * E0], xT[:, t * P:(t + 1) * P], Wr[:, :],
                                        start=(t == 0), stop=True, skip_group_check=True)
            last.then_inc(logits_made, 1)
            pe.wait_ge(pick_made, 2)
            nc.tensor.matmul(psc[:, :], tri[:, :], flat(OH), start=True, stop=True)
            nc.tensor.matmul(pst[:, :], ones[:, :], flat(OH), start=True, stop=True).then_inc(counts_made, 1)
            pe.wait_ge(w_made, 1)
            for t in range(TT):
                last = nc.tensor.transpose(psw[0:E0, t * P:(t + 1) * P], w[:, t, :], ident[:, :])
                if t % 4 == 3:
                    last.then_inc(wT_made, 1)

        @block.scalar
        def _(act):
            act.wait_ge(dve_step, 2)
            nc.scalar.activation(e[:, :, :], e[:, :, :], ACT.Exp).then_inc(act_step, 1)
            for j in range(4):
                act.wait_ge(wT_made, j + 1)
                nc.scalar.activation(wT[:, j * BANK:(j + 1) * BANK], psw[0:E0, j * BANK:(j + 1) * BANK],
                                     ACT.Copy).then_inc(wT_out, 1)

        @block.vector
        def _(dve):
            done = 0
            dve.wait_ge(loaded, 48)

            def then(ins_):
                nonlocal done
                ins_.then_inc(dve_step, 1)
                done += 1
                dve.wait_ge(dve_step, done)

            dve.wait_ge(logits_made, 1)
            l = psl[:, :].rearrange("p (t e) -> p t e", e=E0)
            then(nc.vector.tensor_reduce(m[:, :], l, axis=AX.X, op=ALU.max))
            then(nc.vector.tensor_tensor(e[:, :, :], l, wide(m), op=ALU.subtract))
            dve.wait_ge(act_step, 1)
            then(nc.vector.tensor_reduce(s[:, :], e[:, :, :], axis=AX.X, op=ALU.add))
            then(nc.vector.reciprocal(r[:, :], s[:, :]))
            then(nc.vector.tensor_tensor(p[:, :, :], e[:, :, :], wide(r), op=ALU.mult))
            for k, best in enumerate((top, top2)):
                then(nc.vector.tensor_reduce(best[:, :], p[:, :, :], axis=AX.X, op=ALU.max))
                then(nc.vector.tensor_tensor(q[:, :, :], p[:, :, :], wide(best), op=ALU.is_equal))
                then(nc.vector.tensor_tensor(q[:, :, :], q[:, :, :], revb, op=ALU.mult))
                then(nc.vector.tensor_reduce(m[:, :], q[:, :, :], axis=AX.X, op=ALU.max))
                then(nc.vector.tensor_tensor(pick(k), revb, wide(m), op=ALU.is_equal))
                nc.vector.sem_inc(pick_made, 1)
                if k == 0:
                    then(nc.vector.scalar_tensor_tensor(p[:, :, :], pick(k), -2.0, p[:, :, :], op0=ALU.mult, op1=ALU.add))
            then(nc.vector.tensor_tensor(s[:, :], top[:, :], top2[:, :], op=ALU.add))
            then(nc.vector.reciprocal(r[:, :], s[:, :]))
            then(nc.vector.tensor_tensor(top[:, :], top[:, :], r[:, :], op=ALU.mult))
            then(nc.vector.tensor_tensor(top2[:, :], top2[:, :], r[:, :], op=ALU.mult))
            dve.wait_ge(counts_made, 1)
            then(nc.vector.tensor_copy(flat(TO), pst[:, :]))
            then(nc.vector.tensor_tensor_scan(flat(RK), reset[:, :], flat(TO), 0.0, op0=ALU.mult, op1=ALU.add))
            then(nc.vector.tensor_tensor(flat(RK), flat(RK), flat(TO), op=ALU.subtract))
            then(nc.vector.tensor_tensor(flat(RK), flat(RK), psc[:, :], op=ALU.add))
            then(nc.vector.scalar_tensor_tensor(flat(OH), flat(RK), float(CAP0), flat(OH), op0=ALU.is_le, op1=ALU.mult))
            then(nc.vector.tensor_tensor(q[:, :, :], pick(0), wide(top), op=ALU.mult))
            then(nc.vector.tensor_tensor(w[:, :, :], pick(1), wide(top2), op=ALU.mult))
            then(nc.vector.tensor_tensor(w[:, :, :], w[:, :, :], q[:, :, :], op=ALU.add))
            nc.vector.sem_inc(w_made, 1)



def experts_first(core, X, xT, wts_dram, ident, gate_fm, loads):
    nc, ins = core.nc, core.ins
    FC, RING = F0 // P, 4
    (base_in, w_in0, w_in1, base_made, h_made, g_made, gw_made, down_made, y_out, yT_made, x_done) = core.signals(
        "base_in w_in0 w_in1 base_made h_made g_made gw_made down_made y_out yT_made x_done")
    core.clear_signals()
    w_in = (w_in0, w_in1)
    NJ = T // BANK
    U = NJ * FC
    with ExitStack() as c:
        W1 = [core.sbuf(c, "w1", [P, F0]) for _ in range(2)]
        b1 = [core.sbuf(c, "b1", [P, FC]) for _ in range(2)]
        W2 = [core.sbuf(c, "w2", [P, FC, D]) for _ in range(2)]
        WB = [core.sbuf(c, "wb", [P, T]) for _ in range(2)]
        G = [core.sbuf(c, "g", [P, BANK]) for _ in range(RING)]
        b2 = core.sbuf(c, "b2", [E0, D])
        wT = core.sbuf(c, "wT", [E0, T])
        yT = core.sbuf(c, "yT", [P, T])
        Hp = [core.psum(c, "hp", BANK) for _ in range(RING)]
        Y = [core.psum(c, "y", BANK) for _ in range(NJ)]
        block = c.enter_context(nc.Block())

        @block.sync
        def _(sp):
            sp.dma_start(b2[:, :], ins["L0_ffn_b2"]).then_inc(base_in, 16)
            sp.dma_start(wT[:, :], wts_dram[0:E0, :]).then_inc(base_in, 16)
            with sp.Fori(0, E0 // 2) as i:
                for s in range(2):
                    e = 2 * i + s
                    sp.wait_ge(down_made, (e + 1) * U)
                    sp.dma_start(W1[s][:, :], ins["L0_ffn_W1"][bass.ds(e, 1), :, :].rearrange("e p f -> p (e f)")).then_inc(w_in[s], 16)
                    with nc.allow_non_contiguous_dma(reason="512 values"):
                        sp.dma_start(b1[s][:, :], ins["L0_ffn_b1"][bass.ds(e, 1), :].rearrange("e (c p) -> p (e c)", p=P)).then_inc(w_in[s], 16)
                    sp.dma_start(W2[s][:, :, :], ins["L0_ffn_W2"][bass.ds(e, 1), :, :].rearrange("e (c p) d -> p (e c) d", p=P)).then_inc(w_in[s], 16)
                    sp.dma_start(WB[s][:, :], wts_dram[bass.ds(e, 1), :].to_broadcast([P, T])).then_inc(w_in[s], 16)
            loads(sp)

        @block.tensor
        def _(pe):
            pe.wait_ge(base_in, 32)
            for j in range(NJ):
                nc.tensor.matmul(Y[j][:, :], b2[:, :], wT[:, j * BANK:(j + 1) * BANK], start=True, stop=False,
                                 skip_group_check=True)

            def hidden(s, k, n):
                j, f = divmod(k, FC)
                pe.wait_ge(g_made, n + k + 1)
                nc.tensor.matmul(Hp[k % RING][:, :], W1[s][:, f * P:(f + 1) * P], xT[:, j * BANK:(j + 1) * BANK],
                                 start=True, stop=True).then_inc(h_made, 1)

            def down(s, k, n):
                j, f = divmod(k, FC)
                pe.wait_ge(gw_made, n + k + 1)
                nc.tensor.matmul(Y[j][:, :], W2[s][:, f, :], G[k % RING][:, :], start=False, stop=False,
                                 skip_group_check=True).then_inc(down_made, 1)

            pe.sem_inc(down_made, 2 * U)
            with pe.Fori(0, E0 // 2) as i:
                for s in range(2):
                    pe.wait_ge(w_in[s], 64 * i + 64)
                    n = (2 * i + s) * U
                    for k in range(U + 2):
                        if k < U:
                            hidden(s, k, n)
                        if k >= 2:
                            down(s, k - 2, n)
            for j in range(NJ):
                pe.wait_ge(y_out, j + 1)
                for t in range(4):
                    at = j * BANK + t * P
                    last = nc.tensor.transpose(Hp[j][:, t * P:(t + 1) * P], yT[:, at:at + P], ident[:, :])
                last.then_inc(yT_made, 1)

        @block.scalar
        def _(act):
            act.sem_inc(g_made, RING)
            with act.Fori(0, E0 // 2) as i:
                for s in range(2):
                    act.wait_ge(w_in[s], 64 * i + 64)
                    n = (2 * i + s) * U
                    for k in range(U):
                        act.wait_ge(h_made, n + k + 1)
                        act.wait_ge(down_made, n + k + 1 - RING + 2 * U)
                        nc.scalar.activation(G[k % RING][:, :], Hp[k % RING][:, :], ACT.Gelu,
                                             bias=b1[s][:, k % FC:k % FC + 1]).then_inc(g_made, 1)

        @block.vector
        def _(dve):
            with dve.Fori(0, E0 // 2) as i:
                for s in range(2):
                    dve.wait_ge(w_in[s], 64 * i + 64)
                    n = (2 * i + s) * U
                    for k in range(U):
                        j = k // FC
                        dve.wait_ge(g_made, n + k + 1 + RING)
                        nc.vector.tensor_tensor(G[k % RING][:, :], G[k % RING][:, :], WB[s][:, j * BANK:(j + 1) * BANK],
                                                op=ALU.mult).then_inc(gw_made, 1)
            dve.wait_ge(down_made, (2 + E0) * U)
            add_transposed(nc, dve, X, Y, yT, Hp, gate_fm, y_out, yT_made, x_done)


def add_transposed(nc, dve, X, Y, yT, back, gate_fm, y_out, yT_made, x_done):
    for j in range(T // BANK):
        b = j * BANK // N
        nc.vector.tensor_scalar(yT[:, j * BANK:(j + 1) * BANK], Y[j][:, :], gate_fm[:, b:b + 1], None,
                                op0=ALU.mult).then_inc(y_out, 1)
    for j in range(T // BANK):
        dve.wait_ge(yT_made, j + 1)
        rows = X[:, 4 * j:4 * j + 4, :]
        nc.vector.tensor_tensor(rows, rows, back[j][:, :].rearrange("p (t d) -> p t d", d=D), op=ALU.add).then_inc(x_done, 1)



def prepare_second(core, ident, raw, raw_in, guT, dnT, rwT, sgT, suT, sdT):
    nc, ins = core.nc, core.ins
    banked, out_made = core.signals("banked out_made")
    core.clear_signals()
    NPAIR = E1 // 2
    with ExitStack() as c:
        gu, dn, rw, sg, su, sd = raw
        Z = [core.psum(c, "z", BANK) for _ in range(4)]
        block = c.enter_context(nc.Block())

        batches = []
        for k in range(NPAIR // 2):
            src = [gu[:, 4 * k + e, :] for e in range(4)]
            batches.append((src, [(guT[:, 2 * k + a, s, :, :], lambda z, a=a, s=s: z[:, :].rearrange(
                "h (a e s i) -> h a e s i", a=2, e=2, s=2)[:, a, :, s, :]) for a in range(2) for s in range(2)]))
        for k in range(NPAIR // 4):
            src = [dn[:, 8 * k + 2 * e:8 * k + 2 * e + 2, :] for e in range(4)]
            batches.append((src, [(dnT[:, 4 * k:4 * k + 4, :], lambda z: z[:, :].rearrange("p (a h) -> p a h", a=4))]))
        batches.append(([sg[:, 0, :], sg[:, 1, :], su[:, 0, :], su[:, 1, :]],
                        [(sgT[:, :], lambda z: z[:, 0:SI]), (suT[:, :], lambda z: z[:, SI:2 * SI])]))
        batches.append(([sd[:, 0:P], sd[:, P:SI], rw[:, :]],
                        [(sdT[:, :, :], lambda z: z[:, 0:SI].rearrange("p (a h) -> p a h", a=2)),
                         (rwT[:, :], lambda z: z[:, SI:SI + E1])]))
        copies = [len(dst) for _, dst in batches]

        @block.tensor
        def _(pe):
            pe.wait_ge(raw_in, 96)
            for n, (src, _) in enumerate(batches):
                if n >= 4:
                    pe.wait_ge(out_made, sum(copies[:n - 3]))
                for j, x in enumerate(src):
                    x = x.rearrange("p a i -> p (a i)") if len(x.shape) == 3 else x
                    rows = x.shape[0]
                    last = nc.tensor.transpose(Z[n % 4][:, j * P:j * P + rows], x, ident[0:rows, 0:rows])
                last.then_inc(banked, 1)

        @block.vector
        def _(dve):
            for n, (_, dst) in enumerate(batches):
                dve.wait_ge(banked, n + 1)
                for to, view in dst:
                    nc.vector.tensor_copy(to, view(Z[n % 4])).then_inc(out_made, 1)


def route_second(core, xT, wts_dram, ident, tri, ones, rwT):
    nc, ins = core.nc, core.ins
    (loaded, logits_made, act_step, dve_step, pick_made, counts_made, w_made, wT_made, wT_out, stored) = core.signals(
        "loaded logits_made act_step dve_step pick_made counts_made w_made wT_made wT_out stored")
    core.clear_signals()
    W = TT * E1
    with ExitStack() as c:
        sb = lambda n: core.sbuf(c, n, [P, TT, E1])
        small = lambda n: core.sbuf(c, n, [P, TT])
        bias = core.sbuf(c, "bias", [P, E1])
        reset_e = core.sbuf(c, "reset_e", [P, W])
        reset_t = core.sbuf(c, "reset_t", [P, W])
        score, v, gt, eq, rk = sb("score"), sb("v"), sb("gt"), sb("eq"), sb("rk")
        top = core.sbuf(c, "top", [P, TT, 8])
        room, s, r = small("room"), small("s"), small("r")
        OH, RK, TO = (core.sbuf(c, n, [P, E1, TT]) for n in ("oh", "rk", "to"))
        w = sb("w")
        wT = core.sbuf(c, "wT", [E1, T])
        psl = core.psum(c, "l", W)
        psc = core.psum(c, "c", W)
        pst = core.psum(c, "tot", W)
        psw = core.psum(c, "wt", T)
        block = c.enter_context(nc.Block())
        wide = lambda t: t[:, :].unsqueeze(2).to_broadcast([P, TT, E1])
        byt = lambda t: t[:, :, :].rearrange("p e t -> p t e")
        flat = lambda t: t[:, :, :].rearrange("p a b -> p (a b)")

        @block.sync
        def _(sp):
            sp.dma_start(bias[:, :], ins["L1_ffn_e_score_correction_bias"].rearrange("(a e) -> a e", a=1).to_broadcast([P, E1])).then_inc(loaded, 16)
            sp.dma_start(reset_t[:, :], ins["const_reset"].to_broadcast([P, W])).then_inc(loaded, 16)
            sp.dma_start(reset_e[:, :], ins["const_reset_e"].to_broadcast([P, W])).then_inc(loaded, 16)
            sp.wait_ge(wT_out, 4)
            sp.dma_start(wts_dram[:, :], wT[:, :]).then_inc(stored, 16)
            sp.wait_ge(stored, 16)

        @block.tensor
        def _(pe):
            for t in range(TT):
                last = nc.tensor.matmul(psl[:, t * E1:(t + 1) * E1], xT[:, t * P:(t + 1) * P], rwT[:, :],
                                        start=(t == 0), stop=True, skip_group_check=True)
            last.then_inc(logits_made, 1)
            pe.wait_ge(pick_made, 1)
            nc.tensor.matmul(psc[:, :], tri[:, :], flat(OH), start=True, stop=True)
            nc.tensor.matmul(pst[:, :], ones[:, :], flat(OH), start=True, stop=True).then_inc(counts_made, 1)
            pe.wait_ge(w_made, 1)
            for t in range(TT):
                last = nc.tensor.transpose(psw[0:E1, t * P:(t + 1) * P], w[:, t, :], ident[:, :])
                if t % 4 == 3:
                    last.then_inc(wT_made, 1)

        @block.scalar
        def _(act):
            act.wait_ge(logits_made, 1)
            nc.scalar.activation(flat(score), psl[:, :], ACT.Sigmoid).then_inc(act_step, 1)
            for j in range(4):
                act.wait_ge(wT_made, j + 1)
                nc.scalar.activation(wT[:, j * BANK:(j + 1) * BANK], psw[0:E1, j * BANK:(j + 1) * BANK],
                                     ACT.Copy).then_inc(wT_out, 1)

        @block.vector
        def _(dve):
            done = 0
            dve.wait_ge(loaded, 48)

            def then(ins_):
                nonlocal done
                ins_.then_inc(dve_step, 1)
                done += 1
                dve.wait_ge(dve_step, done)

            dve.wait_ge(act_step, 1)
            then(nc.vector.tensor_tensor(v[:, :, :], score[:, :, :], bias[:, :].unsqueeze(1).to_broadcast([P, TT, E1]), op=ALU.add))
            for t in range(TT):
                nc.vector.max(top[:, t, :], v[:, t, :]).then_inc(dve_step, 1)
            done += TT
            dve.wait_ge(dve_step, done)
            eighth = top[:, :, TOP1 - 1:TOP1].to_broadcast([P, TT, E1])
            then(nc.vector.tensor_tensor(gt[:, :, :], v[:, :, :], eighth, op=ALU.is_gt))
            then(nc.vector.tensor_tensor(eq[:, :, :], v[:, :, :], eighth, op=ALU.is_equal))
            then(nc.vector.tensor_reduce(room[:, :], gt[:, :, :], axis=AX.X, op=ALU.add))
            then(nc.vector.tensor_scalar(room[:, :], room[:, :], -1.0, float(TOP1), op0=ALU.mult, op1=ALU.add))
            then(nc.vector.tensor_tensor_scan(flat(rk), reset_e[:, :], flat(eq), 0.0, op0=ALU.mult, op1=ALU.add))
            then(nc.vector.tensor_tensor(rk[:, :, :], rk[:, :, :], wide(room), op=ALU.is_le))
            then(nc.vector.tensor_tensor(eq[:, :, :], eq[:, :, :], rk[:, :, :], op=ALU.mult))
            then(nc.vector.tensor_tensor(byt(OH), eq[:, :, :], gt[:, :, :], op=ALU.add))
            nc.vector.sem_inc(pick_made, 1)
            then(nc.vector.tensor_tensor(w[:, :, :], score[:, :, :], byt(OH), op=ALU.mult))
            then(nc.vector.tensor_reduce(s[:, :], w[:, :, :], axis=AX.X, op=ALU.add))
            then(nc.vector.tensor_scalar(s[:, :], s[:, :], 1e-20, None, op0=ALU.add))
            then(nc.vector.reciprocal(r[:, :], s[:, :]))
            then(nc.vector.tensor_tensor(w[:, :, :], w[:, :, :], wide(r), op=ALU.mult))
            dve.wait_ge(counts_made, 1)
            then(nc.vector.tensor_copy(flat(TO), pst[:, :]))
            then(nc.vector.tensor_tensor_scan(flat(RK), reset_t[:, :], flat(TO), 0.0, op0=ALU.mult, op1=ALU.add))
            then(nc.vector.tensor_tensor(flat(RK), flat(RK), flat(TO), op=ALU.subtract))
            then(nc.vector.tensor_tensor(flat(RK), flat(RK), psc[:, :], op=ALU.add))
            then(nc.vector.tensor_scalar(flat(RK), flat(RK), float(CAP1), 2.5, op0=ALU.is_le, op1=ALU.mult))
            then(nc.vector.tensor_tensor(w[:, :, :], w[:, :, :], byt(RK), op=ALU.mult))
            nc.vector.sem_inc(w_made, 1)


def experts_second(core, X, xT, wts_dram, ident, gate_fm, guT, dnT, sgT, suT, sdT):
    nc = core.nc
    (wb_in0, wb_in1, g_made, u_made, g_cut, u_cut, u_scaled, silu_made, prod_made, down_made, y_out, yT_made, x_done) = core.signals(
        "wb_in0 wb_in1 g_made u_made g_cut u_cut u_scaled silu_made prod_made down_made y_out yT_made x_done")
    core.clear_signals()
    wb_in = (wb_in0, wb_in1)
    NJ, NPAIR, LIMIT, R = T // BANK, E1 // 2, 7.0, 2
    with ExitStack() as c:
        WB = [core.sbuf(c, "wb", [P, T]) for _ in range(2)]
        g, a, u, h = ([core.sbuf(c, n, [P, BANK]) for _ in range(R)] for n in "gauh")
        yT = core.sbuf(c, "yT", [P, T])
        Gp = [core.psum(c, "gp", BANK) for _ in range(R)]
        Up = [core.psum(c, "up", BANK) for _ in range(R)]
        Y = [core.psum(c, "y", BANK) for _ in range(NJ)]
        block = c.enter_context(nc.Block())
        units = [(m, j) for m in range(-2, NPAIR) for j in range(NJ)]

        @block.sync
        def _(sp):
            for m in range(NPAIR):
                if m >= 2:
                    sp.wait_ge(u_scaled, (m - 1) * NJ)
                for e in range(2):
                    sp.dma_start(WB[m % 2][e * I1:(e + 1) * I1, :],
                                 wts_dram[2 * m + e:2 * m + e + 1, :].to_broadcast([I1, T])).then_inc(wb_in[m % 2], 16)

        @block.tensor
        def _(pe):
            def up(n):
                m, j = units[n]
                if n >= R:
                    pe.wait_ge(g_cut, n - R + 1)
                    pe.wait_ge(u_cut, n - R + 1)
                wg = sgT[:, (m + 2) * P:(m + 3) * P] if m < 0 else guT[:, m, 0, :, :].rearrange("h e i -> h (e i)")
                wu = suT[:, (m + 2) * P:(m + 3) * P] if m < 0 else guT[:, m, 1, :, :].rearrange("h e i -> h (e i)")
                nc.tensor.matmul(Gp[n % R][:, :], wg, xT[:, j * BANK:(j + 1) * BANK], start=True, stop=True).then_inc(g_made, 1)
                nc.tensor.matmul(Up[n % R][:, :], wu, xT[:, j * BANK:(j + 1) * BANK], start=True, stop=True).then_inc(u_made, 1)

            def down(n):
                m, j = units[n]
                pe.wait_ge(prod_made, n + 1)
                wd = sdT[:, m + 2, :] if m < 0 else dnT[:, m, :]
                nc.tensor.matmul(Y[j][:, :], wd, h[n % R][:, :], start=(m == -2), stop=(m == NPAIR - 1),
                                 skip_group_check=True).then_inc(down_made, 1)

            for n in range(len(units) + 2):
                if n < len(units):
                    up(n)
                if n >= 2:
                    down(n - 2)
            for j in range(NJ):
                pe.wait_ge(y_out, j + 1)
                for t in range(4):
                    at = j * BANK + t * P
                    last = nc.tensor.transpose((Gp + Up)[j][:, t * P:(t + 1) * P], yT[:, at:at + P], ident[:, :])
                last.then_inc(yT_made, 1)

        @block.vector
        def _(dve):
            for n, (m, j) in enumerate(units):
                dve.wait_ge(g_made, n + 1)
                if n >= R:
                    dve.wait_ge(silu_made, n - R + 1)
                if m < 0:
                    nc.vector.tensor_copy(g[n % R][:, :], Gp[n % R][:, :]).then_inc(g_cut, 1)
                else:
                    nc.vector.tensor_scalar(g[n % R][:, :], Gp[n % R][:, :], LIMIT, None, op0=ALU.min).then_inc(g_cut, 1)
                dve.wait_ge(u_made, n + 1)
                if n >= R:
                    dve.wait_ge(prod_made, n - R + 1)
                if m < 0:
                    nc.vector.tensor_copy(u[n % R][:, :], Up[n % R][:, :]).then_inc(u_cut, 1)
                else:
                    nc.vector.tensor_scalar(u[n % R][:, :], Up[n % R][:, :], LIMIT, -LIMIT, op0=ALU.min, op1=ALU.max).then_inc(u_cut, 1)
                    dve.wait_ge(u_cut, n + 1)
                    dve.wait_ge(wb_in[m % 2], 32 * (m // 2 + 1))
                    nc.vector.tensor_tensor(u[n % R][:, :], u[n % R][:, :], WB[m % 2][:, j * BANK:(j + 1) * BANK],
                                            op=ALU.mult).then_inc(u_scaled, 1)
                dve.wait_ge(u_cut, n + 1)
                if m >= 0:
                    dve.wait_ge(u_scaled, n + 1 - 2 * NJ)
                dve.wait_ge(silu_made, n + 1)
                if n >= R:
                    dve.wait_ge(down_made, n - R + 1)
                nc.vector.tensor_tensor(h[n % R][:, :], u[n % R][:, :], a[n % R][:, :], op=ALU.mult).then_inc(prod_made, 1)
            dve.wait_ge(down_made, len(units))
            add_transposed(nc, dve, X, Y, yT, Gp + Up, gate_fm, y_out, yT_made, x_done)

        @block.scalar
        def _(act):
            for n in range(len(units)):
                act.wait_ge(g_cut, n + 1)
                if n >= R:
                    act.wait_ge(prod_made, n - R + 1)
                nc.scalar.activation(a[n % R][:, :], g[n % R][:, :], ACT.Silu).then_inc(silu_made, 1)



NG = 16
QA, QQ = 2, 4
ORIGIN = N - P + P // 2 + NG
TABLE = ORIGIN + P
HID = 2 * H
QR = P // NG
TILES = [i for m in range(NT // 2) for i in (NT // 2 - 1 - m, NT // 2 + m)]
ROW = N + P


def load_kerple(core, sp, loaded, par, b1, b2, w1k, kron1, kron2, hid_tab, score_tab):
    nc, ins = core.nc, core.ins
    w1, w2 = ins["L1_attn_w1"], ins["L1_attn_w2"]
    with nc.allow_non_contiguous_dma(reason="a few small weights"):
        for q in range(QQ):
            cols = slice(HID * q, HID * (q + 1))
            for a in range(QA):
                lo = 64 * a + H * q
                sp.dma_start(kron1[a][lo:lo + H, cols], w1[0:H, :]).then_inc(loaded, 16)
            sp.dma_start(w1k[H * q:H * (q + 1), cols], w1[H:2 * H, :]).then_inc(loaded, 16)
            sp.dma_start(kron2[cols, H * q:H * (q + 1)], w2).then_inc(loaded, 16)
            sp.dma_start(b1[cols, :], ins["L1_attn_b1"].rearrange("(m a) -> m a", a=1)).then_inc(loaded, 16)
        for r in range(P // H):
            rows = slice(H * r, H * (r + 1))
            sp.dma_start(par[rows, 0:1], ins["L1_attn_log_p"].rearrange("h a c -> h (a c)")).then_inc(loaded, 16)
            sp.dma_start(par[rows, 1:2], ins["L1_attn_log_a"].rearrange("h a c -> h (a c)")).then_inc(loaded, 16)
            sp.dma_start(b2[rows, 0:1], ins["L1_attn_b2"].rearrange("(h a) -> h a", a=1)).then_inc(loaded, 16)
    sp.dma_start(hid_tab[:, :], ins["const_dist"]).then_inc(loaded, 16)
    sp.dma_start(score_tab[:, :], ins["const_mask"]).then_inc(loaded, 16)


def kerple_tables(core, loaded, par, b1, b2, w1k, kron1, kron2, hid_tab, score_tab):
    nc = core.nc
    act_step, dve_step, tab_made, multiplied, done = core.signals("act_step dve_step tab_made multiplied done")
    core.clear_signals()
    with ExitStack() as c:
        ab = core.sbuf(c, "ab", [P, 2])
        ex = core.sbuf(c, "ex", [P, 2])
        ps = core.psum(c, "k", 3 * BANK)
        block = c.enter_context(nc.Block())
        dist, sign = hid_tab, score_tab

        @block.vector
        def _(dve):
            dve.wait_ge(loaded, 16 * (5 * QQ + 3 * P // H + 2))
            nc.vector.scalar_tensor_tensor(ab[:, :], par[:, :], -1.0, par[:, :], op0=ALU.mult, op1=ALU.max).then_inc(dve_step, 1)
            dve.wait_ge(act_step, 2)
            nc.vector.scalar_tensor_tensor(par[:, :], par[:, :], 0.0, ex[:, :], op0=ALU.max, op1=ALU.add).then_inc(dve_step, 1)
            dve.wait_ge(dve_step, 2)
            nc.vector.tensor_scalar(par[:, 0:1], par[:, 0:1], -1.0, None, op0=ALU.mult).then_inc(dve_step, 1)
            dve.wait_ge(act_step, 3)
            dve.wait_ge(dve_step, 3)
            nc.vector.tensor_scalar(dist[:, :], dist[:, :], par[:, 0:1], None, op0=ALU.mult).then_inc(tab_made, 1)
            dve.wait_ge(tab_made, 1)
            nc.vector.scalar_tensor_tensor(score_tab[:, :], dist[:, :], b2[:, 0:1], sign[:, :], op0=ALU.add, op1=ALU.add).then_inc(done, 1)
            dve.wait_ge(multiplied, 1)
            dve.wait_ge(done, 1)
            nc.vector.tensor_scalar(hid_tab[:, :], ps[:, 0:TABLE], b1[:, 0:1], None, op0=ALU.add).then_inc(done, 1)

        @block.scalar
        def _(act):
            act.wait_ge(dve_step, 1)
            nc.scalar.activation(ex[:, :], ab[:, :], ACT.Exp, scale=-1.0).then_inc(act_step, 1)
            act.wait_ge(act_step, 1)
            nc.scalar.activation(ex[:, :], ex[:, :], ACT.Ln, bias=1.0).then_inc(act_step, 1)
            act.wait_ge(dve_step, 2)
            nc.scalar.activation(dist[:, :], dist[:, :], ACT.Ln, scale=par[:, 1:2], bias=1.0).then_inc(act_step, 1)

        @block.tensor
        def _(pe):
            pe.wait_ge(tab_made, 1)
            for at in range(0, TABLE, BANK):
                w = min(BANK, TABLE - at)
                last = nc.tensor.matmul(ps[:, at:at + w], w1k[0:64, :], dist[0:64, at:at + w], start=True, stop=True)
            last.then_inc(multiplied, 1)



def refined_attention(core, b, X, arena, kT, V, w_out, ident, gate, qs, q_stored, q_dram, kron1, kron2, hid_tab, score_tab):
    nc = core.nc
    SLOTS = 6
    LAG = 4
    f_in = core.signals("f_in0 f_in1 f_in2 f_in3 f_in4 f_in5")
    (q_in, s_made, s_out_act, s_out_dve, h_made, hid_made, gelu_made, r_made, kerple_added, f_made, max_step,
     max_made, p_made, inverted, p_normed, z_made, z_out, pv_made, oT_out, y_made, x_step, x_done) = core.signals(
        "q_in s_made s_out_act s_out_dve h_made hid_made gelu_made r_made kerple_added f_made max_step "
        "max_made p_made inverted p_normed z_made z_out pv_made oT_out y_made x_step x_done")
    core.clear_signals()
    length = [(i + 1) * P for i in TILES]
    base = [0 if k % 2 == 0 else ROW - length[k] for k in range(NT)]
    units = [(k, g, at, min(BANK, length[k] - at)) for k in range(NT) for g in range(NG) for at in range(0, length[k], BANK)]
    first_unit = [next(n for n, u in enumerate(units) if u[0] == k) for k in range(NT)] + [len(units)]
    per_batch = [NG // 4 if length[k] > BANK else NG // 2 if length[k] > BANK - P else NG for k in range(NT)]
    batch_units = [per_batch[k] * -(-length[k] // BANK) for k in range(NT)]
    z_lag = [batch_units[k] + LAG + 2 for k in range(NT)]
    last_batch = [first_unit[k + 1] - batch_units[k] for k in range(NT)]
    with ExitStack() as c:
        work = core.sbuf(c, "work", [P, SLOTS, N])
        oT = core.sbuf(c, "oT", [P, NP, P])
        mx = core.sbuf(c, "mx", [P, 2, NG])
        nmax = core.sbuf(c, "nmax", [P, NG])
        esum = core.sbuf(c, "esum", [P, NG])
        yg = core.sbuf(c, "yg", [P, D])
        PS = core.psum(c, "ps", 8 * BANK)
        bank = lambda n: PS[:, n * BANK:(n + 1) * BANK]
        block = c.enter_context(nc.Block())
        rows = arena[:, :].rearrange("p (g j) -> p g j", g=NG)

        def F(n):
            k, g, at, w = units[n]
            return rows[:, g, base[k] + at:base[k] + at + w]

        row = lambda k, g: rows[:, g, base[k]:base[k] + length[k]]
        hs = lambda n: work[:, n % SLOTS, :]
        hp = lambda n, a: bank(2 * (n % 2) + a)
        rp = lambda n: bank(4 + n % 2)
        O = lambda half: bank(4 + half)
        zp = lambda n: bank(6 + n % 2)
        y = bank(6)

        def batch_done(k, n):
            m = n - first_unit[k] + 1
            if m <= 0 or m % batch_units[k]:
                return []
            q = m // batch_units[k]
            return list(range((q - 1) * per_batch[k], q * per_batch[k]))

        def rows_wait(eng, n):
            if n >= SLOTS:
                eng.wait_ge(f_in[n % SLOTS], 16 * (n // SLOTS))

        @block.sync
        def _(sp):
            sp.wait_ge(q_stored, 16 * NT * (b + 1))
            for k in range(NT):
                i = TILES[k]
                if k:
                    sp.wait_ge(s_made, H * k)
                    sp.dma_start(qs[:, :, :], q_dram[:, :, i * P:(i + 1) * P]).then_inc(q_in, 16)
                if k >= 2:
                    sp.wait_ge(pv_made, k - 1)
                for h in range(H):
                    n = H * k + h
                    if h % 2 == 0:
                        sp.wait_ge(s_out_act, n // 2 + 1)
                    else:
                        sp.wait_ge(s_out_dve, n // 2 + 1)
                    sp.dma_start(rows[h:h + P - H + 1:H, :, base[k]:base[k] + length[k]],
                                 work[:, n % SLOTS, 0:length[k]]).then_inc(f_in[n % SLOTS], 16)

        @block.tensor
        def _(pe):
            def scores(k):
                if k:
                    pe.wait_ge(q_in, 16 * k)
                    pe.wait_ge(hid_made, 2 * first_unit[k])
                for h in range(H):
                    n = H * k + h
                    if h >= 2:
                        if h % 2 == 0:
                            pe.wait_ge(s_out_act, n // 2)
                        else:
                            pe.wait_ge(s_out_dve, n // 2)
                    r = slice(DH * (h % 2), DH * (h % 2) + DH)
                    for at in range(0, length[k], BANK):
                        w = min(BANK, length[k] - at)
                        last = nc.tensor.matmul(bank(2 * (h % 2) + at // BANK)[:, 0:w], qs[r, h // 2, :],
                                                kT[r, h // 2, at:at + w], start=True, stop=True)
                    last.then_inc(s_made, 1)

            def hidden(n):
                w = units[n][3]
                if n >= 2:
                    pe.wait_ge(hid_made, 2 * (n - 1))
                for a in range(QA):
                    last = nc.tensor.matmul(hp(n, a)[:, 0:w], kron1[a][:, :], F(n), start=True, stop=True)
                last.then_inc(h_made, 1)

            def refine(n):
                w = units[n][3]
                pe.wait_ge(gelu_made, n + 1)
                if n >= 2:
                    pe.wait_ge(f_made, n - 1)
                for a in range(QA):
                    last = nc.tensor.matmul(rp(n)[64 * a:64 * a + 64, 0:w], kron2[:, 0:64], hs(n)[:, a * BANK:a * BANK + w],
                                            start=True, stop=True)
                last.then_inc(r_made, 1)

            def transpose(n):
                k, g, at, w = units[n]
                pe.wait_ge(p_normed, NG * k + g + 1)
                if n >= 2:
                    pe.wait_ge(z_out, n - 1)
                for c in range(0, w, P):
                    last = nc.tensor.transpose(zp(n)[:, c:c + P], F(n)[:, c:c + P], ident[:, :])
                last.then_inc(z_made, 1)

            def values(k):
                pe.wait_ge(z_out, first_unit[k + 1])
                pe.wait_ge(f_made, first_unit[k + 1])
                blocks = length[k] // P
                for jb in range(blocks):
                    at = base[k] + jb * P
                    for h in range(H):
                        j = h // 2
                        last = nc.tensor.matmul(O(j // 4)[DH * (h % 2):DH * (h % 2) + DH, (j % 4) * P:(j % 4 + 1) * P],
                                                V[:, jb, h, :], rows[:, :, at + QR * h:at + QR * (h + 1)],
                                                start=(jb == 0 and j % 4 == 0), stop=(jb == blocks - 1), skip_group_check=True)
                last.then_inc(pv_made, 1)

            def project(k):
                pe.wait_ge(oT_out, 2 * k + 2)
                for j in range(NP):
                    last = nc.tensor.matmul(y[:, 0:D], oT[:, j, :], w_out[:, j, :], start=(j == 0), stop=(j == NP - 1))
                last.then_inc(y_made, 1)

            scores(0)
            for k in range(NT):
                lo, hi = first_unit[k], first_unit[k + 1]
                for s in range(SLOTS):
                    pe.wait_ge(f_in[s], 16 * ((H * (k + 1) - s + SLOTS - 1) // SLOTS))
                for n in range(lo, hi + LAG):
                    if n < hi:
                        hidden(n)
                    if k and n == lo + 1:
                        project(k - 1)
                    if k and n == lo + LAG:
                        pe.wait_ge(oT_out, 2 * k)
                        pe.wait_ge(x_step, k)
                    if n >= lo + LAG:
                        refine(n - LAG)
                    if lo <= n - z_lag[k] < last_batch[k]:
                        transpose(n - z_lag[k])
                for n in range(max(lo, hi + LAG - z_lag[k]), last_batch[k]):
                    transpose(n)
                if k + 1 < NT:
                    scores(k + 1)
                for n in range(last_batch[k], hi):
                    transpose(n)
                values(k)
            project(NT - 1)

        @block.scalar
        def _(act):
            def score_out(n):
                L = length[n // H]
                act.wait_ge(s_made, n + 1)
                if n >= H:
                    act.wait_ge(r_made, first_unit[n // H])
                rows_wait(act, n)
                nc.scalar.activation(work[:, n % SLOTS, 0:L], PS[:, 0:L], ACT.Copy, scale=DH ** -0.5).then_inc(s_out_act, 1)

            def gelu(n):
                w = units[n][3]
                act.wait_ge(hid_made, 2 * n + 2)
                h2 = hs(n).rearrange("p (a w) -> p a w", a=QA)[:, :, 0:w]
                nc.scalar.activation(h2, h2, ACT.Gelu).then_inc(gelu_made, 1)

            def exponentials(k, groups):
                for g in groups:
                    act.wait_ge(max_made, NG * k + g + 1)
                    nc.scalar.activation(row(k, g), row(k, g), ACT.Exp, bias=nmax[:, g:g + 1],
                                         accum_out=esum[:, g:g + 1]).then_inc(p_made, 1)

            def transposed_out(n):
                w = units[n][3]
                act.wait_ge(z_made, n + 1)
                nc.scalar.activation(F(n).rearrange("p (c h r) -> p c h r", h=H, r=QR),
                                     zp(n)[:, 0:w].rearrange("p (c r h) -> p c h r", h=H, r=QR), ACT.Copy).then_inc(z_out, 1)

            for h in range(0, H, 2):
                score_out(h)
            for k in range(NT):
                lo, hi = first_unit[k], first_unit[k + 1]
                for n in range(lo, hi + LAG):
                    if n < hi:
                        gelu(n)
                        exponentials(k, batch_done(k, n - LAG))
                    if lo <= n - z_lag[k] < last_batch[k]:
                        transposed_out(n - z_lag[k])
                for n in range(max(lo, hi + LAG - z_lag[k]), last_batch[k]):
                    transposed_out(n)
                groups = batch_done(k, hi - 1)
                each = -(-len(groups) // NP)
                for j in range(NP):
                    exponentials(k, groups[j * each:(j + 1) * each])
                    if k + 1 < NT:
                        score_out(H * (k + 1) + 2 * j)
                for n in range(last_batch[k], hi):
                    transposed_out(n)
                act.wait_ge(pv_made, k + 1)
                if k:
                    act.wait_ge(y_made, k)
                nc.scalar.activation(oT[:, 0:4, :].rearrange("p j (r g) -> p j r g", g=NG),
                                     O(0).rearrange("p (j g r) -> p j r g", g=NG, r=QR), ACT.Copy).then_inc(oT_out, 1)

        @block.gpsimd
        def _(pool):
            for n, (k, g, at, w) in enumerate(units):
                pool.wait_ge(h_made, n + 1)
                start = ORIGIN - (TILES[k] * P + g) + at
                nc.gpsimd.tensor_tensor(F(n), F(n), score_tab[:, start:start + w], op=ALU.add).then_inc(kerple_added, 1)

        @block.vector
        def _(dve):
            max_steps = 0

            def score_out(n):
                L = length[n // H]
                dve.wait_ge(s_made, n + 1)
                if n >= H:
                    dve.wait_ge(r_made, first_unit[n // H])
                rows_wait(dve, n)
                nc.vector.tensor_scalar(work[:, n % SLOTS, 0:L], PS[:, 2 * BANK:2 * BANK + L], DH ** -0.5, None,
                                        op0=ALU.mult).then_inc(s_out_dve, 1)

            def hidden(n):
                k, g, at, w = units[n]
                dve.wait_ge(h_made, n + 1)
                if n >= SLOTS:
                    dve.wait_ge(r_made, n - SLOTS + 1)
                for a in range(QA):
                    start = ORIGIN - (TILES[k] * P + g + 64 * a) + at
                    nc.vector.tensor_tensor(hs(n)[:, a * BANK:a * BANK + w], hp(n, a)[:, 0:w], hid_tab[:, start:start + w],
                                            op=ALU.add).then_inc(hid_made, 1)

            def refined(n):
                k, g, at, w = units[n]
                dve.wait_ge(r_made, n + 1)
                dve.wait_ge(kerple_added, n + 1)
                nc.vector.tensor_tensor_reduce(out=F(n), in0=rp(n)[:, 0:w], in1=F(n), scale=1.0, scalar=2 * NEG,
                                               op0=ALU.add, op1=ALU.max,
                                               accum_out=mx[:, at // BANK, g:g + 1]).then_inc(f_made, 1)

            def maxima(k, n):
                nonlocal max_steps
                groups = batch_done(k, n)
                if not groups:
                    return
                gs = slice(groups[0], groups[-1] + 1)
                dve.wait_ge(f_made, n + 1)
                if length[k] > BANK:
                    nc.vector.tensor_tensor(mx[:, 0, gs], mx[:, 0, gs], mx[:, 1, gs], op=ALU.max).then_inc(max_step, 1)
                    max_steps += 1
                    dve.wait_ge(max_step, max_steps)
                nc.vector.tensor_scalar(nmax[:, gs], mx[:, 0, gs], -1.0, None, op0=ALU.mult).then_inc(max_made, len(groups))

            def normalize(k, groups):
                for g in groups:
                    n = NG * k + g
                    dve.wait_ge(p_made, n + 1)
                    nc.vector.reciprocal(esum[:, g:g + 1], esum[:, g:g + 1]).then_inc(inverted, 1)
                    dve.wait_ge(inverted, n + 1)
                    nc.vector.tensor_scalar(row(k, g), row(k, g), esum[:, g:g + 1], None, op0=ALU.mult).then_inc(p_normed, 1)

            def residual(k):
                dve.wait_ge(y_made, k + 1)
                if k:
                    dve.wait_ge(x_done, k)
                nc.vector.tensor_tensor(yg[:, :], y[:, 0:D], gate[:, b, :], op=ALU.mult).then_inc(x_step, 1)
                dve.wait_ge(x_step, k + 1)
                x = X[:, TILES[k] + b * NT, :]
                nc.vector.tensor_tensor(x, x, yg[:, :], op=ALU.add).then_inc(x_done, 1)

            for h in range(1, H, 2):
                score_out(h)
            for k in range(NT):
                lo, hi = first_unit[k], first_unit[k + 1]
                for n in range(lo, hi + LAG):
                    if n < hi:
                        hidden(n)
                    if k and n == lo + 2:
                        residual(k - 1)
                    if n >= lo + LAG:
                        refined(n - LAG)
                        maxima(k, n - LAG)
                    done = batch_done(k, n - LAG - 2)
                    normalize(k, done[:len(done) // 2])
                    done = batch_done(k, n - LAG - 3)
                    normalize(k, done[len(done) // 2:])
                groups = batch_done(k, hi - 1)
                each = -(-len(groups) // NP)
                for j in range(NP):
                    if k + 1 < NT:
                        score_out(H * (k + 1) + 2 * j + 1)
                    normalize(k, groups[j * each:(j + 1) * each])
                dve.wait_ge(pv_made, k + 1)
                if k:
                    dve.wait_ge(y_made, k)
                nc.vector.tensor_copy(oT[:, 4:8, :].rearrange("p j (r g) -> p j r g", g=NG),
                                      O(1).rearrange("p (j g r) -> p j r g", g=NG, r=QR)).then_inc(oT_out, 1)
            residual(NT - 1)



def host_constants():
    reset = np.ones((1, E1 * TT), np.float32)
    reset[:, ::TT] = 0.0
    reset_e = np.ones((1, E1 * TT), np.float32)
    reset_e[:, ::E1] = 0.0
    behind = (np.arange(P) // H * NG).reshape(P, 1) + ORIGIN - np.arange(TABLE)[None]
    freq = (np.float32(1.0) / np.float32(10000.0) ** (np.arange(0, DH, 2, dtype=np.float32) / np.float32(DH))).astype(np.float32)
    angle = np.outer(np.arange(N, dtype=np.float32), freq).astype(np.float32)
    tiles = lambda t: np.ascontiguousarray(t.reshape(NT, P, DH // 2).transpose(1, 0, 2).astype(np.float32))
    return {
        "const_dist": np.abs(behind).astype(np.float32),
        "const_mask": np.where(behind < 0, NEG, 0.0).astype(np.float32),
        "const_cos": tiles(np.cos(angle)),
        "const_sin": tiles(np.sin(angle)),
        "const_reset_e": reset_e,
        "const_ident": np.eye(P, dtype=np.float32),
        "const_tri": np.triu(np.ones((P, P), np.float32)),
        "const_reset": reset,
        "const_rev": np.arange(E0, 0, -1, dtype=np.float32)[None],
    }


def program(nc, ins, out, stages="01234"):
    with ExitStack() as ctx:
        core = Core(nc, ctx, ins)
        sb = lambda n, s: core.sbuf(ctx, n, s)
        kerple_in, weights_in, raw_in, q_stored = (ctx.enter_context(nc.semaphore(n))
                                                   for n in ("kerple_in", "weights_in", "raw_in", "q_stored"))
        X = sb("X", [P, TT, D])
        xT = sb("xT", [P, T])
        ident = sb("ident", [P, P])
        expo = sb("expo", [P, 1])
        mod = sb("mod", [P, 2, 6, B])
        gate = sb("gate", [P, 2, B, D])
        rows = sb("rows", [P, B, D])
        tri, ones = sb("tri", [P, P]), sb("ones", [P, P])
        q_dram = nc.dram_tensor("queries", (P, NP, N), F32, kind="Internal").ap()
        wts_dram = nc.dram_tensor("expert_weights", (E1, T), F32, kind="Internal").ap()
        modulation(core, X, ident, tri, ones, expo, mod, gate, rows)

        if "0" in stages:
            with ExitStack() as c:
                sc = lambda n, s: core.sbuf(c, n, s)
                w_qkv = sc("w_qkv", [P, 3 * INNER])
                w_out = sc("w_out", [P, NP, D])
                hscale = sc("hscale", [P, H])
                ident16 = core.sbuf(c, "ident16", [P, P], F16)

                def load_weights(sp):
                    sp.dma_start(w_qkv[:, :], ins["L0_attn_w_qkv"]).then_inc(weights_in, 16)
                    sp.dma_start(w_out[:, :, :], ins["L0_attn_w_out"].rearrange("(j p) d -> p j d", p=P)).then_inc(weights_in, 16)
                    sp.dma_start(hscale[:, :], ins["L0_attn_logit_scale"].rearrange("h a c -> (a c) h").to_broadcast([P, H])).then_inc(weights_in, 16)

                layer_norm(core, X, xT, ident, expo, mod[:, 0, 0, :], mod[:, 0, 1, :], rows, load_weights)
                qT, kT = (core.sbuf(c, n, [P, H, N], F16) for n in ("qT", "kT"))
                V = sc("V", [P, NT, H, DH])
                scaled, copied = core.signals("scaled copied")
                core.clear_signals()
                with nc.Block() as block:
                    @block.vector
                    def _(dve):
                        nc.vector.tensor_copy(ident16[:, :], ident[:, :]).then_inc(copied, 1)
                        dve.wait_ge(weights_in, 48)
                        nc.vector.tensor_scalar(hscale[:, :], hscale[:, :], float(np.float32(np.log(1.0 / 0.01))), None, op0=ALU.min).then_inc(scaled, 1)

                    @block.scalar
                    def _(act):
                        act.wait_ge(scaled, 1)
                        nc.scalar.activation(hscale[:, :], hscale[:, :], ACT.Exp, scale=2.0).then_inc(scaled, 1)
                for b in range(B):
                    project_qkv(core, 0, b, xT, w_qkv, qT, kT, V, ident, hscale, ident16=ident16)
                    cosine_attention(core, b, X, qT, kT, V, w_out, ident, gate[:, 0])

        with ExitStack() as outer:
            sc = lambda n, s: core.sbuf(outer, n, s)
            kron1 = [sc("kron1", [P, P]) for _ in range(QA)]
            kron2, w1k = sc("kron2", [P, 64]), sc("w1k", [P, P])
            par, b2, b1 = sc("par", [P, 2]), sc("kb2", [P, 2]), sc("kb1", [P, 1])
            hid_tab, score_tab = sc("hid_tab", [P, TABLE]), sc("score_tab", [P, TABLE])
            kerple = (kerple_in, par, b1, b2, w1k, kron1, kron2, hid_tab, score_tab)
            zeroed, = core.signals("zeroed")
            core.clear_signals()
            with nc.Block() as block:
                @block.vector
                def _(dve):
                    for t in (*kron1, kron2, w1k):
                        nc.vector.memset(t[:, :], 0.0).then_inc(zeroed, 1)
                    dve.wait_ge(zeroed, 4)

            if "1" in stages:
                layer_norm(core, X, xT, ident, expo, mod[:, 0, 3, :], mod[:, 0, 4, :])
                route_first(core, xT, wts_dram, ident, tri, ones)
                experts_first(core, X, xT, wts_dram, ident, mod[:, 0, 5, :], lambda sp: load_kerple(core, sp, *kerple))

            if "2" in stages:
                if "1" not in stages:
                    with nc.Block() as block:
                        @block.sync
                        def _(sp):
                            load_kerple(core, sp, *kerple)
                with ExitStack() as c:
                    arena = core.sbuf(c, "arena", [P, NG * ROW])
                    kT = core.sbuf(c, "kT", [P, NP, N])
                    V = core.sbuf(c, "V", [P, NT, H, DH])
                    w_out = core.sbuf(c, "w_out", [P, NP, D])
                    qs = core.sbuf(c, "qs", [P, NP, P])
                    cos = core.sbuf(c, "cos", [P, NT, DH // 2])
                    sin = core.sbuf(c, "sin", [P, NT, DH // 2])
                    qT = arena[:, 0:NP * N].rearrange("p (a n) -> p a n", a=NP)
                    w_qkv = arena[:, NP * N:NP * N + 3 * INNER]
                    first = 48 if "0" in stages else 0

                    def load_weights(sp):
                        sp.dma_start(w_qkv[:, :], ins["L1_attn_w_qkv"]).then_inc(weights_in, 16)

                    def load_all_weights(sp):
                        load_weights(sp)
                        sp.dma_start(cos[:, :, :], ins["const_cos"]).then_inc(weights_in, 16)
                        sp.dma_start(sin[:, :, :], ins["const_sin"]).then_inc(weights_in, 16)
                        sp.dma_start(w_out[:, :, :], ins["L1_attn_w_o"].rearrange("(j p) d -> p j d", p=P)).then_inc(weights_in, 16)

                    layer_norm(core, X, xT, ident, expo, mod[:, 1, 0, :], mod[:, 1, 1, :], None, load_all_weights)
                    kerple_tables(core, *kerple)
                    for b in range(B):
                        project_qkv(core, 1, b, xT, w_qkv, qT, kT, V, ident, (cos, sin), q_dram,
                                    load=load_weights if b else None, weights=(weights_in, first + 64 + 16 * b),
                                    q_stored=q_stored, qs=qs)
                        refined_attention(core, b, X, arena, kT, V, w_out, ident, gate[:, 1], qs, q_stored, q_dram, kron1, kron2, hid_tab, score_tab)

        if "3" in stages:
            with ExitStack() as c:
                guT = core.sbuf(c, "guT", [P, E1 // 2, 2, 2, I1])
                dnT = core.sbuf(c, "dnT", [P, E1 // 2, D])
                rwT = core.sbuf(c, "rwT", [P, E1])
                sgT, suT = core.sbuf(c, "sgT", [P, SI]), core.sbuf(c, "suT", [P, SI])
                sdT = core.sbuf(c, "sdT", [P, 2, D])
                with ExitStack() as c2:
                    gu = core.sbuf(c2, "gu", [P, E1, D])
                    dn = core.sbuf(c2, "dn", [P, E1, I1])
                    rw = core.sbuf(c2, "rw", [E1, D])
                    sg = core.sbuf(c2, "sg", [P, 2, D])
                    su = core.sbuf(c2, "su", [P, 2, D])
                    sd = core.sbuf(c2, "sd", [P, SI])

                    def load_raw(sp):
                        sp.dma_start(gu[:, :, :], ins["L1_ffn_gate_up_proj"].rearrange("e o h -> o e h")).then_inc(raw_in, 16)
                        sp.dma_start(dn[:, :, :], ins["L1_ffn_down_proj"].rearrange("e h i -> h e i")).then_inc(raw_in, 16)
                        sp.dma_start(rw[:, :], ins["L1_ffn_router_weight"]).then_inc(raw_in, 16)
                        sp.dma_start(sg[:, :, :], ins["L1_ffn_shared_gate"].rearrange("(a p) h -> p a h", p=P)).then_inc(raw_in, 16)
                        sp.dma_start(su[:, :, :], ins["L1_ffn_shared_up"].rearrange("(a p) h -> p a h", p=P)).then_inc(raw_in, 16)
                        sp.dma_start(sd[:, :], ins["L1_ffn_shared_down"]).then_inc(raw_in, 16)

                    layer_norm(core, X, xT, ident, expo, mod[:, 1, 3, :], mod[:, 1, 4, :], None, load_raw)
                    prepare_second(core, ident, (gu, dn, rw, sg, su, sd), raw_in, guT, dnT, rwT, sgT, suT, sdT)
                route_second(core, xT, wts_dram, ident, tri, ones, rwT)
                experts_second(core, X, xT, wts_dram, ident, mod[:, 1, 5, :], guT, dnT, sgT, suT, sdT)

        stored, = core.signals("stored")
        core.clear_signals()
        with nc.Block() as block:
            @block.sync
            def _(sp):
                sp.dma_start(out.rearrange("b (t p) d -> p (b t) d", p=P), X[:, :, :]).then_inc(stored, 16)
                sp.wait_ge(stored, 16)


def kernel(**inputs):
    import concourse.bacc as bacc
    from concourse.bass_utils import run_bass_kernel_spmd

    nc = bacc.Bacc("TRN2", target_bir_lowering=False, num_devices=1)
    arrays = {name: np.ascontiguousarray(a) for name, a in {**inputs, **host_constants()}.items()}
    ins = {name: nc.dram_tensor(name, a.shape, mybir.dt.from_np(a.dtype), kind="ExternalInput").ap()
           for name, a in arrays.items()}
    out = nc.dram_tensor("out", (B, N, D), F32, kind="ExternalOutput").ap()
    program(nc, ins, out)
    return run_bass_kernel_spmd(nc, [arrays], core_ids=[0]).results[0]["out"]
```
